# Optimizing a Trainium2 kernel written in Bass

```python
import numpy as np
import jax
import jax.numpy as jnp

def _softmax(x, axis=-1):
    return jax.nn.softmax(x, axis=axis)

def _gelu(x):
    return jax.nn.gelu(x, approximate=True)

def _silu(x):
    return jax.nn.silu(x)

def _sigmoid(x):
    return jax.nn.sigmoid(x)

def _layernorm(x, axis=-1, eps=1e-05):
    m = jnp.mean(x, axis=axis, keepdims=True)
    v = jnp.var(x, axis=axis, keepdims=True)
    return (x - m) / jnp.sqrt(v + eps)

def _scatter_add(tgt, idx, src, axis=0):
    return tgt.at[idx].add(src)

def _segment_sum(src, seg, n):
    return jax.ops.segment_sum(src, seg, n)
kernel_name = 'mk_prb_d2_jaxref_r8_741ee9'

def setup_inputs(seed: int=0):
    np.random.seed(seed)
    _w = jnp.asarray

    def _L0_attn_setup():
        import jax, jax.numpy as jnp
        import numpy as np
        NUM_HEADS = 16

        def _heads(t, B, N, H, hd):
            return t.reshape(B, N, H, hd).transpose(0, 2, 1, 3)
        key = jax.random.key(seed)
        ks = jax.random.split(key, 9)
        B, N, D = (2, 256, 128)
        w = 0.02
        return {'x': jax.random.normal(ks[0], (B, N, D), dtype=jnp.float32), 'wq': jax.random.normal(ks[1], (D, D), dtype=jnp.float32) * w, 'bq': jax.random.normal(ks[2], (D,), dtype=jnp.float32) * w, 'wk': jax.random.normal(ks[3], (D, D), dtype=jnp.float32) * w, 'bk': jax.random.normal(ks[4], (D,), dtype=jnp.float32) * w, 'wv': jax.random.normal(ks[5], (D, D), dtype=jnp.float32) * w, 'bv': jax.random.normal(ks[6], (D,), dtype=jnp.float32) * w, 'wo': jax.random.normal(ks[7], (D, D), dtype=jnp.float32) * w, 'bo': jax.random.normal(ks[8], (D,), dtype=jnp.float32) * w}
    _L0_attn_in = _L0_attn_setup()

    def _L0_ffn_setup():
        import jax, jax.numpy as jnp
        import numpy as np
        B, T, C, I, E = (4, 256, 128, 352, 7)

        def _swiglu(h, w1, w2, w3):
            return jax.nn.silu(h @ w1.T) * (h @ w3.T) @ w2.T
        key = jax.random.key(seed)
        ks = jax.random.split(key, 9)
        sc_c = 1.0 / np.sqrt(C)
        sc_i = 1.0 / np.sqrt(I)
        return {'x': jax.random.normal(ks[0], (B, T, C), jnp.float32), 'router_w': jax.random.normal(ks[1], (E, C), jnp.float32) * sc_c, 'routing_bias': jnp.zeros((E,), jnp.float32), 'sw1': jax.random.normal(ks[2], (I, C), jnp.float32) * sc_c, 'sw2': jax.random.normal(ks[3], (C, I), jnp.float32) * sc_i, 'sw3': jax.random.normal(ks[4], (I, C), jnp.float32) * sc_c, 'ew1': jax.random.normal(ks[5], (E, I, C), jnp.float32) * sc_c, 'ew2': jax.random.normal(ks[6], (E, C, I), jnp.float32) * sc_i, 'ew3': jax.random.normal(ks[7], (E, I, C), jnp.float32) * sc_c}
    _L0_ffn_in = _L0_ffn_setup()

    def _L1_attn_setup():
        import math
        import jax, jax.numpy as jnp
        import numpy as np
        N_HEADS = 16
        D_EMBED = 128
        key = jax.random.key(seed)
        ks = jax.random.split(key, 5)
        b, l, d = (2, 256, D_EMBED)
        return {'x': jax.random.normal(ks[0], (b, l, d), dtype=jnp.float32), 'w_in': jax.random.normal(ks[1], (3 * d, d), dtype=jnp.float32) * 0.02, 'b_in': jax.random.normal(ks[2], (3 * d,), dtype=jnp.float32) * 0.02, 'w_out': jax.random.normal(ks[3], (d, d), dtype=jnp.float32) * 0.02, 'b_out': jax.random.normal(ks[4], (d,), dtype=jnp.float32) * 0.02}
    _L1_attn_in = _L1_attn_setup()

    def _L1_ffn_setup():
        import jax, jax.numpy as jnp
        import numpy as np
        INPUT_SIZE = 128
        OUTPUT_SIZE = 128
        key = jax.random.key(seed)
        kx, kt, kp, ktn, kpn = jax.random.split(key, 5)
        x = jax.random.normal(kx, (8, 256, INPUT_SIZE), dtype=jnp.float32)
        theta = jax.random.normal(kt, (INPUT_SIZE, OUTPUT_SIZE), dtype=jnp.float32) * 0.02
        phi = jax.random.normal(kp, (INPUT_SIZE, OUTPUT_SIZE), dtype=jnp.float32) * 0.02
        theta_noise = jax.random.normal(ktn, (INPUT_SIZE, OUTPUT_SIZE), dtype=jnp.float32) * 0.01
        phi_noise = jax.random.normal(kpn, (INPUT_SIZE, OUTPUT_SIZE), dtype=jnp.float32) * 0.01
        return {'x': x, 'theta': theta, 'phi': phi, 'theta_noise': theta_noise, 'phi_noise': phi_noise}
    _L1_ffn_in = _L1_ffn_setup()
    _d = {'L0_attn_x': _L0_attn_in['x'], 'L0_attn_wq': _L0_attn_in['wq'], 'L0_attn_bq': _L0_attn_in['bq'], 'L0_attn_wk': _L0_attn_in['wk'], 'L0_attn_bk': _L0_attn_in['bk'], 'L0_attn_wv': _L0_attn_in['wv'], 'L0_attn_bv': _L0_attn_in['bv'], 'L0_attn_wo': _L0_attn_in['wo'], 'L0_attn_bo': _L0_attn_in['bo'], 'L0_ffn_router_w': _L0_ffn_in['router_w'], 'L0_ffn_routing_bias': _L0_ffn_in['routing_bias'], 'L0_ffn_sw1': _L0_ffn_in['sw1'], 'L0_ffn_sw2': _L0_ffn_in['sw2'], 'L0_ffn_sw3': _L0_ffn_in['sw3'], 'L0_ffn_ew1': _L0_ffn_in['ew1'], 'L0_ffn_ew2': _L0_ffn_in['ew2'], 'L0_ffn_ew3': _L0_ffn_in['ew3'], 'L1_attn_w_in': _L1_attn_in['w_in'], 'L1_attn_b_in': _L1_attn_in['b_in'], 'L1_attn_w_out': _L1_attn_in['w_out'], 'L1_attn_b_out': _L1_attn_in['b_out'], 'L1_ffn_theta': _L1_ffn_in['theta'], 'L1_ffn_phi': _L1_ffn_in['phi'], 'L1_ffn_theta_noise': _L1_ffn_in['theta_noise'], 'L1_ffn_phi_noise': _L1_ffn_in['phi_noise']}
    _x0 = _d['L0_attn_x']
    _d['L0_attn_x'] = jax.random.normal(jax.random.fold_in(jax.random.key(seed), 1), (4, 1024, 128), dtype=_x0.dtype)
    del _x0
    return _d

def reference(L0_attn_x, L0_attn_wq, L0_attn_bq, L0_attn_wk, L0_attn_bk, L0_attn_wv, L0_attn_bv, L0_attn_wo, L0_attn_bo, L0_ffn_router_w, L0_ffn_routing_bias, L0_ffn_sw1, L0_ffn_sw2, L0_ffn_sw3, L0_ffn_ew1, L0_ffn_ew2, L0_ffn_ew3, L1_attn_w_in, L1_attn_b_in, L1_attn_w_out, L1_attn_b_out, L1_ffn_theta, L1_ffn_phi, L1_ffn_theta_noise, L1_ffn_phi_noise):

    def _L0_attn_ref(x, wq, bq, wk, bk, wv, bv, wo, bo):
        import jax, jax.numpy as jnp
        import numpy as np
        NUM_HEADS = 16

        def _heads(t, B, N, H, hd):
            return t.reshape(B, N, H, hd).transpose(0, 2, 1, 3)
        B, N, D = x.shape
        H = NUM_HEADS
        hd = D // H
        q = _heads(x @ wq.T + bq, B, N, H, hd)
        k = _heads(x @ wk.T + bk, B, N, H, hd)
        v = _heads(x @ wv.T + bv, B, N, H, hd)
        q2 = jnp.sum(q * q, axis=-1)
        k2 = jnp.sum(k * k, axis=-1)
        qk = jnp.einsum('bhid,bhjd->bhij', q, k)
        d2 = jnp.maximum(q2[..., :, None] + k2[..., None, :] - 2.0 * qk, 1e-12)
        attn = jax.nn.softmax(-jnp.sqrt(d2), axis=-1)
        out = jnp.einsum('bhij,bhjd->bhid', attn, v)
        out = out.transpose(0, 2, 1, 3).reshape(B, N, D)
        return out @ wo.T + bo

    def _L0_ffn_ref(x, router_w, routing_bias, sw1, sw2, sw3, ew1, ew2, ew3):
        import jax, jax.numpy as jnp
        import numpy as np
        B, T, C, I, E = (4, 256, 128, 352, 7)

        def _swiglu(h, w1, w2, w3):
            return jax.nn.silu(h @ w1.T) * (h @ w3.T) @ w2.T
        b, t, c = x.shape
        shared_out = _swiglu(x, sw1, sw2, sw3)
        logits = jnp.clip(x @ router_w.T + routing_bias, -50.0, 50.0)
        probs = jax.nn.sigmoid(logits)
        num_switched = 1
        topk_probs, topk_idx = jax.lax.top_k(probs, num_switched)
        topk_probs = jnp.clip(topk_probs, 1e-08, 1.0 - 1e-08)
        xf = x.reshape(-1, c)
        sel = topk_idx.reshape(-1)
        p = topk_probs.reshape(-1)
        switched = jnp.zeros_like(xf)
        n_experts = ew1.shape[0]
        for e in range(n_experts):
            y = _swiglu(xf, ew1[e], ew2[e], ew3[e])
            w = jnp.where(sel == e, p, 0.0)
            switched = switched + w[:, None] * y
        switched = switched.reshape(b, t, c)
        total_weight = 0.5 + topk_probs.sum(axis=-1)
        total_weight = jnp.clip(total_weight[..., None] + 1e-08, 0.5, 2.0)
        return 0.5 / total_weight * shared_out + switched / total_weight

    def _L1_attn_ref(x, w_in, b_in, w_out, b_out):
        import math
        import jax, jax.numpy as jnp
        import numpy as np
        N_HEADS = 16
        D_EMBED = 128
        b, l, d = x.shape
        h = N_HEADS
        scale = 1.0 / math.sqrt(d // h)
        x_proj = (x @ w_in.T + b_in).reshape(b, l, h, -1)
        q, k, v = jnp.split(x_proj, 3, axis=-1)
        att = jnp.einsum('blhd,bmhd->blmh', q, k) * scale
        att = jax.nn.softmax(att, axis=2)
        opt = jnp.einsum('blmh,blhd->blhd', att, v).reshape(b, l, d)
        return opt @ w_out.T + b_out

    def _L1_ffn_ref(x, theta, phi, theta_noise, phi_noise):
        import jax, jax.numpy as jnp
        import numpy as np
        INPUT_SIZE = 128
        OUTPUT_SIZE = 128
        real = jnp.einsum('bti,io->bto', x, jnp.cos(theta + theta_noise))
        imag = jnp.einsum('bti,io->bto', x, jnp.sin(phi + phi_noise))
        return jnp.sqrt(real * real + imag * imag)
    x = L0_attn_x
    xn = _layernorm(x, axis=-1)
    x = x + _L0_attn_ref(xn, L0_attn_wq, L0_attn_bq, L0_attn_wk, L0_attn_bk, L0_attn_wv, L0_attn_bv, L0_attn_wo, L0_attn_bo) + _L0_ffn_ref(xn, L0_ffn_router_w, L0_ffn_routing_bias, L0_ffn_sw1, L0_ffn_sw2, L0_ffn_sw3, L0_ffn_ew1, L0_ffn_ew2, L0_ffn_ew3)
    xn = _layernorm(x, axis=-1)
    x = x + _L1_attn_ref(xn, L1_attn_w_in, L1_attn_b_in, L1_attn_w_out, L1_attn_b_out) + _L1_ffn_ref(xn, L1_ffn_theta, L1_ffn_phi, L1_ffn_theta_noise, L1_ffn_phi_noise)
    return x

_drawn_inputs = setup_inputs


def setup_inputs(seed=0):
    import zlib

    import numpy as np

    out = dict(_drawn_inputs(seed))
    spreads = {'L0_ffn_routing_bias': (0.0, 0.1)}
    factors = {'L0_attn_wq': 8.0,
     'L0_attn_bq': 8.0,
     'L0_attn_wk': 8.0,
     'L0_attn_bk': 8.0,
     'L0_attn_wv': 8.0,
     'L0_attn_bv': 8.0,
     'L0_attn_wo': 8.0,
     'L0_attn_bo': 2.966,
     'L1_attn_b_in': 8.0,
     'L1_attn_b_out': 3.105,
     'L1_ffn_theta': 8.0,
     'L1_ffn_theta_noise': 8.0}
    for name, (base, spread) in spreads.items():
        noise = np.random.default_rng([zlib.crc32(name.encode()), seed]).standard_normal(out[name].shape)
        drawn = base * np.exp(spread * noise) if base else spread * noise
        out[name] = jnp.asarray(drawn.astype(out[name].dtype))
    for name, factor in factors.items():
        out[name] = (out[name] * factor).astype(out[name].dtype)
    return out
```

```python
from contextlib import ExitStack, contextmanager

import concourse.bass as bass
import numpy as np
from concourse import mybir

F32 = mybir.dt.float32
BF16 = mybir.dt.bfloat16
I32 = mybir.dt.int32
ALU = mybir.AluOpType
ACT = mybir.ActivationFunctionType
AX = mybir.AxisListType.X

P = 128
B, N, D = 4, 1024, 128
H = 16
HD = D // H
NT = N // P
HEADS = B * H
GROUP = 4
GROUPS = HEADS // GROUP
E, I = 7, 352
NE = E + 1
ICH = [(0, 128), (128, 128), (256, 96)]
EPS = 1e-5
VW = HD + 1

PAIRS = [(0, 0), (0, 1), (1, 0), (1, 1), (0, 2), (2, 0)]
SUM_ROW = len(PAIRS) * HD
ROWS = SUM_ROW + 6
KROWS = 72
SCALE1 = float(1.0 / np.sqrt(HD))
BOUND = [900.0, 80.0]

NEG_HALF_TURN = float(np.pi)
TWO_PI = [6.28125, 0.0019350051879882812, 3.0199159819e-07]
MAGIC = 12582912.0


@contextmanager
def phase_semaphores(nc):
    sems = []

    def take(name):
        sems.append(nc.alloc_semaphore(name=name))
        return sems[-1]

    yield take
    nc.clear_and_free_semaphores(sems)
    nc.all_engine_barrier()


class Chain:

    def __init__(self, eng, sem):
        self.eng, self.sem, self.base, self.count = eng, sem, 0, 0

    def per_iteration(self, index, steps):
        self.base, self.count = index * steps, 0

    def step(self, instruction):
        instruction.then_inc(self.sem, 1)
        self.count += 1

    def wait(self, passed=None):
        self.eng.wait_ge(self.sem, self.base + self.count)
        if passed is not None:
            self.eng.sem_inc(passed, 1)


def wait_alone(eng, sem, value, passed):
    eng.wait_ge(sem, value)
    eng.sem_inc(passed, 1)


def bcast(ap, axis, n):
    return ap.unsqueeze(axis).to_broadcast([*ap.shape[:axis], n, *ap.shape[axis:]])


def load_constants(nc, ctx, d, R):
    sb = lambda n, s, t=F32: ctx.enter_context(nc.sbuf_tensor(n, s, t))
    R["X"] = sb("X", [P, B * NT, D])
    R["WT"] = sb("WT", [P, B * NT, NE])
    R["ident"] = sb("ident", [P, P])
    R["blk"] = sb("blk", [P, 64])
    R["desc"] = sb("desc", [P, E])
    R["flag"] = sb("flag", [1, 2], I32)
    R["gmax"] = sb("gmax", [64, 2 * B])
    R["ones"] = sb("ones", [HEADS, 3 * N], BF16)
    R["cs"] = sb("cs", [P, 2 * D])
    names = ["wq0", "wk0", "wv0", "wo0", "wq1", "wk1", "wv1", "wo1"]
    for n in names:
        R[n] = sb(n + "_sb", [P, D])
    R["rw"] = sb("rw_sb", [P, E])
    R["rb"] = sb("rb_sb", [P, E])
    cols = ["bq0", "bk0", "bq1", "bk1"]
    for n in cols:
        R[n] = sb(n + "_sb", [P, 1])
    rows = ["bv0", "bo0", "bv1", "bo1"]
    for n in rows:
        R[n] = sb(n + "_sb", [P, D])
    R["bq0s"] = sb("bq0s", [P, 1])

    with phase_semaphores(nc) as take, ExitStack() as own:
        tmp = lambda n, s, t=F32: own.enter_context(nc.sbuf_tensor(n, s, t))
        ang = tmp("ang", [P, 2, D])
        noise = tmp("noise", [P, 2, D])
        turns = tmp("turns", [P, 2, D])
        sem = lambda n: take(n)
        loaded, angles_in, made, reduced, ones_out, trig_done = (
            sem(n) for n in ("const_loaded", "angles_in", "const_made", "angles_reduced",
                             "ones_out", "trig_done"))
        block = own.enter_context(nc.Block())
        n_loads = B + 3 + len(names) + 2 + len(cols) + len(rows)

        @block.sync
        def _(sp):
            for b in range(B):
                sp.dma_start(R["X"][:, b * NT:(b + 1) * NT, :],
                             d["x"][b * N:(b + 1) * N, :].rearrange("(t p) c -> p t c", p=P)
                             ).then_inc(loaded, 16)
            for n in ("ident", "blk", "desc"):
                sp.dma_start(R[n][:], d[n]).then_inc(loaded, 16)
            for n in names + ["rw"]:
                sp.dma_start(R[n][:], d[n]).then_inc(loaded, 16)
            for n in rows + ["rb"]:
                sp.dma_start(R[n][:], d[n].to_broadcast([P, R[n].shape[1]])).then_inc(loaded, 16)
            for n in cols:
                sp.dma_start(R[n][:], d[n]).then_inc(loaded, 16)
            sp.wait_ge(made, 1)
            for side, row in ((0, SUM_ROW), (1, SUM_ROW + 3)):
                sp.dma_start(d["stack0"][:, 1 - side, row:row + 3, :],
                             R["ones"][:].rearrange("n (r t) -> n r t", r=3)
                             ).then_inc(ones_out, 16)
            sp.wait_ge(loaded, 16 * n_loads)
            sp.wait_ge(ones_out, 32)

        @block.scalar
        def _(act):
            for i, (a, b) in enumerate((("theta", "theta_noise"), ("phi", "phi_noise"))):
                act.dma_start(ang[:, i, :], d[a]).then_inc(angles_in, 16)
                act.dma_start(noise[:, i, :], d[b]).then_inc(angles_in, 16)
            act.wait_ge(reduced, 1)
            nc.scalar.activation(R["cs"][:].rearrange("p (a c) -> p a c", a=2), ang[:, :, :],
                                 ACT.Sin).then_inc(trig_done, 1)

        @block.vector
        def _(dve):
            nc.vector.memset(R["ones"][:], 1.0).then_inc(made, 1)
            chain = Chain(dve, made)
            chain.count = 1
            chain.step(nc.vector.memset(R["gmax"][:], 0.0))
            dve.wait_ge(angles_in, 64)
            chain.step(nc.vector.tensor_tensor(ang[:, :, :], ang[:, :, :], noise[:, :, :], ALU.add))
            chain.wait()
            for i, quarter in ((0, 0.25), (1, 0.0)):
                chain.step(nc.vector.tensor_scalar(turns[:, i, :], ang[:, i, :],
                                                   float(1 / (2 * np.pi)), quarter, ALU.mult, ALU.add))
            chain.wait()
            chain.step(nc.vector.tensor_scalar(turns[:, :, :], turns[:, :, :], MAGIC, None, ALU.add))
            chain.wait()
            chain.step(nc.vector.tensor_scalar(turns[:, :, :], turns[:, :, :], MAGIC, None, ALU.subtract))
            chain.wait()
            for part in TWO_PI:
                chain.step(nc.vector.scalar_tensor_tensor(
                    out=ang[:, :, :], in0=turns[:, :, :], scalar=-part, in1=ang[:, :, :],
                    op0=ALU.mult, op1=ALU.add))
                chain.wait()
            chain.step(nc.vector.tensor_scalar(ang[:, 0, :], ang[:, 0, :], float(np.pi / 2), None, ALU.add))
            chain.wait()
            nc.vector.tensor_scalar(ang[:, :, :], ang[:, :, :], 3.1415925, -3.1415925,
                                    ALU.min, ALU.max).then_inc(reduced, 1)
            dve.wait_ge(loaded, 16 * n_loads)
            chain.step(nc.vector.tensor_scalar(R["bq0s"][:], R["bq0"][:], -2.0, None, ALU.mult))
            dve.wait_ge(trig_done, 1)


def each_batch(eng, batch):
    batch(0)
    with eng.Fori(1, B) as b:
        batch(b)


def prepare(nc, d, R, layer):
    first = layer == 0
    L = str(layer)
    with phase_semaphores(nc) as take, ExitStack() as ctx:
        sb = lambda n, s, t=F32: ctx.enter_context(nc.sbuf_tensor(n + L, s, t))
        ps = lambda n, s: ctx.enter_context(nc.psum_tensor(n + L, s, F32))
        sem = lambda n: take("p_" + n + L)
        X, WT = R["X"], R["WT"]
        stats, mv = sb("stats", [P, NT, 6]), sb("mv", [P, NT, 2])
        rstd = sb("rstd", [P, NT])
        xn = sb("xn", [P, NT, D])
        xt = sb("xt", [P, N])
        qf, kf = sb("qf", [P, N]), sb("kf", [P, N])
        qsq, ksq = sb("qsq", [P, N]), sb("ksq", [P, N])
        qp, kp = sb("qp", [P, 3, N], BF16), sb("kp", [P, 3, N], BF16)
        qr, kr = sb("qr", [P, N]), sb("kr", [P, N])
        sums, sumr, sump = sb("sums", [64, N]), sb("sumr", [64, N]), sb("sump", [64, 3, N], BF16)
        pX, pQ, pK, pV = ps("pX", [P, N]), ps("pQ", [P, N]), ps("pK", [P, N]), ps("pV", [P, N])
        if first:
            lg, pr, eq = sb("lg", [P, NT, E]), sb("pr", [P, NT, E]), sb("eq", [P, NT, E])
            vt = sb("vt", [P, H, NT, VW])
            top, wgt, inv = sb("top", [P, NT]), sb("wgt", [P, NT]), sb("inv", [P, NT])
        else:
            at, att = sb("at", [P, NT, D]), sb("att_t", [P, N])
            ri, mag = sb("ri", [P, NT, 2, D]), sb("mag", [P, NT, D])

        s_dve, s_pool, passed = sem("dve_chain"), sem("pool_chain"), sem("passed")
        at_in, att_p, att_ready, wo_done, x_ready = (
            sem(n) for n in ("at_in", "att_p", "att_ready", "wo_done", "x_ready"))
        var_ready, std_ready, xn_ready, xt_p, xt_ready, xt_kept = (
            sem(n) for n in ("var_ready", "std_ready", "xn_ready", "xt_p", "xt_ready", "xt_kept"))
        q_p, k_p, v_p, qk_f, sq_ready, sum_p, sum_out, v_out = (
            sem(n) for n in ("q_p", "k_p", "v_p", "qk_f", "sq_ready", "sum_p", "sum_out", "v_out"))
        qp_ready, kp_ready, sump_ready, stored, v_stored = (
            sem(n) for n in ("qp_ready", "kp_ready", "sump_ready", "stored", "v_stored"))
        route_p, lg_ready, e_ready, route_out = (
            sem(n) for n in ("route_p", "lg_ready", "e_ready", "route_out"))
        mix_p, mix_out, pow_ready, mag_ready, mag_used = (
            sem(n) for n in ("mix_p", "mix_out", "pow_ready", "mag_ready", "mag_used"))
        block = ctx.enter_context(nc.Block())
        stack = d["stack" + L]
        n_stores = 2 * len(PAIRS) + (6 if first else 0)

        @block.sync
        def _(sp):
            def batch(b):
                if not first:
                    sp.wait_ge(att_p, NT * b)
                    for g in range(GROUP):
                        src = d["att0"][bass.ds(b * GROUP + g, 1), :, :]
                        sp.dma_start(at[:, :, g * 32:(g + 1) * 32],
                                     src.rearrange("o (t p) c -> p (o t) c", p=P)).then_inc(at_in, 16)
                dst = stack[bass.ds(b * H, H)]
                sp.wait_ge(qp_ready, b + 1)
                for r, (_, a) in enumerate(PAIRS):
                    sp.dma_start(dst[:, 0, r * HD:(r + 1) * HD, :], qp[:, a, :]).then_inc(stored, 16)
                sp.wait_ge(kp_ready, b + 1)
                for r, (a, _) in enumerate(PAIRS):
                    sp.dma_start(dst[:, 1, r * HD:(r + 1) * HD, :], kp[:, a, :]).then_inc(stored, 16)
                if first:
                    sp.wait_ge(sump_ready, b + 1)
                    for a in range(3):
                        sp.dma_start(dst[:, 0, SUM_ROW + a, :], sump[0:H, a, :]).then_inc(stored, 16)
                        sp.dma_start(dst[:, 1, SUM_ROW + 3 + a, :], sump[32:32 + H, a, :]).then_inc(stored, 16)
            each_batch(sp, batch)
            sp.wait_ge(stored, 16 * n_stores * B)
            if first:
                sp.wait_ge(v_stored, 16 * B)

        @block.tensor
        def _(pe):
            def batch(b):
                if not first:
                    pe.wait_ge(at_in, 16 * GROUP * (b + 1))
                    pe.wait_ge(qk_f, 2 * b)
                    for t in range(NT):
                        nc.tensor.transpose(pQ[:, t * P:(t + 1) * P], at[:, t, :], R["ident"][:]).then_inc(att_p, 1)
                    pe.wait_ge(att_ready, b + 1)
                    for t in range(NT):
                        mm = nc.tensor.matmul(pK[:, t * P:(t + 1) * P], att[:, t * P:(t + 1) * P],
                                              R["wo0"][:], start=True, stop=True)
                    mm.then_inc(wo_done, 1)
                pe.wait_ge(sum_out, b)
                if not first:
                    pe.wait_ge(mix_out, 4 * b)
                for t in range(NT):
                    pe.wait_ge(xn_ready, NT * b + t + 1)
                    nc.tensor.transpose(pX[:, t * P:(t + 1) * P], xn[:, t, :], R["ident"][:]).then_inc(xt_p, 1)
                if first:
                    pe.wait_ge(route_out, b)
                    pe.wait_ge(qk_f, 2 * b)
                pe.wait_ge(xt_ready, 2 * (b + 1))
                for half in range(2):
                    cols = slice(half * 512, (half + 1) * 512)
                    mm = nc.tensor.matmul(pQ[:, cols], R["wq" + L][:], xt[:, cols], start=True, stop=True)
                mm.then_inc(q_p, 1)
                if not first:
                    pe.wait_ge(x_ready, b + 1)
                for half in range(2):
                    cols = slice(half * 512, (half + 1) * 512)
                    mm = nc.tensor.matmul(pK[:, cols], R["wk" + L][:], xt[:, cols], start=True, stop=True)
                mm.then_inc(k_p, 1)
                pe.wait_ge(v_out, b)
                for t in range(NT):
                    mm = nc.tensor.matmul(pV[:, t * P:(t + 1) * P], xt[:, t * P:(t + 1) * P],
                                          R["wv" + L][:], start=True, stop=True)
                mm.then_inc(v_p, 1)
                pe.wait_ge(sq_ready, b + 1)
                for half in range(2):
                    cols = slice(half * 512, (half + 1) * 512)
                    nc.tensor.matmul(pX[0:32, cols], R["blk"][:, 0:32], qsq[:, cols], start=True, stop=True)
                    mm = nc.tensor.matmul(pX[32:64, cols], R["blk"][:, 32:64], ksq[:, cols], start=True, stop=True)
                mm.then_inc(sum_p, 1)
                if first:
                    pe.wait_ge(qk_f, 2 * b + 2)
                    for t in range(NT):
                        mm = nc.tensor.matmul(pQ[:, t * 8:t * 8 + E], xt[:, t * P:(t + 1) * P],
                                              R["rw"][:], start=True, stop=True)
                    mm.then_inc(route_p, 1)
                else:
                    pe.wait_ge(sum_out, b + 1)
                    for r in range(4):
                        if r >= 2:
                            pe.wait_ge(mix_out, 4 * b + r - 1)
                        for j in range(2):
                            t, at_col = 2 * r + j, (r % 2) * 512 + j * 256
                            mm = nc.tensor.matmul(pX[:, at_col:at_col + 256], xt[:, t * P:(t + 1) * P],
                                                  R["cs"][:], start=True, stop=True)
                        mm.then_inc(mix_p, 1)
            each_batch(pe, batch)

        @block.scalar
        def _(act):
            def batch(b):
                if not first:
                    for half in range(2):
                        cols = slice(half * 512, (half + 1) * 512)
                        act.wait_ge(att_p, NT * b + 4 * (half + 1))
                        cp = nc.scalar.activation(att[:, cols], pQ[:, cols], ACT.Copy)
                    cp.then_inc(att_ready, 1)
                act.wait_ge(var_ready, b + 1)
                nc.scalar.activation(rstd[:], mv[:, :, 1], ACT.Sqrt).then_inc(std_ready, 1)
                if first:
                    act.wait_ge(route_p, b)
                    act.wait_ge(xt_kept, b)
                else:
                    act.wait_ge(mix_p, 4 * b)
                for half in range(2):
                    cols = slice(half * 512, (half + 1) * 512)
                    act.wait_ge(xt_p, NT * b + 4 * (half + 1))
                    nc.scalar.activation(xt[:, cols], pX[:, cols], ACT.Copy).then_inc(xt_ready, 1)
                act.wait_ge(q_p, b + 1)
                act.wait_ge(qp_ready, b)
                if first:
                    nc.scalar.activation(qf[:], pQ[:], ACT.Identity, bias=R["bq0s"][:], scale=-2.0).then_inc(qk_f, 1)
                else:
                    nc.scalar.activation(qf[:], pQ[:], ACT.Identity, bias=R["bq1"][:]).then_inc(qk_f, 1)
                act.wait_ge(k_p, b + 1)
                act.wait_ge(kp_ready, b)
                nc.scalar.activation(kf[:], pK[:], ACT.Identity, bias=R["bk" + L][:]).then_inc(qk_f, 1)
                act.wait_ge(sum_p, b)
                act.wait_ge(qk_f, 2 * b + 2)
                nc.scalar.activation(qsq[:], qf[:], ACT.Square)
                nc.scalar.activation(ksq[:], kf[:], ACT.Square).then_inc(sq_ready, 1)
                if first:
                    act.wait_ge(lg_ready, b + 1)
                    nc.scalar.activation(pr[:, :, :], lg[:, :, :], ACT.Exp, scale=-1.0).then_inc(e_ready, 1)
                else:
                    for r in range(4):
                        act.wait_ge(mix_p, 4 * b + r + 1)
                        if r == 0:
                            act.wait_ge(pow_ready, b)
                        nc.scalar.activation(ri[:, 2 * r:2 * r + 2, :, :].rearrange("p t a c -> p (t a c)"),
                                             pX[:, (r % 2) * 512:(r % 2 + 1) * 512], ACT.Square
                                             ).then_inc(mix_out, 1)
                    act.wait_ge(pow_ready, b + 1)
                    nc.scalar.activation(mag[:, :, :], mag[:, :, :], ACT.Sqrt).then_inc(mag_ready, 1)
            each_batch(act, batch)

        @block.gpsimd
        def _(pool):
            steps = 3
            def batch(b):
                chain = Chain(pool, s_pool)
                chain.per_iteration(b, steps)
                if first:
                    wait_alone(pool, xt_ready, 2 * (b + 1), passed)
                    nc.gpsimd.tensor_copy(R["XNT"][:, bass.ds(b * N, N)], xt[:]).then_inc(xt_kept, 1)
                pool.wait_ge(stored, 16 * n_stores * b)
                wait_alone(pool, qk_f, 2 * b + 2, passed)
                chain.step(nc.gpsimd.tensor_copy(kp[:, 0, :], kf[:]))
                chain.wait()
                chain.step(nc.gpsimd.tensor_tensor(kr[:], kf[:], kp[:, 0, :], ALU.subtract))
                chain.wait(passed)
                chain.step(nc.gpsimd.tensor_copy(kp[:, 1, :], kr[:]))
                chain.wait()
                assert chain.count == steps
                nc.gpsimd.tensor_tensor(kp[:, 2, :], kr[:], kp[:, 1, :], ALU.subtract).then_inc(kp_ready, 1)
                if first:
                    pool.wait_ge(v_out, b + 1)
                    pool.dma_start(d["v0"][bass.ds(b * H, H)].rearrange("h p w -> p h w"),
                                   vt[:].rearrange("p h t w -> p h (t w)")).then_inc(v_stored, 16)
            each_batch(pool, batch)

        @block.vector
        def _(dve):
            chain = Chain(dve, s_dve)
            if first:
                chain.step(nc.vector.memset(vt[:].rearrange("p h t w -> p (h t) w")[:, :, HD], 1.0))
            before = chain.count
            steps = 22 if first else 8
            def batch(b):
                chain.base, chain.count = b * steps + before, 0
                xb = X[:, bass.ds(b * NT, NT), :]
                if not first:
                    dve.wait_ge(wo_done, b + 1)
                    chain.step(nc.vector.tensor_tensor(xb, xb, pK[:].rearrange("p (t c) -> p t c", c=D), ALU.add))
                    chain.wait()
                    nc.vector.tensor_tensor(xb, xb, bcast(R["bo0"][:], 1, NT), ALU.add).then_inc(x_ready, 1)
                    wait_alone(dve, x_ready, b + 1, passed)
                for t in range(NT):
                    st = nc.vector.bn_stats(stats[:, t, :], X[:, bass.ds(b * NT + t, 1), :].rearrange("p o c -> p (o c)"))
                chain.step(st)
                dve.wait_ge(xn_ready, NT * b)
                chain.wait(passed)
                for t in range(NT):
                    st = nc.vector.bn_aggr(mv[:, t, :], stats[:, t, :])
                chain.step(st)
                chain.wait()
                nc.vector.tensor_scalar(mv[:, :, 1], mv[:, :, 1], EPS, None, ALU.add).then_inc(var_ready, 1)
                dve.wait_ge(std_ready, b + 1)
                chain.step(nc.vector.reciprocal(rstd[:], rstd[:]))
                chain.wait()
                dve.wait_ge(xt_p, NT * b)
                for t in range(NT):
                    nc.vector.tensor_scalar(xn[:, t, :], X[:, bass.ds(b * NT + t, 1), :].rearrange("p o c -> p (o c)"),
                                            mv[:, t, 0:1], rstd[:, t:t + 1],
                                            ALU.subtract, ALU.mult).then_inc(xn_ready, 1)
                dve.wait_ge(qk_f, 2 * b + 1)
                dve.wait_ge(stored, 16 * n_stores * b)
                chain.step(nc.vector.tensor_copy(qp[:, 0, :], qf[:]))
                chain.wait()
                chain.step(nc.vector.tensor_tensor(qr[:], qf[:], qp[:, 0, :], ALU.subtract))
                chain.wait()
                chain.step(nc.vector.tensor_copy(qp[:, 1, :], qr[:]))
                chain.wait()
                nc.vector.tensor_tensor(qp[:, 2, :], qr[:], qp[:, 1, :], ALU.subtract).then_inc(qp_ready, 1)
                dve.wait_ge(v_p, b + 1)
                if first:
                    dve.wait_ge(v_stored, 16 * b)
                    for t in range(NT):
                        va = nc.vector.tensor_tensor(vt[:, :, t, 0:HD],
                                                     pV[:, t * P:(t + 1) * P].rearrange("p (h e) -> p h e", e=HD),
                                                     R["bv0"][:].rearrange("p (h e) -> p h e", e=HD), ALU.add)
                    va.then_inc(v_out, 1)
                else:
                    nc.vector.tensor_tensor(R["V1"][:, bass.ds(b * NT, NT), :],
                                            pV[:].rearrange("p (t c) -> p t c", c=D),
                                            bcast(R["bv1"][:], 1, NT), ALU.add).then_inc(v_out, 1)
                dve.wait_ge(sum_p, b + 1)
                nc.vector.tensor_copy(sums[:], pX[0:64, :]).then_inc(sum_out, 1)
                dve.wait_ge(sum_out, b + 1)
                gm = R["gmax"][:, bass.ds(b + layer * B, 1)]
                chain.step(nc.vector.tensor_reduce(gm, sums[:], axis=AX, op=ALU.max))
                if first:
                    chain.step(nc.vector.tensor_copy(sump[:, 0, :], sums[:]))
                    chain.wait()
                    chain.step(nc.vector.tensor_tensor(sumr[:], sums[:], sump[:, 0, :], ALU.subtract))
                    chain.wait()
                    chain.step(nc.vector.tensor_copy(sump[:, 1, :], sumr[:]))
                    chain.wait()
                    nc.vector.tensor_tensor(sump[:, 2, :], sumr[:], sump[:, 1, :], ALU.subtract).then_inc(sump_ready, 1)
                    dve.wait_ge(route_p, b + 1)
                    nc.vector.tensor_tensor(lg[:, :, :], pQ[:, 0:64].rearrange("p (t e) -> p t e", e=8)[:, :, 0:E],
                                            bcast(R["rb"][:], 1, NT), ALU.add).then_inc(route_out, 1)
                    dve.wait_ge(route_out, b + 1)
                    nc.vector.tensor_scalar(lg[:, :, :], lg[:, :, :], -50.0, 50.0, ALU.max, ALU.min).then_inc(lg_ready, 1)
                    dve.wait_ge(e_ready, b + 1)
                    chain.step(nc.vector.tensor_scalar(pr[:, :, :], pr[:, :, :], 1.0, None, ALU.add))
                    chain.wait()
                    chain.step(nc.vector.reciprocal(pr[:, :, :], pr[:, :, :]))
                    chain.wait()
                    chain.step(nc.vector.tensor_reduce(top[:], pr[:, :, :], axis=AX, op=ALU.max))
                    chain.wait()
                    chain.step(nc.vector.tensor_tensor(eq[:, :, :], pr[:, :, :], bcast(top[:], 2, E), ALU.is_equal))
                    chain.wait()
                    chain.step(nc.vector.tensor_tensor(eq[:, :, :], eq[:, :, :], bcast(R["desc"][:], 1, NT), ALU.mult))
                    chain.wait()
                    chain.step(nc.vector.tensor_reduce(inv[:], eq[:, :, :], axis=AX, op=ALU.max))
                    chain.wait()
                    chain.step(nc.vector.tensor_tensor(eq[:, :, :], eq[:, :, :], bcast(inv[:], 2, E), ALU.is_equal))
                    chain.step(nc.vector.tensor_scalar(top[:], top[:], 1e-8, 1.0 - 1e-8, ALU.max, ALU.min))
                    chain.wait()
                    chain.step(nc.vector.tensor_scalar(inv[:], top[:], 0.5, 1e-8, ALU.add, ALU.add))
                    chain.wait()
                    chain.step(nc.vector.tensor_scalar(inv[:], inv[:], 0.5, 2.0, ALU.max, ALU.min))
                    chain.wait()
                    chain.step(nc.vector.reciprocal(inv[:], inv[:]))
                    chain.wait()
                    wb = WT[:, bass.ds(b * NT, NT), :]
                    nc.vector.tensor_scalar(wb[:, :, 0], inv[:], 0.25, None, ALU.mult)
                    chain.step(nc.vector.scalar_tensor_tensor(out=wgt[:], in0=top[:], scalar=0.5, in1=inv[:],
                                                              op0=ALU.mult, op1=ALU.mult))
                    chain.wait()
                    nc.vector.tensor_tensor(wb[:, :, 1:NE], eq[:, :, :], bcast(wgt[:], 2, E), ALU.mult)
                else:
                    dve.wait_ge(mix_out, 4 * b + 4)
                    dve.wait_ge(mag_used, b)
                    nc.vector.tensor_tensor(mag[:, :, :], ri[:, :, 0, :], ri[:, :, 1, :], ALU.add).then_inc(pow_ready, 1)
                    dve.wait_ge(mag_ready, b + 1)
                    nc.vector.tensor_tensor(xb, xb, mag[:, :, :], ALU.add).then_inc(mag_used, 1)
                assert chain.count == steps, chain.count
            each_batch(dve, batch)


def guard(nc, R, layer):
    L = str(layer)
    with phase_semaphores(nc) as take, ExitStack() as ctx:
        top = ctx.enter_context(nc.sbuf_tensor("gtop" + L, [64, 1], F32))
        over = ctx.enter_context(nc.sbuf_tensor("gover" + L, [1, 1], F32))
        pt = ctx.enter_context(nc.psum_tensor("gpt" + L, [1, 64], F32))
        top_ready = take("gtop_ready" + L)
        turned = take("gturned" + L)
        chain_sem = take("gchain" + L)
        block = ctx.enter_context(nc.Block())

        @block.tensor
        def _(pe):
            pe.wait_ge(top_ready, 1)
            nc.tensor.transpose(pt[:], top[:], R["ident"][0:64, 0:64]).then_inc(turned, 1)

        @block.vector
        def _(dve):
            chain = Chain(dve, chain_sem)
            nc.vector.tensor_reduce(top[:], R["gmax"][:, layer * B:(layer + 1) * B], axis=AX,
                                    op=ALU.max).then_inc(top_ready, 1)
            dve.wait_ge(turned, 1)
            chain.step(nc.vector.tensor_reduce(over[:], pt[:], axis=AX, op=ALU.max))
            chain.wait()
            chain.step(nc.vector.tensor_scalar(over[:], over[:], BOUND[layer], None, ALU.is_gt))
            chain.wait()
            chain.step(nc.vector.tensor_copy(R["flag"][:, layer:layer + 1], over[:]))
            chain.wait()


CH = 8
RING = 3


def ring_slot(p):
    return p % RING


def ring_before(p):
    last = [max(x for x in range(GROUP * CH) if x % RING == s) for s in range(RING)]
    return RING if p >= RING else p + GROUP * CH - last[p]


def attention0(nc, d, R):
    layer, L, lag = 0, "0", GROUP
    with phase_semaphores(nc) as take, ExitStack() as ctx:
        sb = lambda n, s, t=F32: ctx.enter_context(nc.sbuf_tensor(n + L, s, t))
        ps = lambda n, s: ctx.enter_context(nc.psum_tensor(n + L, s, F32))
        sem = lambda n: take("a0_" + n)
        S = [sb(f"scores{i}", [P, CH * N]) for i in range(GROUP)]
        stk = [sb(f"stk{i}", [KROWS, 2, N], BF16) for i in range(GROUP)]
        val = [sb(f"val{i}", [P, CH, VW]) for i in range(GROUP)]
        ot = sb("ot", [P, 256])
        rden = sb("rden", [P, GROUP, NT])
        attg = sb("attg", [P, NT, 32])
        mcol = sb("mcol", [P, 1])
        ring = [ps(f"ring{i}", [P, N]) for i in range(RING)]
        pvb = [ps(f"pvb{i}", [P, 512]) for i in range(2)]
        stk_in = [sem(f"stk_in{i}") for i in range(GROUP)]
        val_in = [sem(f"val_in{i}") for i in range(GROUP)]
        qk_done, evac_done, root_done, exp_done, pv_done = (
            sem(n) for n in ("qk_done", "evac_done", "root_done", "exp_done", "pv_done"))
        zeroed = sem("zeroed")
        attg_free, g_slot = sem("attg_free"), sem("g_slot")
        cleared, ot_ready, turned, rden_ready, att_ready, att_out = (
            sem(n) for n in ("cleared", "ot_ready", "turned", "rden_ready", "att_ready", "att_out"))
        g_in, g_s, g_copied, g_root, g_max, g_exp, g_turn, g_pt, g_pv, g_rd, g_att, g_out = (
            sem("g_" + n) for n in ("in", "s", "copied", "root", "max", "exp", "turn", "pt",
                                    "pv", "rd", "att", "out"))
        block = ctx.enter_context(nc.Block())
        Q, K = 0, 1
        CHG = GROUP * CH

        def qk(pe, group, place, wait_ring=True):
            pe.wait_ge(stk_in[place], 16 * (group + 1))
            for j in range(CH):
                yield
                p = place * CH + j
                if wait_ring or p >= RING:
                    pe.wait_ge(evac_done, CHG * group + p - ring_before(p) + 1)
                for half in range(2):
                    cols = slice(half * 512, (half + 1) * 512)
                    mm = nc.tensor.matmul(ring[ring_slot(p)][:, cols], stk[place][:, K, j * P:(j + 1) * P],
                                          stk[place][:, Q, cols], start=True, stop=True)
                mm.then_inc(qk_done, 1)

        def pv(pe, group, place, j):
            if j == 0:
                pe.wait_ge(val_in[place], 16 * (group + 1))
                if place >= 2:
                    pe.wait_ge(att_ready, GROUP * group + place - 1)
                pe.wait_ge(exp_done, GROUP * group + place + 1)
            for c in range(4):
                mm = nc.tensor.matmul(pvb[place % 2][32 * c:32 * c + VW, 0:256], val[place][:, j, :],
                                      S[place][:, j * N + c * 256:j * N + (c + 1) * 256],
                                      start=(j == 0), stop=(j == CH - 1))
            mm.then_inc(pv_done, 1)

        def turn(pe, group, place):
            pe.wait_ge(ot_ready, GROUP * group + place + 1)
            for t in range(2):
                mm = nc.tensor.transpose(pvb[place % 2][:, 256 + t * P:256 + (t + 1) * P],
                                         ot[:, t * P:(t + 1) * P], R["ident"][:])
            mm.then_inc(turned, 1)

        def pe_group(pe, group, last):
            for place in range(GROUP):
                ahead = place + lag
                go = not last or ahead < GROUP
                steps = qk(pe, group + ahead // GROUP, ahead % GROUP) if go else None
                if go:
                    next(steps)
                for j in range(CH):
                    pv(pe, group, place, j)
                    if j == 3 and place:
                        turn(pe, group, place - 1)
                    if go:
                        next(steps, None)
            turn(pe, group, GROUP - 1)
            if not last:
                pe.wait_ge(att_ready, GROUP * group + GROUP)

        def take_out(dve, group, place):
            dve.wait_ge(pv_done, CHG * group + (place + 1) * CH)
            nc.vector.tensor_copy(ot[:], pvb[place % 2][:, 0:256]).then_inc(ot_ready, 1)

        def divide(dve, group, place):
            dve.wait_ge(turned, GROUP * group + place + 1)
            if place == 0:
                dve.wait_ge(attg_free, group + 1)
            t = pvb[place % 2][:, 256:512].rearrange("p (k w) -> p k w", w=32)
            nc.vector.reciprocal(rden[:, place, :], t[:, :, HD]).then_inc(rden_ready, 1)
            dve.wait_ge(rden_ready, GROUP * group + place + 1)
            nc.vector.tensor_tensor(attg[:, :, place * HD:(place + 1) * HD], t[:, :, 0:HD],
                                    bcast(rden[:, place, :], 2, HD), ALU.mult).then_inc(att_ready, 1)

        def evac(dve, group, place, j, wait_free):
            p = place * CH + j
            dve.wait_ge(qk_done, CHG * group + p + 1)
            if wait_free:
                dve.wait_ge(pv_done, CHG * (group - 1) + p + 1)
            nc.vector.tensor_scalar(S[place][:, j * N:(j + 1) * N], ring[ring_slot(p)][:], 1e-12, None,
                                    ALU.max).then_inc(evac_done, 1)

        def dve_group(dve, group, last):
            for place in range(GROUP):
                if not last:
                    for j in range(CH):
                        evac(dve, group + 1, place, j, True)
                        if j == 5 and place:
                            divide(dve, group, place - 1)
                elif place:
                    divide(dve, group, place - 1)
                take_out(dve, group, place)
            divide(dve, group, GROUP - 1)

        def store_out(pool, group):
            pool.wait_ge(att_ready, GROUP * group + GROUP)
            for t in range(2):
                dst = d["att" + L][bass.ds(group, 1), :, :].rearrange(
                    "o (c t p) w -> t p (o c) w", c=4, t=2)[t]
                pool.dma_start(dst, attg[:, 4 * t:4 * t + 4, :]).then_inc(att_out, 16)
            pool.wait_ge(att_out, 32 * (group + 1))
            pool.sem_inc(attg_free, 1)

        def general(eng, which):
            if which == "dve":
                eng.sem_inc(g_att, 1)
            if which == "pool":
                eng.sem_inc(g_slot, 1)
            with eng.Fori(0, GROUPS) as u:
                with eng.Fori(0, GROUP) as h:
                    n = u * GROUP + h
                    if which == "sp":
                        eng.wait_ge(g_att, NT * n + 1)
                        eng.dma_start(stk[0][0:ROWS], d["stack" + L][bass.ds(n, 1), :, 0:ROWS, :]
                                      .rearrange("o s r t -> (o r) s t")).then_inc(g_in, 16)
                        eng.dma_start(val[0][:], d["v" + L][bass.ds(n, 1)]
                                      .rearrange("o p (j w) -> (o p) j w", w=VW)).then_inc(g_in, 16)
                    if which == "pool":
                        eng.wait_ge(g_att, NT * (n + 1) + 1)
                        eng.dma_start(d["att" + L][bass.ds(u, 1), :, bass.ds(h * HD, HD)]
                                      .rearrange("o (t p) w -> p (o t) w", p=P),
                                      attg[:, :, 0:HD]).then_inc(g_out, 16)
                        eng.wait_ge(g_out, 16 * (n + 1))
                        eng.sem_inc(g_slot, 1)
                    for i in range(NT) if which in ("pe", "act", "dve") else ():
                        k = n * NT + i
                        if which == "pe":
                            if i == 0:
                                eng.wait_ge(g_in, 32 * (n + 1))
                            eng.wait_ge(g_att, k + 1)
                            for half in range(2):
                                cols = slice(half * 512, (half + 1) * 512)
                                mm = nc.tensor.matmul(ring[0][:, cols], stk[0][:, Q, i * P:(i + 1) * P],
                                                      stk[0][:, K, cols], start=True, stop=True)
                            mm.then_inc(g_s, 1)
                            eng.wait_ge(g_exp, k + 1)
                            for j in range(CH):
                                mm = nc.tensor.transpose(ring[1][:, j * P:(j + 1) * P],
                                                         S[0][:, j * P:(j + 1) * P], R["ident"][:])
                            mm.then_inc(g_turn, 1)
                            eng.wait_ge(g_pt, k + 1)
                            for j in range(CH):
                                mm = nc.tensor.matmul(pvb[0][:, 0:VW], S[1][:, j * P:(j + 1) * P],
                                                      val[0][:, j, :], start=(j == 0), stop=(j == CH - 1))
                            mm.then_inc(g_pv, 1)
                        if which == "dve":
                            eng.wait_ge(g_s, k + 1)
                            nc.vector.tensor_scalar(S[0][:, 0:N], ring[0][:], 1e-12, None,
                                                    ALU.max).then_inc(g_copied, 1)
                            eng.wait_ge(g_root, k + 1)
                            nc.vector.tensor_reduce(mcol[:], S[0][:, 0:N], axis=AX, op=ALU.min).then_inc(g_max, 1)
                            eng.wait_ge(g_turn, k + 1)
                            nc.vector.tensor_copy(S[1][:, 0:N], ring[1][:]).then_inc(g_pt, 1)
                            eng.wait_ge(g_pv, k + 1)
                            nc.vector.reciprocal(rden[:, 0, 0:1], pvb[0][:, HD:VW]).then_inc(g_rd, 1)
                            eng.wait_ge(g_rd, k + 1)
                            if i == 0:
                                eng.wait_ge(g_slot, n + 1)
                            nc.vector.tensor_scalar(attg[:, i, 0:HD], pvb[0][:, 0:HD], rden[:, 0, 0:1], None,
                                                    ALU.mult).then_inc(g_att, 1)
                        if which == "act":
                            eng.wait_ge(g_copied, k + 1)
                            nc.scalar.activation(S[0][:, 0:N], S[0][:, 0:N], ACT.Sqrt).then_inc(g_root, 1)
                            eng.wait_ge(g_max, k + 1)
                            nc.scalar.activation(S[0][:, 0:N], S[0][:, 0:N], ACT.Exp, bias=mcol[:],
                                                 scale=-1.0).then_inc(g_exp, 1)

        def by_guard(eng, which, fast):
            flag = eng.value_load(R["flag"][0:1, layer:layer + 1], min_val=0, max_val=1)
            with eng.If(flag != 0):
                general(eng, which)
            with eng.Else():
                fast(eng)

        @block.sync
        def _(sp):
            sp.wait_ge(zeroed, GROUP)
            def load(group, place):
                sp.dma_start(stk[place][0:ROWS], d["stack" + L][bass.ds(group * GROUP + place, 1), :, 0:ROWS, :]
                             .rearrange("o s r t -> (o r) s t")).then_inc(stk_in[place], 16)

            def fast(sp):
                for place in range(GROUP):
                    load(0, place)
                with sp.Fori(1, GROUPS) as u:
                    for place in range(GROUP):
                        sp.wait_ge(qk_done, CHG * (u - 1) + (place + 1) * CH)
                        load(u, place)
            by_guard(sp, "sp", fast)

        @block.gpsimd
        def _(pool):
            def load(group, place):
                pool.dma_start(val[place][:], d["v" + L][bass.ds(group * GROUP + place, 1)]
                               .rearrange("o p (j w) -> (o p) j w", w=VW)).then_inc(val_in[place], 16)

            def fast(pool):
                pool.sem_inc(attg_free, 1)
                for place in range(GROUP):
                    load(0, place)
                with pool.Fori(0, GROUPS - 1) as u:
                    for place in range(GROUP):
                        pool.wait_ge(pv_done, CHG * u + (place + 1) * CH)
                        load(u + 1, place)
                    store_out(pool, u)
                store_out(pool, GROUPS - 1)
            by_guard(pool, "pool", fast)

        @block.tensor
        def _(pe):
            def fast(pe):
                pe.wait_ge(cleared, 2)
                for place in range(lag):
                    for _ in qk(pe, 0, place, wait_ring=False):
                        pass
                with pe.Fori(0, GROUPS - 1) as u:
                    pe_group(pe, u, last=False)
                pe_group(pe, GROUPS - 1, last=True)
            by_guard(pe, "pe", fast)

        @block.vector
        def _(dve):
            for i in range(GROUP):
                nc.vector.memset(stk[i][:].rearrange("r s t -> r (s t)").bitcast(F32), 0.0).then_inc(zeroed, 1)
            def fast(dve):
                for i in range(2):
                    nc.vector.memset(pvb[i][:], 0.0).then_inc(cleared, 1)
                for place in range(GROUP):
                    for j in range(CH):
                        evac(dve, 0, place, j, False)
                with dve.Fori(0, GROUPS - 1) as u:
                    dve_group(dve, u, last=False)
                dve_group(dve, GROUPS - 1, last=True)
            by_guard(dve, "dve", fast)

        @block.scalar
        def _(act):
            def fast(act):
                with act.Fori(0, GROUPS) as u:
                    for place in range(GROUP):
                        act.wait_ge(evac_done, CHG * u + (place + 1) * CH)
                        nc.scalar.activation(S[place][:], S[place][:], ACT.Sqrt).then_inc(root_done, 1)
                    for place in range(GROUP):
                        act.wait_ge(root_done, GROUP * u + place + 1)
                        nc.scalar.activation(S[place][:], S[place][:], ACT.Exp, scale=-1.0).then_inc(exp_done, 1)
            by_guard(act, "act", fast)


def attention1(nc, d, R):
    RING1, PAIR = 4, 2 * GROUP
    with phase_semaphores(nc) as take, ExitStack() as ctx:
        sb = lambda n, s, t=F32: ctx.enter_context(nc.sbuf_tensor("a1_" + n, s, t))
        sem = lambda n: take("a1_" + n)
        stk = [sb(f"stk{i}", [KROWS, 2, N], BF16) for i in range(GROUP)]
        den = [sb(f"den{i}", [P, GROUP, NT]) for i in range(2)]
        wsum = [sb(f"wsum{i}", [P, GROUP, NT]) for i in range(2)]
        top, neg = sb("top", [P, 1]), sb("neg", [P, 1])
        ring = [ctx.enter_context(nc.psum_tensor(f"a1_ring{i}", [P, N], F32)) for i in range(RING1)]
        stk_in = [sem(f"stk_in{i}") for i in range(GROUP)]
        qk_done, exp_done, inv_done, w_done, v_done = (
            sem(n) for n in ("qk_done", "exp_done", "inv_done", "w_done", "v_done"))
        zeroed = sem("zeroed")
        g_in, g_s, g_max, g_neg, g_exp, g_inv, g_w, g_v = (
            sem("g_" + n) for n in ("in", "s", "max", "neg", "exp", "inv", "w", "v"))
        block = ctx.enter_context(nc.Block())
        Q, K = 0, 1
        CHP = PAIR * NT

        def load(sp, n, place, done):
            sp.dma_start(stk[place][0:SUM_ROW], d["stack1"][bass.ds(n, 1), :, 0:SUM_ROW, :]
                         .rearrange("o s r t -> (o r) s t")).then_inc(done, 16)

        def scores(out, place, i):
            for half in range(2):
                cols = slice(half * 512, (half + 1) * 512)
                mm = nc.tensor.matmul(out[:, cols], stk[place][:, Q, i * P:(i + 1) * P],
                                      stk[place][:, K, cols], start=True, stop=True)
            return mm

        def weigh(dve, b, column, side, count, inv_sem, w_sem, v_sem):
            nc.vector.reciprocal(wsum[side][:], den[side][:]).then_inc(inv_sem, 1)
            dve.wait_ge(inv_sem, count)
            nc.vector.tensor_tensor(wsum[side][:], wsum[side][:], den[side][:], ALU.mult).then_inc(w_sem, 1)
            dve.wait_ge(w_sem, count)
            vals = R["V1"][:, bass.ds(b * NT, NT), bass.ds(column, GROUP * HD)].rearrange(
                "p t (h e) -> p t h e", e=HD)
            for h in range(GROUP):
                mul = nc.vector.tensor_tensor(vals[:, :, h, :], vals[:, :, h, :],
                                              bcast(wsum[side][:, h, :], 2, HD), ALU.mult)
            mul.then_inc(v_sem, 1)

        def general(eng, which):
            if which == "dve":
                eng.sem_inc(g_v, 1)
            with eng.Fori(0, B) as b:
                with eng.Fori(0, GROUP) as g:
                    u = b * GROUP + g
                    for h in range(GROUP):
                        n = u * GROUP + h
                        if which == "sp":
                            eng.wait_ge(g_v, u + 1)
                            load(eng, n, h, g_in)
                        for i in range(NT):
                            k = n * NT + i
                            if which == "pe":
                                if i == 0:
                                    eng.wait_ge(g_in, 16 * GROUP * (u + 1))
                                if h == 0 and i == 0:
                                    eng.wait_ge(g_v, u + 1)
                                elif i or h:
                                    eng.wait_ge(g_exp, k)
                                scores(ring[0], h, i).then_inc(g_s, 1)
                            if which == "dve":
                                eng.wait_ge(g_s, k + 1)
                                nc.vector.tensor_reduce(top[:], ring[0][:], axis=AX, op=ALU.max).then_inc(g_max, 1)
                                eng.wait_ge(g_max, k + 1)
                                nc.vector.tensor_scalar(neg[:], top[:], -SCALE1, None, ALU.mult).then_inc(g_neg, 1)
                                eng.wait_ge(g_exp, k + 1)
                            if which == "act":
                                eng.wait_ge(g_neg, k + 1)
                                nc.scalar.activation(ring[0][:], ring[0][:], ACT.Exp, scale=SCALE1, bias=neg[:],
                                                     accum_out=den[0][:, h, i:i + 1]).then_inc(g_exp, 1)
                    if which == "dve":
                        weigh(eng, b, g * GROUP * HD, 0, u + 1, g_inv, g_w, g_v)

        def by_guard(eng, which, fast):
            flag = eng.value_load(R["flag"][0:1, 1:2], min_val=0, max_val=1)
            with eng.If(flag != 0):
                general(eng, which)
            with eng.Else():
                fast(eng)

        @block.sync
        def _(sp):
            sp.wait_ge(zeroed, GROUP)
            def fast(sp):
                for place in range(GROUP):
                    load(sp, place, place, stk_in[place])
                with sp.Fori(1, GROUPS) as u:
                    for place in range(GROUP):
                        sp.wait_ge(qk_done, GROUP * NT * (u - 1) + (place + 1) * NT)
                        load(sp, u * GROUP + place, place, stk_in[place])
            by_guard(sp, "sp", fast)

        @block.tensor
        def _(pe):
            def heads(body, start):
                for h in range(PAIR):
                    pe.wait_ge(stk_in[h % GROUP], 16 * (2 * body + h // GROUP + 1))
                    for i in range(NT):
                        k = body * CHP + h * NT + i
                        if not start or h * NT + i >= RING1:
                            pe.wait_ge(exp_done, k - RING1 + 1)
                        scores(ring[(h * NT + i) % RING1], h % GROUP, i).then_inc(qk_done, 1)

            def fast(pe):
                heads(0, True)
                with pe.Fori(1, HEADS // PAIR) as body:
                    heads(body, False)
            by_guard(pe, "pe", fast)

        @block.scalar
        def _(act):
            def heads(body, start):
                for h in range(PAIR):
                    side = h // GROUP
                    if h % GROUP == 0 and not start:
                        act.wait_ge(v_done, 2 * (body - 1) + side + 1)
                    for i in range(NT):
                        k = body * CHP + h * NT + i
                        act.wait_ge(qk_done, k + 1)
                        tile = ring[(h * NT + i) % RING1]
                        nc.scalar.activation(tile[:], tile[:], ACT.Exp, scale=SCALE1,
                                             accum_out=den[side][:, h % GROUP, i:i + 1]).then_inc(exp_done, 1)

            def fast(act):
                heads(0, True)
                with act.Fori(1, HEADS // PAIR) as body:
                    heads(body, False)
            by_guard(act, "act", fast)

        @block.vector
        def _(dve):
            for i in range(GROUP):
                nc.vector.memset(stk[i][:].rearrange("r s t -> r (s t)").bitcast(F32), 0.0).then_inc(zeroed, 1)
            def fast(dve):
                with dve.Fori(0, B) as b:
                    with dve.Fori(0, 2) as half:
                        for side in range(2):
                            u = b * 4 + half * 2 + side
                            dve.wait_ge(exp_done, GROUP * NT * (u + 1))
                            weigh(dve, b, half * 2 * GROUP * HD + side * GROUP * HD, side, u + 1,
                                  inv_done, w_done, v_done)
            by_guard(dve, "dve", fast)


TB = 512
NB = B * N // TB


def experts(nc, d, R):
    with phase_semaphores(nc) as take, ExitStack() as ctx:
        sb = lambda n, s, t=F32: ctx.enter_context(nc.sbuf_tensor(n, s, t))
        ps = lambda n, s: ctx.enter_context(nc.psum_tensor(n, s, F32))
        sem = lambda n: take(n)
        XNT, X, WT = R["XNT"], R["X"], R["WT"]
        w13 = [sb(f"w13_{i}", [P, 2, I]) for i in range(2)]
        w2 = [sb(f"w2_{i}", [P, 3, D]) for i in range(2)]
        th = [sb(f"th{c}", [P, TB]) for c in range(3)]
        hid = [[sb(f"hid{i}_{c}", [P, TB]) for c in range(3)] for i in range(2)]
        p1 = [ps(f"p1_{c}", [P, TB]) for c in range(3)]
        p3 = [ps(f"p3_{c}", [P, TB]) for c in range(3)]
        py = ps("py", [P, TB])
        w_in = [sem(f"w_in{i}") for i in range(2)]
        passed = sem("w_passed")
        up_done, tanh_done, gate_done, hid_done, y_done, acc_done = (
            sem(n) for n in ("up_done", "tanh_done", "gate_done", "hid_done", "y_done", "acc_done"))
        block = ctx.enter_context(nc.Block())
        TT = TB // P

        @block.sync
        def _(sp):
            def load(e, i):
                sp.dma_start(w13[i][:], d["w13"][bass.ds(e, 1)].rearrange("o c a i -> (o c) a i")).then_inc(w_in[i], 16)
                sp.dma_start(w2[i][:], d["w2"][bass.ds(e, 1)].rearrange("o p k c -> (o p) k c")).then_inc(w_in[i], 16)
            load(0, 0)
            load(1, 1)
            with sp.Fori(1, NE // 2) as pair:
                for i in range(2):
                    sp.wait_ge(y_done, NB * (2 * (pair - 1) + i + 1))
                    load(2 * pair + i, i)

        @block.tensor
        def _(pe):
            with pe.Fori(0, NE // 2) as pair:
                for i in range(2):
                    wait_alone(pe, w_in[i], 32 * (pair + 1), passed)
                    with pe.Fori(0, NB // 2) as half:
                        for s in range(2):
                            n = (2 * pair + i) * NB + half * 2 + s
                            for c, (lo, w) in enumerate(ICH):
                                pe.wait_ge(hid_done, 3 * n + 1)
                                xs = XNT[:, bass.ds((half * 2 + s) * TB, TB)]
                                nc.tensor.matmul(p1[c][0:w, :], w13[i][:, 0, lo:lo + w], xs, start=True, stop=True)
                                nc.tensor.matmul(p3[c][0:w, :], w13[i][:, 1, lo:lo + w], xs,
                                                 start=True, stop=True).then_inc(up_done, 1)
                            pe.wait_ge(hid_done, 3 * n + 4)
                            pe.wait_ge(acc_done, n + 1)
                            for t in range(TT):
                                for c, (lo, w) in enumerate(ICH):
                                    mm = nc.tensor.matmul(py[:, t * P:(t + 1) * P], hid[s][c][0:w, t * P:(t + 1) * P],
                                                          w2[i][0:w, c, :], start=(c == 0), stop=(c == 2))
                            mm.then_inc(y_done, 1)

        @block.scalar
        def _(act):
            with act.Fori(0, NE * NB) as n:
                for c, (lo, w) in enumerate(ICH):
                    act.wait_ge(up_done, 3 * n + c + 1)
                    act.wait_ge(gate_done, 3 * n + 1)
                    nc.scalar.activation(th[c][0:w, :], p1[c][0:w, :], ACT.Tanh, scale=0.5).then_inc(tanh_done, 1)

        @block.vector
        def _(dve):
            for free in (hid_done, gate_done, acc_done):
                dve.sem_inc(free, 1)
            with dve.Fori(0, NE) as e:
                with dve.Fori(0, NB // 2) as half:
                    for s in range(2):
                        blk = half * 2 + s
                        n = e * NB + blk
                        for c, (lo, w) in enumerate(ICH):
                            dve.wait_ge(tanh_done, 3 * n + c + 1)
                            nc.vector.scalar_tensor_tensor(out=th[c][0:w, :], in0=th[c][0:w, :], scalar=1.0,
                                                           in1=p1[c][0:w, :], op0=ALU.add,
                                                           op1=ALU.mult).then_inc(gate_done, 1)
                            dve.wait_ge(gate_done, 3 * n + c + 2)
                            nc.vector.tensor_tensor(hid[s][c][0:w, :], th[c][0:w, :], p3[c][0:w, :],
                                                    ALU.mult).then_inc(hid_done, 1)
                        dve.wait_ge(y_done, n + 1)
                        for t in range(TT):
                            xt = X[:, bass.ds(blk * TT + t, 1), :].rearrange("p o c -> p (o c)")
                            wt = WT[:, bass.ds(blk * TT + t, 1), bass.ds(e, 1)].rearrange("p o c -> p (o c)")
                            st = nc.vector.scalar_tensor_tensor(out=xt, in0=py[:, t * P:(t + 1) * P], scalar=wt,
                                                                in1=xt, op0=ALU.mult, op1=ALU.add)
                        st.then_inc(acc_done, 1)
                        dve.wait_ge(acc_done, n + 2)


def finish(nc, d, R):
    with phase_semaphores(nc) as take, ExitStack() as ctx:
        sb = lambda n, s, t=F32: ctx.enter_context(nc.sbuf_tensor(n, s, t))
        ps = lambda n, s: ctx.enter_context(nc.psum_tensor(n, s, F32))
        sem = lambda n: take(n)
        V1 = R["V1"]
        att = [sb(f"fatt{i}", [P, N]) for i in range(2)]
        pT = [ps(f"fpT{i}", [P, N]) for i in range(2)]
        pO = [ps(f"fpO{i}", [P, N]) for i in range(2)]
        turned, att_ready, wo_done, added, summed, out_done = (
            sem(n) for n in ("f_turned", "f_att_ready", "f_wo_done", "f_added", "f_summed", "f_out_done"))
        block = ctx.enter_context(nc.Block())

        @block.sync
        def _(sp):
            for b in range(B):
                sp.wait_ge(summed, b + 1)
                sp.dma_start(d["out"][b * N:(b + 1) * N, :].rearrange("(t p) c -> p t c", p=P),
                             R["X"][:, b * NT:(b + 1) * NT, :]).then_inc(out_done, 16)
            sp.wait_ge(out_done, 16 * B)

        @block.tensor
        def _(pe):
            for b in range(B):
                if b >= 2:
                    pe.wait_ge(att_ready, 2 * (b - 1))
                for t in range(NT):
                    nc.tensor.transpose(pT[b % 2][:, t * P:(t + 1) * P], V1[:, b * NT + t, :],
                                        R["ident"][:]).then_inc(turned, 1)
                if b >= 2:
                    pe.wait_ge(added, b - 1)
                pe.wait_ge(att_ready, 2 * (b + 1))
                for t in range(NT):
                    mm = nc.tensor.matmul(pO[b % 2][:, t * P:(t + 1) * P], att[b % 2][:, t * P:(t + 1) * P],
                                          R["wo1"][:], start=True, stop=True)
                mm.then_inc(wo_done, 1)

        @block.scalar
        def _(act):
            for b in range(B):
                if b >= 2:
                    act.wait_ge(wo_done, b - 1)
                for half in range(2):
                    cols = slice(half * 512, (half + 1) * 512)
                    act.wait_ge(turned, NT * b + 4 * (half + 1))
                    nc.scalar.activation(att[b % 2][:, cols], pT[b % 2][:, cols], ACT.Copy).then_inc(att_ready, 1)

        @block.vector
        def _(dve):
            for b in range(B):
                xb = R["X"][:, b * NT:(b + 1) * NT, :]
                dve.wait_ge(wo_done, b + 1)
                nc.vector.tensor_tensor(xb, xb, pO[b % 2][:].rearrange("p (t c) -> p t c", c=D),
                                        ALU.add).then_inc(added, 1)
                dve.wait_ge(added, b + 1)
                nc.vector.tensor_tensor(xb, xb, bcast(R["bo1"][:], 1, NT), ALU.add).then_inc(summed, 1)


def build(nc, d):
    with ExitStack() as ctx:
        R = {}
        load_constants(nc, ctx, d, R)
        with ExitStack() as layer0:
            R["XNT"] = layer0.enter_context(nc.sbuf_tensor("XNT", [P, B * N], F32))
            prepare(nc, d, R, 0)
            guard(nc, R, 0)
            experts(nc, d, R)
        attention0(nc, d, R)
        R["V1"] = ctx.enter_context(nc.sbuf_tensor("V1", [P, B * NT, D], F32))
        prepare(nc, d, R, 1)
        guard(nc, R, 1)
        attention1(nc, d, R)
        finish(nc, d, R)


def kernel(L0_attn_x, L0_attn_wq, L0_attn_bq, L0_attn_wk, L0_attn_bk, L0_attn_wv, L0_attn_bv,
           L0_attn_wo, L0_attn_bo, L0_ffn_router_w, L0_ffn_routing_bias, L0_ffn_sw1, L0_ffn_sw2,
           L0_ffn_sw3, L0_ffn_ew1, L0_ffn_ew2, L0_ffn_ew3, L1_attn_w_in, L1_attn_b_in,
           L1_attn_w_out, L1_attn_b_out, L1_ffn_theta, L1_ffn_phi, L1_ffn_theta_noise,
           L1_ffn_phi_noise):
    import concourse.bacc as bacc
    from concourse.bass_utils import run_bass_kernel_spmd

    w_in = np.asarray(L1_attn_w_in).reshape(H, 3, HD, D)
    b_in = np.asarray(L1_attn_b_in).reshape(H, 3, HD)
    w1 = np.concatenate([np.asarray(L0_ffn_sw1)[None], np.asarray(L0_ffn_ew1)])
    w3 = np.concatenate([np.asarray(L0_ffn_sw3)[None], np.asarray(L0_ffn_ew3)])
    w2 = np.concatenate([np.asarray(L0_ffn_sw2)[None], np.asarray(L0_ffn_ew2)])
    w13 = np.stack([w1, w3], axis=1).transpose(0, 3, 1, 2)
    w2c = np.zeros((NE, 3 * P, D), np.float32)
    w2c[:, :I] = w2.transpose(0, 2, 1)
    w2c = w2c.reshape(NE, 3, P, D).transpose(0, 2, 1, 3)
    blk = np.zeros((P, 64), np.float32)
    for r in range(P):
        blk[r, r // HD] = 0.25
        blk[r, 32 + r // HD] = 1.0
    arrays = {
        "x": np.asarray(L0_attn_x).reshape(B * N, D),
        "wq0": np.asarray(L0_attn_wq).T, "wk0": np.asarray(L0_attn_wk).T,
        "wv0": np.asarray(L0_attn_wv).T, "wo0": np.asarray(L0_attn_wo).T,
        "bq0": np.asarray(L0_attn_bq)[:, None], "bk0": np.asarray(L0_attn_bk)[:, None],
        "bv0": np.asarray(L0_attn_bv)[None], "bo0": np.asarray(L0_attn_bo)[None],
        "rw": np.asarray(L0_ffn_router_w).T, "rb": np.asarray(L0_ffn_routing_bias)[None],
        "w13": w13, "w2": w2c,
        "wq1": w_in[:, 0].reshape(D, D).T, "wk1": w_in[:, 1].reshape(D, D).T,
        "wv1": w_in[:, 2].reshape(D, D).T, "wo1": np.asarray(L1_attn_w_out).T,
        "bq1": b_in[:, 0].reshape(D, 1), "bk1": b_in[:, 1].reshape(D, 1),
        "bv1": b_in[:, 2].reshape(1, D), "bo1": np.asarray(L1_attn_b_out)[None],
        "theta": np.asarray(L1_ffn_theta), "phi": np.asarray(L1_ffn_phi),
        "theta_noise": np.asarray(L1_ffn_theta_noise), "phi_noise": np.asarray(L1_ffn_phi_noise),
        "ident": np.eye(P, dtype=np.float32), "blk": blk,
        "desc": np.repeat(np.arange(E, 0, -1, dtype=np.float32)[None], P, axis=0),
    }
    arrays = {n: np.ascontiguousarray(a) for n, a in arrays.items()}
    nc = bacc.Bacc("TRN2", target_bir_lowering=False, num_devices=1)
    d = {n: nc.dram_tensor(f"in_{n}", a.shape, F32, kind="ExternalInput").ap() for n, a in arrays.items()}
    for layer in "01":
        d["stack" + layer] = nc.dram_tensor("stack" + layer, (HEADS, 2, ROWS, N), BF16, kind="Internal").ap()
    d["v0"] = nc.dram_tensor("v0", (HEADS, P, NT * VW), F32, kind="Internal").ap()
    d["att0"] = nc.dram_tensor("att0", (GROUPS, N, GROUP * HD), F32, kind="Internal").ap()
    d["out"] = nc.dram_tensor("out", (B * N, D), F32, kind="ExternalOutput").ap()
    build(nc, d)
    r = run_bass_kernel_spmd(nc, [{f"in_{n}": a for n, a in arrays.items()}], core_ids=[0])
    return r.results[0]["out"].reshape(B, N, D)
```

```python
from contextlib import ExitStack, contextmanager

import concourse.bass as bass
import numpy as np
from concourse import mybir

F32 = mybir.dt.float32
BF16 = mybir.dt.bfloat16
I32 = mybir.dt.int32
U32 = mybir.dt.uint32
ALU = mybir.AluOpType
ACT = mybir.ActivationFunctionType
AX = mybir.AxisListType.X

P = 128
B, N, D = 4, 1024, 128
H = 16
HD = D // H
NT = N // P
HEADS = B * H
GROUP = 4
GROUPS = HEADS // GROUP
E, I = 7, 352
NE = E + 1
ICH = [(0, 128), (128, 128), (256, 96)]
EPS = 1e-5
VW = HD + 1

PAIRS = [(0, 0), (0, 1), (1, 0), (1, 1), (0, 2), (2, 0)]
SUM_ROW = len(PAIRS) * HD
ROWS = SUM_ROW + 6
KROWS = 72
SCALE1 = float(1.0 / np.sqrt(HD))
BOUND = [900.0, 80.0]

JOBS = 5
TILES = GROUPS * JOBS
SHARED = B * NT
PLACES = TILES - SHARED
assert PLACES >= SHARED + E - 1
IP = 3 * P

TWO_PI = [6.28125, 0.0019350051879882812, 3.0199159819e-07]
MAGIC = 12582912.0


@contextmanager
def phase_semaphores(nc):
    sems = []

    def take(name):
        sems.append(nc.alloc_semaphore(name=name))
        return sems[-1]

    yield take
    nc.clear_and_free_semaphores(sems)
    nc.all_engine_barrier()


class Chain:

    def __init__(self, eng, sem):
        self.eng, self.sem, self.base, self.count = eng, sem, 0, 0

    def per_iteration(self, index, steps):
        self.base, self.count = index * steps, 0

    def step(self, instruction):
        instruction.then_inc(self.sem, 1)
        self.count += 1

    def wait(self, passed=None):
        self.eng.wait_ge(self.sem, self.base + self.count)
        if passed is not None:
            self.eng.sem_inc(passed, 1)


def wait_alone(eng, sem, value, passed):
    eng.wait_ge(sem, value)
    eng.sem_inc(passed, 1)


def bcast(ap, axis, n):
    return ap.unsqueeze(axis).to_broadcast([*ap.shape[:axis], n, *ap.shape[axis:]])


def load_constants(nc, ctx, early, d, R):
    sb = lambda n, s, t=F32: ctx.enter_context(nc.sbuf_tensor(n, s, t))
    sb_early = lambda n, s, t=F32: early.enter_context(nc.sbuf_tensor(n, s, t))
    R["WT"] = sb("WT", [P, B * NT, 2])
    R["pos"] = sb("pos", [P, B * NT], U32)
    R["expert"] = sb("expert", [1, TILES], I32)
    R["ident"] = sb("ident", [P, P])
    R["blk"] = sb("blk", [P, 64])
    R["flag"] = sb("flag", [1, 2], I32)
    R["gmax"] = sb("gmax", [64, 2 * B])
    R["cs"] = sb("cs", [P, 2 * D])
    names = ["wo0", "wq1", "wk1", "wv1", "wo1", "wq0", "wk0", "wv0"]
    cols = ["bq1", "bk1", "bq0", "bk0"]
    rows = ["bo0", "bv1", "bo1", "bv0"]
    is_early = lambda n: n[-1] == "0" and n[1] != "o"
    for want, alloc in ((False, sb), (True, sb_early)):
        for group, width in ((names, D), (cols, 1), (rows, D)):
            for n in group:
                if is_early(n) == want:
                    R[n] = alloc(n + "_sb", [P, width])
    R["rw"], R["rb"] = sb_early("rw_sb", [P, E]), sb_early("rb_sb", [P, E])
    R["desc"], R["bq0s"] = sb_early("desc", [P, E]), sb_early("bq0s", [P, 1])

    with phase_semaphores(nc) as take, ExitStack() as own:
        tmp = lambda n, s, t=F32: own.enter_context(nc.sbuf_tensor(n, s, t))
        R["ones"] = tmp("ones", [HEADS, 3 * N], BF16)
        zeros = tmp("zeros", [P, NT * D])
        ang = tmp("ang", [P, 2, D])
        noise = tmp("noise", [P, 2, D])
        turns = tmp("turns", [P, 2, D])
        sem = lambda n: take(n)
        loaded, angles_in, made, reduced, ones_out, trig_done = (
            sem(n) for n in ("const_loaded", "angles_in", "const_made", "angles_reduced",
                             "ones_out", "trig_done"))
        block = own.enter_context(nc.Block())
        n_loads = 3 + len(names) + 2 + len(cols) + len(rows)

        @block.sync
        def _(sp):
            for n in ("ident", "blk", "desc"):
                sp.dma_start(R[n][:], d[n]).then_inc(loaded, 16)
            for n in names + ["rw"]:
                sp.dma_start(R[n][:], d[n]).then_inc(loaded, 16)
            for n in rows + ["rb"]:
                sp.dma_start(R[n][:], d[n].to_broadcast([P, R[n].shape[1]])).then_inc(loaded, 16)
            for n in cols:
                sp.dma_start(R[n][:], d[n]).then_inc(loaded, 16)
            sp.wait_ge(made, 2)
            for side, row in ((0, SUM_ROW), (1, SUM_ROW + 3)):
                sp.dma_start(d["stack0"][:, 1 - side, row:row + 3, :],
                             R["ones"][:].rearrange("n (r t) -> n r t", r=3)
                             ).then_inc(ones_out, 16)
            for n in range(0, PLACES, NT):
                sp.dma_start(d["xg"][(SHARED + n) * P:(SHARED + n + NT) * P, :]
                             .rearrange("(t p) c -> p t c", p=P),
                             zeros[:].rearrange("p (t c) -> p t c", c=D)).then_inc(ones_out, 16)
            sp.wait_ge(loaded, 16 * n_loads)
            sp.wait_ge(ones_out, 32 + 16 * (PLACES // NT))

        @block.scalar
        def _(act):
            for i, (a, b) in enumerate((("theta", "theta_noise"), ("phi", "phi_noise"))):
                act.dma_start(ang[:, i, :], d[a]).then_inc(angles_in, 16)
                act.dma_start(noise[:, i, :], d[b]).then_inc(angles_in, 16)
            act.wait_ge(reduced, 1)
            nc.scalar.activation(R["cs"][:].rearrange("p (a c) -> p a c", a=2), ang[:, :, :],
                                 ACT.Sin).then_inc(trig_done, 1)

        @block.vector
        def _(dve):
            nc.vector.memset(R["ones"][:], 1.0).then_inc(made, 1)
            nc.vector.memset(zeros[:], 0.0).then_inc(made, 1)
            chain = Chain(dve, made)
            chain.count = 2
            chain.step(nc.vector.memset(R["gmax"][:], 0.0))
            dve.wait_ge(angles_in, 64)
            chain.step(nc.vector.tensor_tensor(ang[:, :, :], ang[:, :, :], noise[:, :, :], ALU.add))
            chain.wait()
            for i, quarter in ((0, 0.25), (1, 0.0)):
                chain.step(nc.vector.tensor_scalar(turns[:, i, :], ang[:, i, :],
                                                   float(1 / (2 * np.pi)), quarter, ALU.mult, ALU.add))
            chain.wait()
            chain.step(nc.vector.tensor_scalar(turns[:, :, :], turns[:, :, :], MAGIC, None, ALU.add))
            chain.wait()
            chain.step(nc.vector.tensor_scalar(turns[:, :, :], turns[:, :, :], MAGIC, None, ALU.subtract))
            chain.wait()
            for part in TWO_PI:
                chain.step(nc.vector.scalar_tensor_tensor(
                    out=ang[:, :, :], in0=turns[:, :, :], scalar=-part, in1=ang[:, :, :],
                    op0=ALU.mult, op1=ALU.add))
                chain.wait()
            chain.step(nc.vector.tensor_scalar(ang[:, 0, :], ang[:, 0, :], float(np.pi / 2), None, ALU.add))
            chain.wait()
            nc.vector.tensor_scalar(ang[:, :, :], ang[:, :, :], 3.1415925, -3.1415925,
                                    ALU.min, ALU.max).then_inc(reduced, 1)
            dve.wait_ge(loaded, 16 * n_loads)
            chain.step(nc.vector.tensor_scalar(R["bq0s"][:], R["bq0"][:], -2.0, None, ALU.mult))
            dve.wait_ge(trig_done, 1)


def each_batch(eng, batch):
    batch(0)
    with eng.Fori(1, B) as b:
        batch(b)


def prepare(nc, d, R, layer):
    first = layer == 0
    L = str(layer)
    with phase_semaphores(nc) as take, ExitStack() as ctx:
        sb = lambda n, s, t=F32: ctx.enter_context(nc.sbuf_tensor(n + L, s, t))
        ps = lambda n, s: ctx.enter_context(nc.psum_tensor(n + L, s, F32))
        sem = lambda n: take("p_" + n + L)
        X, WT = R["X"], R["WT"]
        stats, mv = sb("stats", [P, NT, 6]), sb("mv", [P, NT, 2])
        rstd = sb("rstd", [P, NT])
        xn = sb("xn", [P, NT, D])
        xt = sb("xt", [P, N])
        qf, kf = sb("qf", [P, N]), sb("kf", [P, N])
        qsq, ksq = sb("qsq", [P, N]), sb("ksq", [P, N])
        qp, kp = sb("qp", [P, 3, N], BF16), sb("kp", [P, 3, N], BF16)
        qr, kr = sb("qr", [P, N]), sb("kr", [P, N])
        sums, sumr, sump = sb("sums", [64, N]), sb("sumr", [64, N]), sb("sump", [64, 3, N], BF16)
        pX, pQ, pK, pV = ps("pX", [P, N]), ps("pQ", [P, N]), ps("pK", [P, N]), ps("pV", [P, N])
        if first:
            lg, pr = sb("lg", [P, NT, E]), sb("pr", [P, NT, E])
            vt = sb("vt", [P, H, NT, VW])
            top, inv = sb("top", [P, NT]), sb("inv", [P, NT])
        else:
            at, att = sb("at", [P, NT, D]), sb("att_t", [P, N])
            ysh, yro = sb("ysh", [P, NT, D]), sb("yro", [P, B * NT, D])
            ri, mag = sb("ri", [P, NT, 2, D]), sb("mag", [P, NT, D])

        s_dve, s_pool, passed = sem("dve_chain"), sem("pool_chain"), sem("passed")
        y_half, xn_stored = sem("y_half"), sem("xn_stored")
        x_in, y_used, yr_in, yr_ready = sem("x_in"), sem("y_used"), sem("yr_in"), sem("yr_ready")
        at_in, att_p, att_ready, wo_done, x_ready = (
            sem(n) for n in ("at_in", "att_p", "att_ready", "wo_done", "x_ready"))
        var_ready, std_ready, xn_ready, xt_p, xt_ready, xt_kept = (
            sem(n) for n in ("var_ready", "std_ready", "xn_ready", "xt_p", "xt_ready", "xt_kept"))
        q_p, k_p, v_p, qk_f, sq_ready, sum_p, sum_out, v_out = (
            sem(n) for n in ("q_p", "k_p", "v_p", "qk_f", "sq_ready", "sum_p", "sum_out", "v_out"))
        qp_ready, kp_ready, sump_ready, stored, v_stored = (
            sem(n) for n in ("qp_ready", "kp_ready", "sump_ready", "stored", "v_stored"))
        route_p, lg_ready, e_ready, route_out = (
            sem(n) for n in ("route_p", "lg_ready", "e_ready", "route_out"))
        mix_p, mix_out, pow_ready, mag_ready, mag_used = (
            sem(n) for n in ("mix_p", "mix_out", "pow_ready", "mag_ready", "mag_used"))
        block = ctx.enter_context(nc.Block())
        stack = d["stack" + L]
        n_stores = 2 * len(PAIRS) + (6 if first else 0)

        @block.sync
        def _(sp):
            def batch(b):
                sp.dma_start(X[:, bass.ds(b * NT, NT), :],
                             d["x"][bass.ds(b * N, N), :].rearrange("(t p) c -> p t c", p=P)).then_inc(x_in, 16)
                if not first:
                    sp.wait_ge(y_used, b)
                    sp.dma_start(ysh[:, :, :], d["yg"][bass.ds(b * N, N), :]
                                 .rearrange("(t p) c -> p t c", p=P)).then_inc(x_in, 16)
                    sp.wait_ge(att_p, NT * b)
                    for g in range(GROUP):
                        src = d["att0"][bass.ds(b * GROUP + g, 1), :, :]
                        sp.dma_start(at[:, :, g * 32:(g + 1) * 32],
                                     src.rearrange("o (t p) c -> p (o t) c", p=P)).then_inc(at_in, 16)
                else:
                    sp.wait_ge(xn_ready, NT * (b + 1))
                    sp.dma_start(d["xg"][bass.ds(b * N, N), :].rearrange("(t p) c -> p t c", p=P),
                                 xn[:, :, :]).then_inc(xn_stored, 16)
                dst = stack[bass.ds(b * H, H)]
                sp.wait_ge(qp_ready, b + 1)
                for r, (_, a) in enumerate(PAIRS):
                    sp.dma_start(dst[:, 0, r * HD:(r + 1) * HD, :], qp[:, a, :]).then_inc(stored, 16)
                sp.wait_ge(kp_ready, b + 1)
                for r, (a, _) in enumerate(PAIRS):
                    sp.dma_start(dst[:, 1, r * HD:(r + 1) * HD, :], kp[:, a, :]).then_inc(stored, 16)
                if first:
                    sp.wait_ge(sump_ready, b + 1)
                    for a in range(3):
                        sp.dma_start(dst[:, 0, SUM_ROW + a, :], sump[0:H, a, :]).then_inc(stored, 16)
                        sp.dma_start(dst[:, 1, SUM_ROW + 3 + a, :], sump[32:32 + H, a, :]).then_inc(stored, 16)
            each_batch(sp, batch)
            sp.wait_ge(stored, 16 * n_stores * B)
            if first:
                sp.wait_ge(v_stored, 16 * B)
                sp.wait_ge(xn_stored, 16 * B)

        @block.tensor
        def _(pe):
            def batch(b):
                if not first:
                    pe.wait_ge(at_in, 16 * GROUP * (b + 1))
                    pe.wait_ge(qk_f, 2 * b)
                    for t in range(NT):
                        nc.tensor.transpose(pQ[:, t * P:(t + 1) * P], at[:, t, :], R["ident"][:]).then_inc(att_p, 1)
                    pe.wait_ge(att_ready, b + 1)
                    for t in range(NT):
                        mm = nc.tensor.matmul(pK[:, t * P:(t + 1) * P], att[:, t * P:(t + 1) * P],
                                              R["wo0"][:], start=True, stop=True)
                    mm.then_inc(wo_done, 1)
                pe.wait_ge(sum_out, b)
                if not first:
                    pe.wait_ge(mix_out, 4 * b)
                for t in range(NT):
                    pe.wait_ge(xn_ready, NT * b + t + 1)
                    nc.tensor.transpose(pX[:, t * P:(t + 1) * P], xn[:, t, :], R["ident"][:]).then_inc(xt_p, 1)
                if first:
                    pe.wait_ge(route_out, b)
                    pe.wait_ge(qk_f, 2 * b)
                pe.wait_ge(xt_ready, 2 * (b + 1))
                for half in range(2):
                    cols = slice(half * 512, (half + 1) * 512)
                    mm = nc.tensor.matmul(pQ[:, cols], R["wq" + L][:], xt[:, cols], start=True, stop=True)
                mm.then_inc(q_p, 1)
                if not first:
                    pe.wait_ge(x_ready, b + 1)
                for half in range(2):
                    cols = slice(half * 512, (half + 1) * 512)
                    mm = nc.tensor.matmul(pK[:, cols], R["wk" + L][:], xt[:, cols], start=True, stop=True)
                mm.then_inc(k_p, 1)
                pe.wait_ge(v_out, b)
                for t in range(NT):
                    mm = nc.tensor.matmul(pV[:, t * P:(t + 1) * P], xt[:, t * P:(t + 1) * P],
                                          R["wv" + L][:], start=True, stop=True)
                mm.then_inc(v_p, 1)
                pe.wait_ge(sq_ready, b + 1)
                for half in range(2):
                    cols = slice(half * 512, (half + 1) * 512)
                    nc.tensor.matmul(pX[0:32, cols], R["blk"][:, 0:32], qsq[:, cols], start=True, stop=True)
                    mm = nc.tensor.matmul(pX[32:64, cols], R["blk"][:, 32:64], ksq[:, cols], start=True, stop=True)
                mm.then_inc(sum_p, 1)
                if first:
                    pe.wait_ge(qk_f, 2 * b + 2)
                    for t in range(NT):
                        mm = nc.tensor.matmul(pQ[:, t * 8:t * 8 + E], xt[:, t * P:(t + 1) * P],
                                              R["rw"][:], start=True, stop=True)
                    mm.then_inc(route_p, 1)
                else:
                    pe.wait_ge(sum_out, b + 1)
                    for r in range(4):
                        if r >= 2:
                            pe.wait_ge(mix_out, 4 * b + r - 1)
                        for j in range(2):
                            t, at_col = 2 * r + j, (r % 2) * 512 + j * 256
                            mm = nc.tensor.matmul(pX[:, at_col:at_col + 256], xt[:, t * P:(t + 1) * P],
                                                  R["cs"][:], start=True, stop=True)
                        mm.then_inc(mix_p, 1)
            each_batch(pe, batch)

        @block.scalar
        def _(act):
            def batch(b):
                if not first:
                    for half in range(2):
                        cols = slice(half * 512, (half + 1) * 512)
                        act.wait_ge(att_p, NT * b + 4 * (half + 1))
                        cp = nc.scalar.activation(att[:, cols], pQ[:, cols], ACT.Copy)
                    cp.then_inc(att_ready, 1)
                act.wait_ge(var_ready, b + 1)
                nc.scalar.activation(rstd[:], mv[:, :, 1], ACT.Sqrt).then_inc(std_ready, 1)
                if first:
                    act.wait_ge(route_p, b)
                else:
                    act.wait_ge(mix_p, 4 * b)
                for half in range(2):
                    cols = slice(half * 512, (half + 1) * 512)
                    act.wait_ge(xt_p, NT * b + 4 * (half + 1))
                    nc.scalar.activation(xt[:, cols], pX[:, cols], ACT.Copy).then_inc(xt_ready, 1)
                act.wait_ge(q_p, b + 1)
                act.wait_ge(qp_ready, b)
                if first:
                    nc.scalar.activation(qf[:], pQ[:], ACT.Identity, bias=R["bq0s"][:], scale=-2.0).then_inc(qk_f, 1)
                else:
                    nc.scalar.activation(qf[:], pQ[:], ACT.Identity, bias=R["bq1"][:]).then_inc(qk_f, 1)
                act.wait_ge(k_p, b + 1)
                act.wait_ge(kp_ready, b)
                nc.scalar.activation(kf[:], pK[:], ACT.Identity, bias=R["bk" + L][:]).then_inc(qk_f, 1)
                act.wait_ge(sum_p, b)
                act.wait_ge(qk_f, 2 * b + 2)
                nc.scalar.activation(qsq[:], qf[:], ACT.Square)
                nc.scalar.activation(ksq[:], kf[:], ACT.Square).then_inc(sq_ready, 1)
                if first:
                    act.wait_ge(lg_ready, b + 1)
                    nc.scalar.activation(pr[:, :, :], lg[:, :, :], ACT.Exp, scale=-1.0).then_inc(e_ready, 1)
                else:
                    for r in range(4):
                        act.wait_ge(mix_p, 4 * b + r + 1)
                        if r == 0:
                            act.wait_ge(pow_ready, b)
                        nc.scalar.activation(ri[:, 2 * r:2 * r + 2, :, :].rearrange("p t a c -> p (t a c)"),
                                             pX[:, (r % 2) * 512:(r % 2 + 1) * 512], ACT.Square
                                             ).then_inc(mix_out, 1)
                    act.wait_ge(pow_ready, b + 1)
                    nc.scalar.activation(mag[:, :, :], mag[:, :, :], ACT.Sqrt).then_inc(mag_ready, 1)
            each_batch(act, batch)

        @block.gpsimd
        def _(pool):
            steps = 3
            def batch(b):
                chain = Chain(pool, s_pool)
                chain.per_iteration(b, steps)
                if not first:
                    for t in range(b * NT, (b + 1) * NT):
                        pool.indirect_dma_start(
                            out=yro[:, t, :], out_offset=None, in_=d["yg"][:, :],
                            in_offset=bass.IndirectOffsetOnAxis(ap=R["pos"][:, t:t + 1], axis=0)
                        ).then_inc(yr_in, 16)
                    pool.wait_ge(yr_in, 16 * NT * (b + 1))
                    pool.sem_inc(yr_ready, 1)
                pool.wait_ge(stored, 16 * n_stores * b)
                wait_alone(pool, qk_f, 2 * b + 2, passed)
                chain.step(nc.gpsimd.tensor_copy(kp[:, 0, :], kf[:]))
                chain.wait()
                chain.step(nc.gpsimd.tensor_tensor(kr[:], kf[:], kp[:, 0, :], ALU.subtract))
                chain.wait(passed)
                chain.step(nc.gpsimd.tensor_copy(kp[:, 1, :], kr[:]))
                chain.wait()
                assert chain.count == steps
                nc.gpsimd.tensor_tensor(kp[:, 2, :], kr[:], kp[:, 1, :], ALU.subtract).then_inc(kp_ready, 1)
                if first:
                    pool.wait_ge(v_out, b + 1)
                    pool.dma_start(d["v0"][bass.ds(b * H, H)].rearrange("h p w -> p h w"),
                                   vt[:].rearrange("p h t w -> p h (t w)")).then_inc(v_stored, 16)
            if first:
                each_batch(pool, batch)
            else:
                for b in range(B):
                    batch(b)

        @block.vector
        def _(dve):
            chain = Chain(dve, s_dve)
            if first:
                chain.step(nc.vector.memset(vt[:].rearrange("p h t w -> p (h t) w")[:, :, HD], 1.0))
            before = chain.count
            steps = 23 if first else 8
            def batch(b):
                chain.base, chain.count = b * steps + before, 0
                xb = X[:, bass.ds(b * NT, NT), :]
                x_of = lambda t: X[:, bass.ds(b * NT + t, 1), :].rearrange("p o c -> p (o c)")
                if first:
                    wait_alone(dve, x_in, 16 * (b + 1), passed)
                else:
                    dve.wait_ge(x_in, 32 * (b + 1))
                    dve.wait_ge(yr_ready, b + 1)
                    for y, k in ((lambda t: ysh[:, t, :], 0),
                                 (lambda t: yro[:, bass.ds(b * NT + t, 1), :].rearrange("p o c -> p (o c)"), 1)):
                        for t in range(NT):
                            weight = WT[:, bass.ds(b * NT + t, 1), k:k + 1].rearrange("p o c -> p (o c)")
                            add = nc.vector.scalar_tensor_tensor(out=x_of(t), in0=y(t), scalar=weight, in1=x_of(t),
                                                                 op0=ALU.mult, op1=ALU.add)
                        add.then_inc(y_used if k == 1 else y_half, 1)
                        dve.wait_ge(y_used if k == 1 else y_half, b + 1)
                    dve.wait_ge(wo_done, b + 1)
                    chain.step(nc.vector.tensor_tensor(xb, xb, pK[:].rearrange("p (t c) -> p t c", c=D), ALU.add))
                    chain.wait()
                    nc.vector.tensor_tensor(xb, xb, bcast(R["bo0"][:], 1, NT), ALU.add).then_inc(x_ready, 1)
                    wait_alone(dve, x_ready, b + 1, passed)
                for t in range(NT):
                    st = nc.vector.bn_stats(stats[:, t, :], X[:, bass.ds(b * NT + t, 1), :].rearrange("p o c -> p (o c)"))
                chain.step(st)
                dve.wait_ge(xn_ready, NT * b)
                chain.wait(passed)
                for t in range(NT):
                    st = nc.vector.bn_aggr(mv[:, t, :], stats[:, t, :])
                chain.step(st)
                chain.wait()
                nc.vector.tensor_scalar(mv[:, :, 1], mv[:, :, 1], EPS, None, ALU.add).then_inc(var_ready, 1)
                dve.wait_ge(std_ready, b + 1)
                chain.step(nc.vector.reciprocal(rstd[:], rstd[:]))
                chain.wait()
                dve.wait_ge(xt_p, NT * b)
                if first:
                    dve.wait_ge(xn_stored, 16 * b)
                for t in range(NT):
                    nc.vector.tensor_scalar(xn[:, t, :], X[:, bass.ds(b * NT + t, 1), :].rearrange("p o c -> p (o c)"),
                                            mv[:, t, 0:1], rstd[:, t:t + 1],
                                            ALU.subtract, ALU.mult).then_inc(xn_ready, 1)
                dve.wait_ge(qk_f, 2 * b + 1)
                dve.wait_ge(stored, 16 * n_stores * b)
                chain.step(nc.vector.tensor_copy(qp[:, 0, :], qf[:]))
                chain.wait()
                chain.step(nc.vector.tensor_tensor(qr[:], qf[:], qp[:, 0, :], ALU.subtract))
                chain.wait()
                chain.step(nc.vector.tensor_copy(qp[:, 1, :], qr[:]))
                chain.wait()
                nc.vector.tensor_tensor(qp[:, 2, :], qr[:], qp[:, 1, :], ALU.subtract).then_inc(qp_ready, 1)
                dve.wait_ge(v_p, b + 1)
                if first:
                    dve.wait_ge(v_stored, 16 * b)
                    for t in range(NT):
                        va = nc.vector.tensor_tensor(vt[:, :, t, 0:HD],
                                                     pV[:, t * P:(t + 1) * P].rearrange("p (h e) -> p h e", e=HD),
                                                     R["bv0"][:].rearrange("p (h e) -> p h e", e=HD), ALU.add)
                    va.then_inc(v_out, 1)
                else:
                    nc.vector.tensor_tensor(R["V1"][:, bass.ds(b * NT, NT), :],
                                            pV[:].rearrange("p (t c) -> p t c", c=D),
                                            bcast(R["bv1"][:], 1, NT), ALU.add).then_inc(v_out, 1)
                dve.wait_ge(sum_p, b + 1)
                nc.vector.tensor_copy(sums[:], pX[0:64, :]).then_inc(sum_out, 1)
                dve.wait_ge(sum_out, b + 1)
                gm = R["gmax"][:, bass.ds(b + layer * B, 1)]
                chain.step(nc.vector.tensor_reduce(gm, sums[:], axis=AX, op=ALU.max))
                if first:
                    chain.step(nc.vector.tensor_copy(sump[:, 0, :], sums[:]))
                    chain.wait()
                    chain.step(nc.vector.tensor_tensor(sumr[:], sums[:], sump[:, 0, :], ALU.subtract))
                    chain.wait()
                    chain.step(nc.vector.tensor_copy(sump[:, 1, :], sumr[:]))
                    chain.wait()
                    nc.vector.tensor_tensor(sump[:, 2, :], sumr[:], sump[:, 1, :], ALU.subtract).then_inc(sump_ready, 1)
                    dve.wait_ge(route_p, b + 1)
                    nc.vector.tensor_tensor(lg[:, :, :], pQ[:, 0:64].rearrange("p (t e) -> p t e", e=8)[:, :, 0:E],
                                            bcast(R["rb"][:], 1, NT), ALU.add).then_inc(route_out, 1)
                    dve.wait_ge(route_out, b + 1)
                    nc.vector.tensor_scalar(lg[:, :, :], lg[:, :, :], -50.0, 50.0, ALU.max, ALU.min).then_inc(lg_ready, 1)
                    dve.wait_ge(e_ready, b + 1)
                    chain.step(nc.vector.tensor_scalar(pr[:, :, :], pr[:, :, :], 1.0, None, ALU.add))
                    chain.wait()
                    chain.step(nc.vector.reciprocal(pr[:, :, :], pr[:, :, :]))
                    chain.wait()
                    chain.step(nc.vector.tensor_reduce(top[:], pr[:, :, :], axis=AX, op=ALU.max))
                    chain.wait()
                    eq = R["OH"][:, bass.ds(b * NT, NT), :]
                    chain.step(nc.vector.tensor_tensor(eq, pr[:, :, :], bcast(top[:], 2, E), ALU.is_equal))
                    chain.wait()
                    chain.step(nc.vector.tensor_tensor(eq, eq, bcast(R["desc"][:], 1, NT), ALU.mult))
                    chain.wait(passed)
                    chain.step(nc.vector.tensor_reduce(inv[:], eq, axis=AX, op=ALU.max))
                    chain.wait()
                    chain.step(nc.vector.tensor_tensor(eq, eq, bcast(inv[:], 2, E), ALU.is_equal))
                    chain.step(nc.vector.tensor_scalar(top[:], top[:], 1e-8, 1.0 - 1e-8, ALU.max, ALU.min))
                    chain.wait()
                    chain.step(nc.vector.tensor_scalar(inv[:], top[:], 0.5, 1e-8, ALU.add, ALU.add))
                    chain.wait()
                    chain.step(nc.vector.tensor_scalar(inv[:], inv[:], 0.5, 2.0, ALU.max, ALU.min))
                    chain.wait()
                    chain.step(nc.vector.reciprocal(inv[:], inv[:]))
                    chain.wait()
                    wb = WT[:, bass.ds(b * NT, NT), :]
                    chain.step(nc.vector.tensor_scalar(wb[:, :, 0], inv[:], 0.25, None, ALU.mult))
                    chain.step(nc.vector.scalar_tensor_tensor(out=wb[:, :, 1], in0=top[:], scalar=0.5, in1=inv[:],
                                                              op0=ALU.mult, op1=ALU.mult))
                    chain.wait()
                else:
                    dve.wait_ge(mix_out, 4 * b + 4)
                    dve.wait_ge(mag_used, b)
                    nc.vector.tensor_tensor(mag[:, :, :], ri[:, :, 0, :], ri[:, :, 1, :], ALU.add).then_inc(pow_ready, 1)
                    dve.wait_ge(mag_ready, b + 1)
                    nc.vector.tensor_tensor(xb, xb, mag[:, :, :], ALU.add).then_inc(mag_used, 1)
                assert chain.count == steps, chain.count
            each_batch(dve, batch)


def guard(nc, R, layer):
    L = str(layer)
    with phase_semaphores(nc) as take, ExitStack() as ctx:
        top = ctx.enter_context(nc.sbuf_tensor("gtop" + L, [64, 1], F32))
        over = ctx.enter_context(nc.sbuf_tensor("gover" + L, [1, 1], F32))
        pt = ctx.enter_context(nc.psum_tensor("gpt" + L, [1, 64], F32))
        top_ready = take("gtop_ready" + L)
        turned = take("gturned" + L)
        chain_sem = take("gchain" + L)
        block = ctx.enter_context(nc.Block())

        @block.tensor
        def _(pe):
            pe.wait_ge(top_ready, 1)
            nc.tensor.transpose(pt[:], top[:], R["ident"][0:64, 0:64]).then_inc(turned, 1)

        @block.vector
        def _(dve):
            chain = Chain(dve, chain_sem)
            nc.vector.tensor_reduce(top[:], R["gmax"][:, layer * B:(layer + 1) * B], axis=AX,
                                    op=ALU.max).then_inc(top_ready, 1)
            dve.wait_ge(turned, 1)
            chain.step(nc.vector.tensor_reduce(over[:], pt[:], axis=AX, op=ALU.max))
            chain.wait()
            chain.step(nc.vector.tensor_scalar(over[:], over[:], BOUND[layer], None, ALU.is_gt))
            chain.wait()
            chain.step(nc.vector.tensor_copy(R["flag"][:, layer:layer + 1], over[:]))
            chain.wait()


def route(nc, d, R):
    TOK = B * NT
    with phase_semaphores(nc) as take, ExitStack() as ctx:
        sb = lambda n, s, t=F32: ctx.enter_context(nc.sbuf_tensor("r_" + n, s, t))
        tri, ones = sb("tri", [P, P]), sb("ones", [P, P])
        marks, slots = sb("marks", [P, TOK]), sb("slots", [1, PLACES])
        cnt, run = sb("cnt", [P, TOK, E]), [sb(f"run{i}", [P, TOK, E]) for i in range(2)]
        over, tiles = sb("over", [P, E, TOK]), sb("tiles", [P, E])
        end, base = sb("end", [P, E]), sb("base", [P, E])
        past, ex = sb("past", [1, PLACES, E]), sb("ex", [1, PLACES])
        posf, xn = sb("posf", [P, TOK]), sb("xn", [P, TOK, D])
        rank_p = ctx.enter_context(nc.psum_tensor("r_rank", [P, TOK * E], F32))
        count_p = ctx.enter_context(nc.psum_tensor("r_count", [P, TOK * E], F32))
        loaded, xn_in, counted, chain_sem, pos_ready, placed = (
            take("r_" + n) for n in ("loaded", "xn_in", "counted", "chain", "pos_ready", "placed"))
        block = ctx.enter_context(nc.Block())
        OH = R["OH"]

        @block.sync
        def _(sp):
            for tile, name in ((tri, "tri"), (ones, "all_ones"), (marks, "marks"), (slots, "slots")):
                sp.dma_start(tile[:], d[name]).then_inc(loaded, 16)
            sp.dma_start(xn[:, :, :], d["xg"][0:TOK * P, :].rearrange("(t p) c -> p t c", p=P)).then_inc(xn_in, 16)

        @block.tensor
        def _(pe):
            pe.wait_ge(loaded, 64)
            flat = OH[:, :, :].rearrange("p t e -> p (t e)")
            nc.tensor.matmul(rank_p[:], tri[:], flat, start=True, stop=True)
            nc.tensor.matmul(count_p[:], ones[:], flat, start=True, stop=True).then_inc(counted, 1)

        @block.vector
        def _(dve):
            chain = Chain(dve, chain_sem)
            shape = lambda ap: ap.rearrange("p (t e) -> p t e", e=E)
            dve.wait_ge(loaded, 64)
            chain.step(nc.vector.memset(R["expert"][:], 0))
            dve.wait_ge(counted, 1)
            chain.step(nc.vector.tensor_copy(cnt[:, :, :], shape(count_p[:])))
            chain.step(nc.vector.tensor_copy(run[0][:, :, :], shape(count_p[:])))
            chain.wait()
            step, now = 1, 0
            while step < TOK:
                src, dst = run[now], run[1 - now]
                chain.step(nc.vector.tensor_copy(dst[:, 0:step, :], src[:, 0:step, :]))
                chain.step(nc.vector.tensor_tensor(dst[:, step:, :], src[:, step:, :], src[:, 0:TOK - step, :], ALU.add))
                chain.wait()
                step, now = 2 * step, 1 - now
            total = run[now][:, TOK - 1, :]
            chain.step(nc.vector.tensor_tensor(over[:, :, :], bcast(total, 2, TOK), bcast(marks[:], 1, E), ALU.is_gt))
            chain.wait()
            chain.step(nc.vector.tensor_reduce(tiles[:], over[:, :, :], axis=AX, op=ALU.add))
            chain.wait()
            chain.step(nc.vector.tensor_copy(end[:, 0:1], tiles[:, 0:1]))
            chain.wait()
            for e in range(1, E):
                chain.step(nc.vector.tensor_tensor(end[:, e:e + 1], end[:, e - 1:e], tiles[:, e:e + 1], ALU.add))
                chain.wait()
            chain.step(nc.vector.tensor_tensor(base[:], end[:], tiles[:], ALU.subtract))
            chain.wait()
            chain.step(nc.vector.tensor_scalar(base[:], base[:], float(P), float(SHARED * P), ALU.mult, ALU.add))
            chain.step(nc.vector.tensor_tensor(cnt[:, :, :], run[now][:, :, :], cnt[:, :, :], ALU.subtract))
            chain.wait()
            chain.step(nc.vector.tensor_tensor(cnt[:, :, :], cnt[:, :, :], shape(rank_p[:]), ALU.add))
            chain.wait()
            chain.step(nc.vector.tensor_tensor(cnt[:, :, :], cnt[:, :, :], bcast(base[:], 1, TOK), ALU.add))
            chain.wait()
            chain.step(nc.vector.tensor_tensor(cnt[:, :, :], cnt[:, :, :], OH[:, :, :], ALU.mult))
            chain.wait()
            chain.step(nc.vector.tensor_reduce(posf[:], cnt[:, :, :], axis=AX, op=ALU.add))
            chain.wait()
            nc.vector.tensor_copy(R["pos"][:], posf[:]).then_inc(pos_ready, 1)
            chain.step(nc.vector.tensor_tensor(past[:, :, :], bcast(end[0:1, :], 1, PLACES),
                                               bcast(slots[:], 2, E), ALU.is_le))
            chain.wait()
            chain.step(nc.vector.tensor_reduce(ex[:], past[:, :, :], axis=AX, op=ALU.add))
            chain.wait()
            chain.step(nc.vector.tensor_scalar(ex[:], ex[:], 1.0, float(E), ALU.add, ALU.min))
            chain.wait()
            chain.step(nc.vector.tensor_copy(R["expert"][:, SHARED:TILES], ex[:]))
            chain.wait()

        @block.gpsimd
        def _(pool):
            pool.wait_ge(pos_ready, 1)
            pool.wait_ge(xn_in, 16)
            for t in range(TOK):
                pool.indirect_dma_start(
                    out=d["xg"][:, :], out_offset=bass.IndirectOffsetOnAxis(ap=R["pos"][:, t:t + 1], axis=0),
                    in_=xn[:, t, :], in_offset=None).then_inc(placed, 16)
            pool.wait_ge(placed, 16 * TOK)


CH = 8
RING = 3


def ring_uses(ahead, now):
    uses = []
    for place in range(GROUP):
        for j in range(CH):
            if ahead:
                uses.append(("qk", place, j))
                if (place, j) == (0, 3):
                    uses.append(("tokens", 0))
            if now and (place, j) in HIDDEN_AT:
                uses.append(("hidden", HIDDEN_AT.index((place, j))))
    return (uses + [("up", j) for j in range(JOBS) if ahead] + [("down", 0)] * now)


HIDDEN_AT = [(2, 2), (2, 6), (3, 2)]
ROUND = ring_uses(True, True)
CYCLE = len(ROUND)
assert CYCLE % RING == 0 and len(HIDDEN_AT) == (JOBS + 1) // 2
FIRST, LAST = ring_uses(True, False), ring_uses(False, True)
ALONE = [u for u in ROUND if u[0] != "qk"]
ALONE = [u for u in ALONE if u[0] in ("tokens", "up")] + [u for u in ALONE if u[0] in ("hidden", "down")]


def attention0(nc, d, R):
    layer, L = 0, "0"
    SLOTS = 2
    with phase_semaphores(nc) as take, ExitStack() as ctx:
        sb = lambda n, s, t=F32: ctx.enter_context(nc.sbuf_tensor(n + L, s, t))
        ps = lambda n, s: ctx.enter_context(nc.psum_tensor(n + L, s, F32))
        sem = lambda n: take("a0_" + n)
        S = [sb(f"scores{i}", [P, CH * N]) for i in range(GROUP)]
        stk = [sb(f"stk{i}", [KROWS, 2, N], BF16) for i in range(SLOTS)]
        w13, w2 = sb("w13", [P, NE, 2, I]), sb("w2", [P, NE, 3, D])
        xj, xjt = sb("xj", [P, JOBS, D]), sb("xjt", [P, JOBS * P])
        h1, gate = sb("h1", [P, JOBS, I]), sb("gate", [P, JOBS, IP])
        ht = sb("ht", [P, JOBS, IP])
        yj = ht[:, :, 0:D]
        val = [sb(f"val{i}", [P, CH, VW]) for i in range(GROUP)]
        ot = sb("ot", [P, 256])
        rden = sb("rden", [P, GROUP, NT])
        attg = sb("attg", [P, NT, 32])
        mcol = sb("mcol", [P, 1])
        ring = [ps(f"ring{i}", [P, N]) for i in range(RING)]
        pvb = [ps(f"pvb{i}", [P, 512]) for i in range(2)]
        stk_in = [sem(f"stk_in{i}") for i in range(SLOTS)]
        val_in = [sem(f"val_in{i}") for i in range(GROUP)]
        ring_full, ring_free, root_done, exp_done, pv_done = (
            sem(n) for n in ("ring_full", "ring_free", "root_done", "exp_done", "pv_done"))
        zeroed = sem("zeroed")
        w_in, xj_in, h1_done, tanh_done, part_done, hid_done, y_stored, y_free = (
            sem("j_" + n) for n in ("w_in", "xj_in", "h1_done", "tanh_done", "part_done", "hid_done",
                                    "y_stored", "y_free"))
        attg_free, g_slot = sem("attg_free"), sem("g_slot")
        cleared, ot_ready, turned, rden_ready, att_ready, att_out = (
            sem(n) for n in ("cleared", "ot_ready", "turned", "rden_ready", "att_ready", "att_out"))
        g_in, g_s, g_copied, g_root, g_max, g_exp, g_turn, g_pt, g_pv, g_rd, g_att, g_out = (
            sem("g_" + n) for n in ("in", "s", "copied", "root", "max", "exp", "turn", "pt",
                                    "pv", "rd", "att", "out"))
        block = ctx.enter_context(nc.Block())
        Q, K = 0, 1
        CHG = GROUP * CH

        def count(uses, base, use):
            return base + uses.index(use) + 1

        def take(pe, uses, base, use, ago=RING):
            if not isinstance(base, int) or base + uses.index(use) >= ago:
                pe.wait_ge(ring_free, count(uses, base, use) - ago)
            return ring[uses.index(use) % RING]

        def filled(dve, uses, base, use):
            dve.wait_ge(ring_full, count(uses, base, use))
            return ring[uses.index(use) % RING]

        def qk(pe, uses, base, group, place, j):
            slot = place % SLOTS
            if j == 0:
                pe.wait_ge(stk_in[slot], 16 * (GROUP // SLOTS * group + place // SLOTS + 1))
            tile = take(pe, uses, base, ("qk", place, j))
            for half in range(2):
                cols = slice(half * 512, (half + 1) * 512)
                mm = nc.tensor.matmul(tile[:, cols], stk[slot][:, K, j * P:(j + 1) * P],
                                      stk[slot][:, Q, cols], start=True, stop=True)
            mm.then_inc(ring_full, 1)

        def pv(pe, group, place, j):
            if j == 0:
                pe.wait_ge(val_in[place], 16 * (group + 1))
                if place >= 2:
                    pe.wait_ge(att_ready, GROUP * group + place - 1)
                pe.wait_ge(exp_done, GROUP * group + place + 1)
            for c in range(4):
                mm = nc.tensor.matmul(pvb[place % 2][32 * c:32 * c + VW, 0:256], val[place][:, j, :],
                                      S[place][:, j * N + c * 256:j * N + (c + 1) * 256],
                                      start=(j == 0), stop=(j == CH - 1))
            mm.then_inc(pv_done, 1)

        def turn(pe, group, place):
            pe.wait_ge(ot_ready, GROUP * group + place + 1)
            for t in range(2):
                mm = nc.tensor.transpose(pvb[place % 2][:, 256 + t * P:256 + (t + 1) * P],
                                         ot[:, t * P:(t + 1) * P], R["ident"][:])
            mm.then_inc(turned, 1)

        def load_jobs(sp, v):
            sp.dma_start(xj[:, :, :], d["xg"][bass.ds(v * (JOBS * P), JOBS * P), :]
                         .rearrange("(j p) c -> p j c", p=P)).then_inc(xj_in, 16)

        def experts_of(pe, v):
            return [pe.value_load(R["expert"][0:1, bass.ds(v * JOBS + j, 1)], min_val=0, max_val=E)
                    for j in range(JOBS)]

        def turn_tokens(pe, uses, base, v, **ago):
            pe.wait_ge(xj_in, 16 * (v + 1))
            tile = take(pe, uses, base, ("tokens", 0), **ago)
            for j in range(JOBS):
                mm = nc.tensor.transpose(tile[:, j * P:(j + 1) * P], xj[:, j, :], R["ident"][:])
            mm.then_inc(ring_full, 1)

        def up(pe, uses, base, v, **ago):
            e = experts_of(pe, v)
            pe.wait_ge(ring_free, count(uses, base, ("tokens", 0)))
            for j in range(JOBS):
                tile = take(pe, uses, base, ("up", j), **ago)
                for side in range(2):
                    mm = nc.tensor.matmul(tile[:, side * 512:side * 512 + I], xjt[:, j * P:(j + 1) * P],
                                          w13[:, bass.ds(e[j], 1), side, :].rearrange("p o i -> p (o i)"),
                                          start=True, stop=True)
                mm.then_inc(ring_full, 1)

        def keep_tokens(dve, uses, base):
            tile = filled(dve, uses, base, ("tokens", 0))
            nc.vector.tensor_copy(xjt[:], tile[:, 0:JOBS * P]).then_inc(ring_free, 1)

        def keep_up(dve, uses, base, v):
            for j in range(JOBS):
                tile = filled(dve, uses, base, ("up", j))
                nc.vector.tensor_copy(h1[:, j, :], tile[:, 0:I]).then_inc(h1_done, 1)
                dve.wait_ge(h1_done, JOBS * v + j + 1)
                nc.vector.tensor_tensor(gate[:, j, 0:I], h1[:, j, :], tile[:, 512:512 + I],
                                        ALU.mult).then_inc(ring_free, 1)

        def tanh(act, uses, base):
            act.wait_ge(ring_free, count(uses, base, ("up", JOBS - 1)))
            nc.scalar.activation(h1[:, :, :], h1[:, :, :], ACT.Tanh, scale=0.5).then_inc(tanh_done, 1)

        def hidden(pool, v):
            pool.wait_ge(tanh_done, v + 1)
            nc.gpsimd.tensor_tensor(h1[:, :, :], h1[:, :, :], gate[:, :, 0:I], ALU.mult).then_inc(part_done, 1)
            pool.wait_ge(part_done, v + 1)
            nc.gpsimd.tensor_tensor(gate[:, :, 0:I], gate[:, :, 0:I], h1[:, :, :], ALU.add).then_inc(hid_done, 1)

        def turn_hidden(pe, uses, base, v, i, **ago):
            pe.wait_ge(hid_done, v + 1)
            tile = take(pe, uses, base, ("hidden", i), **ago)
            for j in range(2 * i, min(2 * i + 2, JOBS)):
                for c in range(3):
                    at_col = (j % 2) * 512 + c * P
                    mm = nc.tensor.transpose(tile[:, at_col:at_col + P], gate[:, j, c * P:(c + 1) * P],
                                             R["ident"][:])
            mm.then_inc(ring_full, 1)

        def keep_hidden(dve, uses, base, v, i):
            tile = filled(dve, uses, base, ("hidden", i))
            if i == 0:
                dve.wait_ge(y_free, v + 1)
            n = min(2, JOBS - 2 * i)
            nc.vector.tensor_copy(ht[:, 2 * i:2 * i + n, :],
                                  tile[:].rearrange("p (j w) -> p j w", w=512)[:, 0:n, 0:IP]
                                  ).then_inc(ring_free, 1)

        def down(pe, uses, base, v, **ago):
            e = experts_of(pe, v)
            pe.wait_ge(ring_free, count(uses, base, ("hidden", JOBS // 2)))
            tile = take(pe, uses, base, ("down", 0), **ago)
            for j in range(JOBS):
                for c in range(3):
                    mm = nc.tensor.matmul(tile[:, j * P:(j + 1) * P], ht[:, j, c * P:(c + 1) * P],
                                          w2[:, bass.ds(e[j], 1), c, :].rearrange("p o n -> p (o n)"),
                                          start=(c == 0), stop=(c == 2))
            mm.then_inc(ring_full, 1)

        def keep_down(dve, uses, base):
            tile = filled(dve, uses, base, ("down", 0))
            nc.vector.tensor_copy(yj, tile[:, 0:JOBS * P].rearrange("p (j c) -> p j c", c=D)
                                  ).then_inc(ring_free, 1)

        def store_jobs(pool, uses, base, v):
            pool.wait_ge(ring_free, count(uses, base, ("down", 0)))
            pool.dma_start(d["yg"][bass.ds(v * (JOBS * P), JOBS * P), :].rearrange("(j p) c -> p j c", p=P),
                           yj).then_inc(y_stored, 16)
            pool.wait_ge(y_stored, 16 * (v + 1))
            pool.sem_inc(y_free, 1)

        def pe_round(pe, base, ahead, now):
            uses = ring_uses(ahead is not None, now is not None)
            for place in range(GROUP):
                for j in range(CH):
                    if now is not None:
                        pv(pe, now, place, j)
                        if j == 3 and place:
                            turn(pe, now, place - 1)
                    if ahead is not None:
                        qk(pe, uses, base, ahead, place, j)
                        if (place, j) == (0, 3):
                            turn_tokens(pe, uses, base, ahead)
                    if now is not None and (place, j) in HIDDEN_AT:
                        turn_hidden(pe, uses, base, now, HIDDEN_AT.index((place, j)))
            if now is not None:
                turn(pe, now, GROUP - 1)
            if ahead is not None:
                up(pe, uses, base, ahead)
            if now is not None:
                down(pe, uses, base, now)
                if ahead is not None:
                    pe.wait_ge(att_ready, GROUP * now + GROUP)

        def take_out(dve, group, place):
            dve.wait_ge(pv_done, CHG * group + (place + 1) * CH)
            nc.vector.tensor_copy(ot[:], pvb[place % 2][:, 0:256]).then_inc(ot_ready, 1)

        def divide(dve, group, place):
            dve.wait_ge(turned, GROUP * group + place + 1)
            if place == 0:
                dve.wait_ge(attg_free, group + 1)
            t = pvb[place % 2][:, 256:512].rearrange("p (k w) -> p k w", w=32)
            nc.vector.reciprocal(rden[:, place, :], t[:, :, HD]).then_inc(rden_ready, 1)
            dve.wait_ge(rden_ready, GROUP * group + place + 1)
            nc.vector.tensor_tensor(attg[:, :, place * HD:(place + 1) * HD], t[:, :, 0:HD],
                                    bcast(rden[:, place, :], 2, HD), ALU.mult).then_inc(att_ready, 1)

        def keep_distances(dve, uses, base, now, place, j):
            tile = filled(dve, uses, base, ("qk", place, j))
            if now is not None:
                dve.wait_ge(pv_done, CHG * now + place * CH + j + 1)
            nc.vector.tensor_scalar(S[place][:, j * N:(j + 1) * N], tile[:], 1e-12, None,
                                    ALU.max).then_inc(ring_free, 1)

        def dve_round(dve, base, ahead, now):
            uses = ring_uses(ahead is not None, now is not None)
            for place in range(GROUP):
                for j in range(CH):
                    if ahead is not None:
                        keep_distances(dve, uses, base, now, place, j)
                        if (place, j) == (0, 3):
                            keep_tokens(dve, uses, base)
                    if now is not None:
                        if (place, j) in HIDDEN_AT:
                            keep_hidden(dve, uses, base, now, HIDDEN_AT.index((place, j)))
                        if j == 5 and place:
                            divide(dve, now, place - 1)
                if now is not None:
                    take_out(dve, now, place)
            if now is not None:
                divide(dve, now, GROUP - 1)
            if ahead is not None:
                keep_up(dve, uses, base, ahead)
            if now is not None:
                keep_down(dve, uses, base)

        def store_out(pool, group):
            pool.wait_ge(att_ready, GROUP * group + GROUP)
            for t in range(2):
                dst = d["att" + L][bass.ds(group, 1), :, :].rearrange(
                    "o (c t p) w -> t p (o c) w", c=4, t=2)[t]
                pool.dma_start(dst, attg[:, 4 * t:4 * t + 4, :]).then_inc(att_out, 16)
            pool.wait_ge(att_out, 32 * (group + 1))
            pool.sem_inc(attg_free, 1)

        def general(eng, which):
            if which == "dve":
                eng.sem_inc(g_att, 1)
            if which == "pool":
                eng.sem_inc(g_slot, 1)
            with eng.Fori(0, GROUPS) as u:
                with eng.Fori(0, GROUP) as h:
                    n = u * GROUP + h
                    if which == "sp":
                        eng.wait_ge(g_att, NT * n + 1)
                        eng.dma_start(stk[0][0:ROWS], d["stack" + L][bass.ds(n, 1), :, 0:ROWS, :]
                                      .rearrange("o s r t -> (o r) s t")).then_inc(g_in, 16)
                        eng.dma_start(val[0][:], d["v" + L][bass.ds(n, 1)]
                                      .rearrange("o p (j w) -> (o p) j w", w=VW)).then_inc(g_in, 16)
                    if which == "pool":
                        eng.wait_ge(g_att, NT * (n + 1) + 1)
                        eng.dma_start(d["att" + L][bass.ds(u, 1), :, bass.ds(h * HD, HD)]
                                      .rearrange("o (t p) w -> p (o t) w", p=P),
                                      attg[:, :, 0:HD]).then_inc(g_out, 16)
                        eng.wait_ge(g_out, 16 * (n + 1))
                        eng.sem_inc(g_slot, 1)
                    for i in range(NT) if which in ("pe", "act", "dve") else ():
                        k = n * NT + i
                        if which == "pe":
                            if i == 0:
                                eng.wait_ge(g_in, 32 * (n + 1))
                            eng.wait_ge(g_att, k + 1)
                            for half in range(2):
                                cols = slice(half * 512, (half + 1) * 512)
                                mm = nc.tensor.matmul(ring[0][:, cols], stk[0][:, Q, i * P:(i + 1) * P],
                                                      stk[0][:, K, cols], start=True, stop=True)
                            mm.then_inc(g_s, 1)
                            eng.wait_ge(g_exp, k + 1)
                            for j in range(CH):
                                mm = nc.tensor.transpose(ring[1][:, j * P:(j + 1) * P],
                                                         S[0][:, j * P:(j + 1) * P], R["ident"][:])
                            mm.then_inc(g_turn, 1)
                            eng.wait_ge(g_pt, k + 1)
                            for j in range(CH):
                                mm = nc.tensor.matmul(pvb[0][:, 0:VW], S[1][:, j * P:(j + 1) * P],
                                                      val[0][:, j, :], start=(j == 0), stop=(j == CH - 1))
                            mm.then_inc(g_pv, 1)
                        if which == "dve":
                            eng.wait_ge(g_s, k + 1)
                            nc.vector.tensor_scalar(S[0][:, 0:N], ring[0][:], 1e-12, None,
                                                    ALU.max).then_inc(g_copied, 1)
                            eng.wait_ge(g_root, k + 1)
                            nc.vector.tensor_reduce(mcol[:], S[0][:, 0:N], axis=AX, op=ALU.min).then_inc(g_max, 1)
                            eng.wait_ge(g_turn, k + 1)
                            nc.vector.tensor_copy(S[1][:, 0:N], ring[1][:]).then_inc(g_pt, 1)
                            eng.wait_ge(g_pv, k + 1)
                            nc.vector.reciprocal(rden[:, 0, 0:1], pvb[0][:, HD:VW]).then_inc(g_rd, 1)
                            eng.wait_ge(g_rd, k + 1)
                            if i == 0:
                                eng.wait_ge(g_slot, n + 1)
                            nc.vector.tensor_scalar(attg[:, i, 0:HD], pvb[0][:, 0:HD], rden[:, 0, 0:1], None,
                                                    ALU.mult).then_inc(g_att, 1)
                        if which == "act":
                            eng.wait_ge(g_copied, k + 1)
                            nc.scalar.activation(S[0][:, 0:N], S[0][:, 0:N], ACT.Sqrt).then_inc(g_root, 1)
                            eng.wait_ge(g_max, k + 1)
                            nc.scalar.activation(S[0][:, 0:N], S[0][:, 0:N], ACT.Exp, bias=mcol[:],
                                                 scale=-1.0).then_inc(g_exp, 1)

        def jobs_alone(eng, which):
            uses, n = ALONE, len(ALONE)
            if which == "sp":
                load_jobs(eng, 0)
                with eng.Fori(1, GROUPS) as v:
                    eng.wait_ge(ring_free, count(uses, n * (v - 1), ("tokens", 0)))
                    load_jobs(eng, v)
            if which == "pool":
                eng.sem_inc(y_free, 1)
                with eng.Fori(0, GROUPS) as v:
                    hidden(eng, v)
                    store_jobs(eng, uses, n * v, v)
            if which == "pe":
                eng.wait_ge(w_in, 32)
                eng.wait_ge(g_att, NT * HEADS + 1)
                def tiles(v):
                    turn_tokens(eng, uses, n * v, v, ago=1)
                    up(eng, uses, n * v, v, ago=1)
                    for i in range(len(HIDDEN_AT)):
                        turn_hidden(eng, uses, n * v, v, i, ago=1)
                    down(eng, uses, n * v, v, ago=1)
                tiles(0)
                with eng.Fori(1, GROUPS) as v:
                    tiles(v)
            if which == "act":
                with eng.Fori(0, GROUPS) as v:
                    tanh(eng, uses, n * v)
            if which == "dve":
                with eng.Fori(0, GROUPS) as v:
                    keep_tokens(eng, uses, n * v)
                    keep_up(eng, uses, n * v, v)
                    for i in range(len(HIDDEN_AT)):
                        keep_hidden(eng, uses, n * v, v, i)
                    keep_down(eng, uses, n * v)

        def by_guard(eng, which, fast):
            flag = eng.value_load(R["flag"][0:1, layer:layer + 1], min_val=0, max_val=1)
            with eng.If(flag != 0):
                general(eng, which)
                jobs_alone(eng, which)
            with eng.Else():
                fast(eng)

        @block.sync
        def _(sp):
            sp.dma_start(w13[:, :, :, :], d["w13"].rearrange("e c a i -> c e a i")).then_inc(w_in, 16)
            sp.dma_start(w2[:, :, :, :], d["w2"].rearrange("e p k c -> p e k c")).then_inc(w_in, 16)
            sp.wait_ge(zeroed, SLOTS + 1)

            def load(group, place):
                sp.dma_start(stk[place % SLOTS][0:ROWS],
                             d["stack0"][bass.ds(group * GROUP + place, 1), :, 0:ROWS, :]
                             .rearrange("o s r t -> (o r) s t")).then_inc(stk_in[place % SLOTS], 16)

            def fast(sp):
                load(0, 0)
                load(0, 1)
                load_jobs(sp, 0)
                for place in range(SLOTS, GROUP):
                    sp.wait_ge(ring_full, count(ROUND, 0, ("qk", place - SLOTS, CH - 1)))
                    load(0, place)
                with sp.Fori(1, GROUPS) as u:
                    for place in range(GROUP):
                        before = u - 1 if place < SLOTS else u
                        sp.wait_ge(ring_full, count(ROUND, CYCLE * before,
                                                    ("qk", (place - SLOTS) % GROUP, CH - 1)))
                        load(u, place)
                        if place == 1:
                            sp.wait_ge(ring_free, count(ROUND, CYCLE * (u - 1), ("tokens", 0)))
                            load_jobs(sp, u)
            by_guard(sp, "sp", fast)

        @block.gpsimd
        def _(pool):
            def load(group, place):
                pool.dma_start(val[place][:], d["v" + L][bass.ds(group * GROUP + place, 1)]
                               .rearrange("o p (j w) -> (o p) j w", w=VW)).then_inc(val_in[place], 16)

            def fast(pool):
                pool.sem_inc(attg_free, 1)
                pool.sem_inc(y_free, 1)
                for place in range(GROUP):
                    load(0, place)
                with pool.Fori(0, GROUPS - 1) as u:
                    for place in range(GROUP):
                        pool.wait_ge(pv_done, CHG * u + (place + 1) * CH)
                        load(u + 1, place)
                        if place == 0:
                            hidden(pool, u)
                    store_out(pool, u)
                    store_jobs(pool, ROUND, CYCLE * (u + 1), u)
                hidden(pool, GROUPS - 1)
                store_out(pool, GROUPS - 1)
                store_jobs(pool, LAST, CYCLE * GROUPS, GROUPS - 1)
            by_guard(pool, "pool", fast)

        @block.tensor
        def _(pe):
            def fast(pe):
                pe.wait_ge(cleared, 2)
                pe.wait_ge(w_in, 32)
                pe_round(pe, 0, 0, None)
                pe.wait_ge(ring_free, CYCLE)
                pe.sem_inc(ring_full, CYCLE - len(FIRST))
                with pe.Fori(0, GROUPS - 1) as u:
                    pe_round(pe, CYCLE * (u + 1), u + 1, u)
                pe_round(pe, CYCLE * GROUPS, None, GROUPS - 1)
            by_guard(pe, "pe", fast)

        @block.vector
        def _(dve):
            nc.vector.memset(gate[:, :, I:IP], 0.0).then_inc(zeroed, 1)
            for i in range(SLOTS):
                nc.vector.memset(stk[i][:].rearrange("r s t -> r (s t)").bitcast(F32), 0.0).then_inc(zeroed, 1)
            def fast(dve):
                for i in range(2):
                    nc.vector.memset(pvb[i][:], 0.0).then_inc(cleared, 1)
                dve_round(dve, 0, 0, None)
                dve.wait_ge(ring_free, len(FIRST))
                dve.sem_inc(ring_free, CYCLE - len(FIRST))
                with dve.Fori(0, GROUPS - 1) as u:
                    dve_round(dve, CYCLE * (u + 1), u + 1, u)
                dve_round(dve, CYCLE * GROUPS, None, GROUPS - 1)
            by_guard(dve, "dve", fast)

        @block.scalar
        def _(act):
            def fast(act):
                with act.Fori(0, GROUPS) as u:
                    for place in range(GROUP):
                        act.wait_ge(ring_free, count(ROUND, CYCLE * u, ("qk", place, CH - 1)))
                        nc.scalar.activation(S[place][:], S[place][:], ACT.Sqrt).then_inc(root_done, 1)
                    for place in range(GROUP):
                        if place == 2:
                            tanh(act, ROUND, CYCLE * u)
                        act.wait_ge(root_done, GROUP * u + place + 1)
                        nc.scalar.activation(S[place][:], S[place][:], ACT.Exp, scale=-1.0).then_inc(exp_done, 1)
            by_guard(act, "act", fast)


def attention1(nc, d, R):
    RING1, PAIR = 4, 2 * GROUP
    with phase_semaphores(nc) as take, ExitStack() as ctx:
        sb = lambda n, s, t=F32: ctx.enter_context(nc.sbuf_tensor("a1_" + n, s, t))
        sem = lambda n: take("a1_" + n)
        stk = [sb(f"stk{i}", [KROWS, 2, N], BF16) for i in range(GROUP)]
        den = [sb(f"den{i}", [P, GROUP, NT]) for i in range(2)]
        wsum = [sb(f"wsum{i}", [P, GROUP, NT]) for i in range(2)]
        top, neg = sb("top", [P, 1]), sb("neg", [P, 1])
        ring = [ctx.enter_context(nc.psum_tensor(f"a1_ring{i}", [P, N], F32)) for i in range(RING1)]
        stk_in = [sem(f"stk_in{i}") for i in range(GROUP)]
        qk_done, exp_done, inv_done, w_done, v_done = (
            sem(n) for n in ("qk_done", "exp_done", "inv_done", "w_done", "v_done"))
        zeroed = sem("zeroed")
        g_in, g_s, g_max, g_neg, g_exp, g_inv, g_w, g_v = (
            sem("g_" + n) for n in ("in", "s", "max", "neg", "exp", "inv", "w", "v"))
        block = ctx.enter_context(nc.Block())
        Q, K = 0, 1
        CHP = PAIR * NT

        def load(sp, n, place, done):
            sp.dma_start(stk[place][0:SUM_ROW], d["stack1"][bass.ds(n, 1), :, 0:SUM_ROW, :]
                         .rearrange("o s r t -> (o r) s t")).then_inc(done, 16)

        def scores(out, place, i):
            for half in range(2):
                cols = slice(half * 512, (half + 1) * 512)
                mm = nc.tensor.matmul(out[:, cols], stk[place][:, Q, i * P:(i + 1) * P],
                                      stk[place][:, K, cols], start=True, stop=True)
            return mm

        def weigh(dve, b, column, side, count, inv_sem, w_sem, v_sem):
            nc.vector.reciprocal(wsum[side][:], den[side][:]).then_inc(inv_sem, 1)
            dve.wait_ge(inv_sem, count)
            nc.vector.tensor_tensor(wsum[side][:], wsum[side][:], den[side][:], ALU.mult).then_inc(w_sem, 1)
            dve.wait_ge(w_sem, count)
            vals = R["V1"][:, bass.ds(b * NT, NT), bass.ds(column, GROUP * HD)].rearrange(
                "p t (h e) -> p t h e", e=HD)
            for h in range(GROUP):
                mul = nc.vector.tensor_tensor(vals[:, :, h, :], vals[:, :, h, :],
                                              bcast(wsum[side][:, h, :], 2, HD), ALU.mult)
            mul.then_inc(v_sem, 1)

        def general(eng, which):
            if which == "dve":
                eng.sem_inc(g_v, 1)
            with eng.Fori(0, B) as b:
                with eng.Fori(0, GROUP) as g:
                    u = b * GROUP + g
                    for h in range(GROUP):
                        n = u * GROUP + h
                        if which == "sp":
                            eng.wait_ge(g_v, u + 1)
                            load(eng, n, h, g_in)
                        for i in range(NT):
                            k = n * NT + i
                            if which == "pe":
                                if i == 0:
                                    eng.wait_ge(g_in, 16 * GROUP * (u + 1))
                                if h == 0 and i == 0:
                                    eng.wait_ge(g_v, u + 1)
                                elif i or h:
                                    eng.wait_ge(g_exp, k)
                                scores(ring[0], h, i).then_inc(g_s, 1)
                            if which == "dve":
                                eng.wait_ge(g_s, k + 1)
                                nc.vector.tensor_reduce(top[:], ring[0][:], axis=AX, op=ALU.max).then_inc(g_max, 1)
                                eng.wait_ge(g_max, k + 1)
                                nc.vector.tensor_scalar(neg[:], top[:], -SCALE1, None, ALU.mult).then_inc(g_neg, 1)
                                eng.wait_ge(g_exp, k + 1)
                            if which == "act":
                                eng.wait_ge(g_neg, k + 1)
                                nc.scalar.activation(ring[0][:], ring[0][:], ACT.Exp, scale=SCALE1, bias=neg[:],
                                                     accum_out=den[0][:, h, i:i + 1]).then_inc(g_exp, 1)
                    if which == "dve":
                        weigh(eng, b, g * GROUP * HD, 0, u + 1, g_inv, g_w, g_v)

        def by_guard(eng, which, fast):
            flag = eng.value_load(R["flag"][0:1, 1:2], min_val=0, max_val=1)
            with eng.If(flag != 0):
                general(eng, which)
            with eng.Else():
                fast(eng)

        @block.sync
        def _(sp):
            sp.wait_ge(zeroed, GROUP)
            def fast(sp):
                for place in range(GROUP):
                    load(sp, place, place, stk_in[place])
                with sp.Fori(1, GROUPS) as u:
                    for place in range(GROUP):
                        sp.wait_ge(qk_done, GROUP * NT * (u - 1) + (place + 1) * NT)
                        load(sp, u * GROUP + place, place, stk_in[place])
            by_guard(sp, "sp", fast)

        @block.tensor
        def _(pe):
            def heads(body, start):
                for h in range(PAIR):
                    pe.wait_ge(stk_in[h % GROUP], 16 * (2 * body + h // GROUP + 1))
                    for i in range(NT):
                        k = body * CHP + h * NT + i
                        if not start or h * NT + i >= RING1:
                            pe.wait_ge(exp_done, k - RING1 + 1)
                        scores(ring[(h * NT + i) % RING1], h % GROUP, i).then_inc(qk_done, 1)

            def fast(pe):
                heads(0, True)
                with pe.Fori(1, HEADS // PAIR) as body:
                    heads(body, False)
            by_guard(pe, "pe", fast)

        @block.scalar
        def _(act):
            def heads(body, start):
                for h in range(PAIR):
                    side = h // GROUP
                    if h % GROUP == 0 and not start:
                        act.wait_ge(v_done, 2 * (body - 1) + side + 1)
                    for i in range(NT):
                        k = body * CHP + h * NT + i
                        act.wait_ge(qk_done, k + 1)
                        tile = ring[(h * NT + i) % RING1]
                        nc.scalar.activation(tile[:], tile[:], ACT.Exp, scale=SCALE1,
                                             accum_out=den[side][:, h % GROUP, i:i + 1]).then_inc(exp_done, 1)

            def fast(act):
                heads(0, True)
                with act.Fori(1, HEADS // PAIR) as body:
                    heads(body, False)
            by_guard(act, "act", fast)

        @block.vector
        def _(dve):
            for i in range(GROUP):
                nc.vector.memset(stk[i][:].rearrange("r s t -> r (s t)").bitcast(F32), 0.0).then_inc(zeroed, 1)
            def fast(dve):
                with dve.Fori(0, B) as b:
                    with dve.Fori(0, 2) as half:
                        for side in range(2):
                            u = b * 4 + half * 2 + side
                            dve.wait_ge(exp_done, GROUP * NT * (u + 1))
                            weigh(dve, b, half * 2 * GROUP * HD + side * GROUP * HD, side, u + 1,
                                  inv_done, w_done, v_done)
            by_guard(dve, "dve", fast)


def finish(nc, d, R):
    with phase_semaphores(nc) as take, ExitStack() as ctx:
        sb = lambda n, s, t=F32: ctx.enter_context(nc.sbuf_tensor(n, s, t))
        ps = lambda n, s: ctx.enter_context(nc.psum_tensor(n, s, F32))
        sem = lambda n: take(n)
        V1 = R["V1"]
        att = [sb(f"fatt{i}", [P, N]) for i in range(2)]
        pT = [ps(f"fpT{i}", [P, N]) for i in range(2)]
        pO = [ps(f"fpO{i}", [P, N]) for i in range(2)]
        turned, att_ready, wo_done, added, summed, out_done = (
            sem(n) for n in ("f_turned", "f_att_ready", "f_wo_done", "f_added", "f_summed", "f_out_done"))
        block = ctx.enter_context(nc.Block())

        @block.sync
        def _(sp):
            for b in range(B):
                sp.wait_ge(summed, b + 1)
                sp.dma_start(d["out"][b * N:(b + 1) * N, :].rearrange("(t p) c -> p t c", p=P),
                             R["X"][:, b * NT:(b + 1) * NT, :]).then_inc(out_done, 16)
            sp.wait_ge(out_done, 16 * B)

        @block.tensor
        def _(pe):
            for b in range(B):
                if b >= 2:
                    pe.wait_ge(att_ready, 2 * (b - 1))
                for t in range(NT):
                    nc.tensor.transpose(pT[b % 2][:, t * P:(t + 1) * P], V1[:, b * NT + t, :],
                                        R["ident"][:]).then_inc(turned, 1)
                if b >= 2:
                    pe.wait_ge(added, b - 1)
                pe.wait_ge(att_ready, 2 * (b + 1))
                for t in range(NT):
                    mm = nc.tensor.matmul(pO[b % 2][:, t * P:(t + 1) * P], att[b % 2][:, t * P:(t + 1) * P],
                                          R["wo1"][:], start=True, stop=True)
                mm.then_inc(wo_done, 1)

        @block.scalar
        def _(act):
            for b in range(B):
                if b >= 2:
                    act.wait_ge(wo_done, b - 1)
                for half in range(2):
                    cols = slice(half * 512, (half + 1) * 512)
                    act.wait_ge(turned, NT * b + 4 * (half + 1))
                    nc.scalar.activation(att[b % 2][:, cols], pT[b % 2][:, cols], ACT.Copy).then_inc(att_ready, 1)

        @block.vector
        def _(dve):
            for b in range(B):
                xb = R["X"][:, b * NT:(b + 1) * NT, :]
                dve.wait_ge(wo_done, b + 1)
                nc.vector.tensor_tensor(xb, xb, pO[b % 2][:].rearrange("p (t c) -> p t c", c=D),
                                        ALU.add).then_inc(added, 1)
                dve.wait_ge(added, b + 1)
                nc.vector.tensor_tensor(xb, xb, bcast(R["bo1"][:], 1, NT), ALU.add).then_inc(summed, 1)


def build(nc, d):
    with ExitStack() as ctx:
        R = {}
        with ExitStack() as own:
            load_constants(nc, ctx, own, d, R)
            for name, shape in (("X", [P, B * NT, D]), ("OH", [P, B * NT, E])):
                R[name] = own.enter_context(nc.sbuf_tensor(name + "_0", shape, F32))
            prepare(nc, d, R, 0)
            guard(nc, R, 0)
            route(nc, d, R)
        attention0(nc, d, R)
        for name in ("X", "V1"):
            R[name] = ctx.enter_context(nc.sbuf_tensor(name + "_1", [P, B * NT, D], F32))
        prepare(nc, d, R, 1)
        guard(nc, R, 1)
        attention1(nc, d, R)
        finish(nc, d, R)


def kernel(L0_attn_x, L0_attn_wq, L0_attn_bq, L0_attn_wk, L0_attn_bk, L0_attn_wv, L0_attn_bv,
           L0_attn_wo, L0_attn_bo, L0_ffn_router_w, L0_ffn_routing_bias, L0_ffn_sw1, L0_ffn_sw2,
           L0_ffn_sw3, L0_ffn_ew1, L0_ffn_ew2, L0_ffn_ew3, L1_attn_w_in, L1_attn_b_in,
           L1_attn_w_out, L1_attn_b_out, L1_ffn_theta, L1_ffn_phi, L1_ffn_theta_noise,
           L1_ffn_phi_noise):
    import concourse.bacc as bacc
    from concourse.bass_utils import run_bass_kernel_spmd

    w_in = np.asarray(L1_attn_w_in).reshape(H, 3, HD, D)
    b_in = np.asarray(L1_attn_b_in).reshape(H, 3, HD)
    w1 = np.concatenate([np.asarray(L0_ffn_sw1)[None], np.asarray(L0_ffn_ew1)])
    w3 = np.concatenate([np.asarray(L0_ffn_sw3)[None], np.asarray(L0_ffn_ew3)])
    w2 = np.concatenate([np.asarray(L0_ffn_sw2)[None], np.asarray(L0_ffn_ew2)])
    w13 = np.stack([w1, w3], axis=1).transpose(0, 3, 1, 2)
    w2c = np.zeros((NE, 3 * P, D), np.float32)
    w2c[:, :I] = w2.transpose(0, 2, 1)
    w2c = w2c.reshape(NE, 3, P, D).transpose(0, 2, 1, 3)
    blk = np.zeros((P, 64), np.float32)
    for r in range(P):
        blk[r, r // HD] = 0.25
        blk[r, 32 + r // HD] = 1.0
    arrays = {
        "x": np.asarray(L0_attn_x).reshape(B * N, D),
        "wq0": np.asarray(L0_attn_wq).T, "wk0": np.asarray(L0_attn_wk).T,
        "wv0": np.asarray(L0_attn_wv).T, "wo0": np.asarray(L0_attn_wo).T,
        "bq0": np.asarray(L0_attn_bq)[:, None], "bk0": np.asarray(L0_attn_bk)[:, None],
        "bv0": np.asarray(L0_attn_bv)[None], "bo0": np.asarray(L0_attn_bo)[None],
        "rw": np.asarray(L0_ffn_router_w).T, "rb": np.asarray(L0_ffn_routing_bias)[None],
        "w13": w13, "w2": w2c,
        "wq1": w_in[:, 0].reshape(D, D).T, "wk1": w_in[:, 1].reshape(D, D).T,
        "wv1": w_in[:, 2].reshape(D, D).T, "wo1": np.asarray(L1_attn_w_out).T,
        "bq1": b_in[:, 0].reshape(D, 1), "bk1": b_in[:, 1].reshape(D, 1),
        "bv1": b_in[:, 2].reshape(1, D), "bo1": np.asarray(L1_attn_b_out)[None],
        "theta": np.asarray(L1_ffn_theta), "phi": np.asarray(L1_ffn_phi),
        "theta_noise": np.asarray(L1_ffn_theta_noise), "phi_noise": np.asarray(L1_ffn_phi_noise),
        "ident": np.eye(P, dtype=np.float32), "blk": blk,
        "tri": np.triu(np.ones((P, P), np.float32), 1), "all_ones": np.ones((P, P), np.float32),
        "marks": np.repeat(P * np.arange(B * NT, dtype=np.float32)[None], P, axis=0),
        "slots": np.arange(PLACES, dtype=np.float32)[None],
        "desc": np.repeat(np.arange(E, 0, -1, dtype=np.float32)[None], P, axis=0),
    }
    arrays = {n: np.ascontiguousarray(a) for n, a in arrays.items()}
    nc = bacc.Bacc("TRN2", target_bir_lowering=False, num_devices=1)
    d = {n: nc.dram_tensor(f"in_{n}", a.shape, F32, kind="ExternalInput").ap() for n, a in arrays.items()}
    for layer in "01":
        d["stack" + layer] = nc.dram_tensor("stack" + layer, (HEADS, 2, ROWS, N), BF16, kind="Internal").ap()
    for n in ("xg", "yg"):
        d[n] = nc.dram_tensor(n, (TILES * P, D), F32, kind="Internal").ap()
    d["v0"] = nc.dram_tensor("v0", (HEADS, P, NT * VW), F32, kind="Internal").ap()
    d["att0"] = nc.dram_tensor("att0", (GROUPS, N, GROUP * HD), F32, kind="Internal").ap()
    d["out"] = nc.dram_tensor("out", (B * N, D), F32, kind="ExternalOutput").ap()
    build(nc, d)
    r = run_bass_kernel_spmd(nc, [{f"in_{n}": a for n, a in arrays.items()}], core_ids=[0])
    return r.results[0]["out"].reshape(B, N, D)
```

```python
from contextlib import ExitStack, contextmanager

import concourse.bass as bass
import numpy as np
from concourse import mybir

F32 = mybir.dt.float32
BF16 = mybir.dt.bfloat16
I32 = mybir.dt.int32
U32 = mybir.dt.uint32
ALU = mybir.AluOpType
ACT = mybir.ActivationFunctionType
AX = mybir.AxisListType.X

P = 128
B, N, D = 4, 1024, 128
H = 16
HD = D // H
NT = N // P
HEADS = B * H
GROUP = 4
GROUPS = HEADS // GROUP
E, I = 7, 352
NE = E + 1
ICH = [(0, 128), (128, 128), (256, 96)]
EPS = 1e-5
VW = HD + 1

PAIRS = [(a, b) for b in range(3) for a in range(3 - b)]
SUM_ROW = len(PAIRS) * HD
ROWS = SUM_ROW + 6
KROWS = 72
SCALE1 = float(1.0 / np.sqrt(HD))
BOUND = [900.0, 80.0]

JOBS = 5
TILES = GROUPS * JOBS
SHARED = B * NT
PLACES = TILES - SHARED
assert PLACES >= SHARED + E - 1
IP = 3 * P

PACKS = {
    "late": {"full": {"ident": P, "wo0": D, "wq1": D, "wk1": D, "wv1": D, "wo1": D, "blk": 64,
                      "bq1": 1, "bk1": 1, "desc": E},
             "rows": {"bo0": D, "bv1": D, "bo1": D}},
    "early": {"full": {"wq0": D, "wk0": D, "wv0": D, "rw": E, "bq0": 1, "bk0": 1},
              "rows": {"bv0": D, "rb": E}},
}

TWO_PI = [6.28125, 0.0019350051879882812, 3.0199159819e-07]
MAGIC = 12582912.0


@contextmanager
def phase_semaphores(nc):
    sems = []

    def take(name):
        sems.append(nc.alloc_semaphore(name=name))
        return sems[-1]

    yield take
    nc.clear_and_free_semaphores(sems)
    nc.all_engine_barrier()


class Chain:

    def __init__(self, eng, sem):
        self.eng, self.sem, self.base, self.count = eng, sem, 0, 0

    def per_iteration(self, index, steps):
        self.base, self.count = index * steps, 0

    def step(self, instruction):
        instruction.then_inc(self.sem, 1)
        self.count += 1

    def wait(self, passed=None):
        self.eng.wait_ge(self.sem, self.base + self.count)
        if passed is not None:
            self.eng.sem_inc(passed, 1)


def wait_alone(eng, sem, value, passed):
    eng.wait_ge(sem, value)
    eng.sem_inc(passed, 1)


def bcast(ap, axis, n):
    return ap.unsqueeze(axis).to_broadcast([*ap.shape[:axis], n, *ap.shape[axis:]])


def load_constants(nc, ctx, early, d, R):
    sb = lambda n, s, t=F32: ctx.enter_context(nc.sbuf_tensor(n, s, t))
    sb_early = lambda n, s, t=F32: early.enter_context(nc.sbuf_tensor(n, s, t))
    R["WT"] = sb("WT", [P, B * NT, 2])
    R["pos"] = sb("pos", [P, B * NT], U32)
    R["expert"] = sb("expert", [1, TILES], I32)
    R["LG"] = sb("LG", [P, B * NT, E])
    R["flag"] = sb("flag", [1, 2], I32)
    R["gmax"] = sb("gmax", [64, 2 * B])
    R["cs"] = sb("cs", [P, 2 * D])
    for pack, alloc in (("late", sb), ("early", sb_early)):
        for kind, widths in PACKS[pack].items():
            tile = alloc(f"{pack}_{kind}", [P, sum(widths.values())])
            R[f"{pack}_{kind}"] = tile
            at_col = 0
            for n, width in widths.items():
                R[n] = tile[:, at_col:at_col + width]
                at_col += width
    R["bq0s"] = sb_early("bq0s", [P, 1])

    with phase_semaphores(nc) as take, ExitStack() as own:
        tmp = lambda n, s, t=F32: own.enter_context(nc.sbuf_tensor(n, s, t))
        ang = tmp("ang", [P, 2, D])
        noise = tmp("noise", [P, 2, D])
        turns = tmp("turns", [P, 2, D])
        loaded, angles_in, made, reduced, trig_done = (
            take(n) for n in ("const_loaded", "angles_in", "const_made", "angles_reduced", "trig_done"))
        block = own.enter_context(nc.Block())

        @block.sync
        def _(sp):
            for i, (a, b) in enumerate((("theta", "theta_noise"), ("phi", "phi_noise"))):
                sp.dma_start(ang[:, i, :], d[a]).then_inc(angles_in, 16)
                sp.dma_start(noise[:, i, :], d[b]).then_inc(angles_in, 16)
            for pack in ("late", "early"):
                sp.dma_start(R[pack + "_full"][:], d[pack + "_full"]).then_inc(loaded, 16)
                rows = R[pack + "_rows"]
                sp.dma_start(rows[:], d[pack + "_rows"].to_broadcast([P, rows.shape[1]])).then_inc(loaded, 16)
            sp.wait_ge(loaded, 64)

        @block.scalar
        def _(act):
            act.wait_ge(reduced, 1)
            nc.scalar.activation(R["cs"][:].rearrange("p (a c) -> p a c", a=2), ang[:, :, :],
                                 ACT.Sin).then_inc(trig_done, 1)

        @block.vector
        def _(dve):
            chain = Chain(dve, made)
            chain.step(nc.vector.memset(R["gmax"][:], 0.0))
            dve.wait_ge(angles_in, 64)
            chain.step(nc.vector.tensor_tensor(ang[:, :, :], ang[:, :, :], noise[:, :, :], ALU.add))
            chain.wait()
            for i, quarter in ((0, 0.25), (1, 0.0)):
                chain.step(nc.vector.tensor_scalar(turns[:, i, :], ang[:, i, :],
                                                   float(1 / (2 * np.pi)), quarter, ALU.mult, ALU.add))
            chain.wait()
            chain.step(nc.vector.tensor_scalar(turns[:, :, :], turns[:, :, :], MAGIC, None, ALU.add))
            chain.wait()
            chain.step(nc.vector.tensor_scalar(turns[:, :, :], turns[:, :, :], MAGIC, None, ALU.subtract))
            chain.wait()
            for part in TWO_PI:
                chain.step(nc.vector.scalar_tensor_tensor(
                    out=ang[:, :, :], in0=turns[:, :, :], scalar=-part, in1=ang[:, :, :],
                    op0=ALU.mult, op1=ALU.add))
                chain.wait()
            chain.step(nc.vector.tensor_scalar(ang[:, 0, :], ang[:, 0, :], float(np.pi / 2), None, ALU.add))
            chain.wait()
            nc.vector.tensor_scalar(ang[:, :, :], ang[:, :, :], 3.1415925, -3.1415925,
                                    ALU.min, ALU.max).then_inc(reduced, 1)
            dve.wait_ge(loaded, 64)
            chain.step(nc.vector.tensor_scalar(R["bq0s"][:], R["bq0"][:], -2.0, None, ALU.mult))
            dve.wait_ge(trig_done, 1)


def each_batch(eng, batch, begin=None):
    if begin is not None:
        begin(0)
    batch(0)
    with eng.Fori(1, B - 1) as b:
        batch(b)
    batch(B - 1)


def prepare(nc, d, R, layer):
    first = layer == 0
    L = str(layer)
    is_first = lambda b: isinstance(b, int) and b == 0
    is_last = lambda b: isinstance(b, int) and b == B - 1
    with phase_semaphores(nc) as take, ExitStack() as ctx:
        sb = lambda n, s, t=F32: ctx.enter_context(nc.sbuf_tensor(n + L, s, t))
        ps = lambda n, s: ctx.enter_context(nc.psum_tensor(n + L, s, F32))
        sem = lambda n: take("p_" + n + L)
        X, WT = R["X"], R["WT"]
        stats, mv = sb("stats", [P, NT, 6]), sb("mv", [P, NT, 2])
        rstd = sb("rstd", [P, NT])
        xn = sb("xn", [P, NT, D])
        xt = sb("xt", [P, N])
        qf, kf = sb("qf", [P, N]), sb("kf", [P, N])
        qsq, ksq = sb("qsq", [P, N]), sb("ksq", [P, N])
        qp, kp = sb("qp", [P, 3, N], BF16), sb("kp", [P, 3, N], BF16)
        qr, kr = sb("qr", [P, N]), sb("kr", [P, N])
        top, over = sb("gtop", [64, 1]), sb("gover", [1, 1])
        pX, pQ, pK, pV = ps("pX", [P, N]), ps("pQ", [P, N]), ps("pK", [P, N]), ps("pV", [P, N])
        if first:
            sums, sumr, sump = sb("sums", [64, N]), sb("sumr", [64, N]), sb("sump", [64, 3, N], BF16)
            vt = sb("vt", [P, H, NT, VW])
            ones = sb("ones", [HEADS, 3 * N], BF16)
        else:
            at, att = sb("at", [P, B * NT, D]), sb("att_t", [P, N])
            ysh, yro = sb("ysh", [P, B * NT, D]), sb("yro", [P, B * NT, D])
            ri, mag = sb("ri", [P, NT, 2, D]), sb("mag", [P, NT, D])

        s_begin, s_dve, passed = sem("begin_chain"), sem("dve_chain"), sem("passed")
        in_stage = [sem(f"in_stage{i}") for i in range(3)]
        yr_in, yr_ready = sem("yr_in"), sem("yr_ready")
        xn_stored, sh_added, ro_added = sem("xn_stored"), sem("sh_added"), sem("ro_added")
        att_p, att_ready, wo_done, wo_added, x_ready = (
            sem(n) for n in ("att_p", "att_ready", "wo_done", "wo_added", "x_ready"))
        var_ready, std_ready, xn_ready, xt_p, xt_ready = (
            sem(n) for n in ("var_ready", "std_ready", "xn_ready", "xt_p", "xt_ready"))
        q_p, k_p, v_p, qk_f, sq_ready, sum_p, sum_out, v_out = (
            sem(n) for n in ("q_p", "k_p", "v_p", "qk_f", "sq_ready", "sum_p", "sum_out", "v_out"))
        kr_ready, kp1_ready, qp_ready, kp_ready, sump_ready, stored, v_stored = (
            sem(n) for n in ("kr_ready", "kp1_ready", "qp_ready", "kp_ready", "sump_ready", "stored", "v_stored"))
        route_p, route_out, top_ready, turned = (
            sem(n) for n in ("route_p", "route_out", "top_ready", "turned"))
        mix_p, mix_out, pow_ready, mag_ready, mag_used = (
            sem(n) for n in ("mix_p", "mix_out", "pow_ready", "mag_ready", "mag_used"))
        sum_stored, s_sums = sem("sum_stored"), sem("sum_chain")
        made, fixed_out = sem("made"), sem("fixed_out")
        pT, pS = (pX, pK) if first else (pV, pQ)
        block = ctx.enter_context(nc.Block())
        stack = d["stack" + L]
        n_stores = 6

        def inputs_in(eng, b):
            stage = b if isinstance(b, int) and b < 2 else 2
            eng.wait_ge(in_stage[stage], 16 * (1 if first else 2 + GROUP * (1 if stage < 2 else B - 2)))

        tiles = lambda name, lo, hi: d[name][lo * N:hi * N, :].rearrange("(t p) c -> p t c", p=P)

        @block.sync
        def _(sp):
            for lo, hi, done in ((0, 1, in_stage[0]), (1, 2, in_stage[1]), (2, B, in_stage[2])):
                span = slice(lo * NT, hi * NT)
                if not first and lo:
                    sp.wait_ge(yr_ready, 1)
                sp.dma_start(X[:, span, :], tiles("x", lo, hi)).then_inc(done, 16)
                if not first:
                    sp.dma_start(ysh[:, span, :], tiles("yg", lo, hi)).then_inc(done, 16)
                    for u in range(lo * GROUP, hi * GROUP):
                        b, g = divmod(u, GROUP)
                        sp.dma_start(at[:, b * NT:(b + 1) * NT, g * 32:(g + 1) * 32],
                                     d["att0"][u].rearrange("(t p) c -> p t c", p=P)).then_inc(done, 16)

            if first:
                sp.wait_ge(made, 1)
                for side, row in ((0, 0), (1, 3)):
                    sp.dma_start(d["sums0"][:, row:row + 3, 1 - side, :],
                                 ones[:].rearrange("n (r t) -> n r t", r=3)).then_inc(fixed_out, 16)

            def store_sums(b):
                sp.wait_ge(sump_ready, b + 1)
                sum_rows = d["sums0"][bass.ds(b * H, H)]
                sp.dma_start(sum_rows[:, 0:3, 0, :], sump[0:H, :, :]).then_inc(sum_stored, 16)
                sp.dma_start(sum_rows[:, 3:6, 1, :], sump[32:32 + H, :, :]).then_inc(sum_stored, 16)

            def store_tokens(b):
                if first:
                    sp.wait_ge(xn_ready, NT * (b + 1))
                    sp.dma_start(d["xg"][bass.ds(b * N, N), :].rearrange("(t p) c -> p t c", p=P),
                                 xn[:, :, :]).then_inc(xn_stored, 16)

            def batch(b):
                if first and not is_first(b):
                    store_sums(b - 1)
                if not is_last(b):
                    store_tokens(b + 1)
                dst = stack[bass.ds(b * H * HD, H * HD)]
                sp.wait_ge(qp_ready, b + 1)
                for b_part in range(3):
                    n, r = 3 - b_part, PAIRS.index((0, b_part))
                    sp.dma_start(dst[:, r:r + n, 0, :],
                                 bcast(qp[:, b_part, :], 1, n)).then_inc(stored, 16)
                sp.wait_ge(kp_ready, b + 1)
                for b_part in range(3):
                    n, r = 3 - b_part, PAIRS.index((0, b_part))
                    sp.dma_start(dst[:, r:r + n, 1, :],
                                 kp[:, 0:n, :]).then_inc(stored, 16)
            each_batch(sp, batch, store_tokens)
            sp.wait_ge(stored, 16 * n_stores * B)
            if first:
                store_sums(B - 1)
                sp.wait_ge(sum_stored, 32 * B)
                sp.wait_ge(v_stored, 16 * B)
                sp.wait_ge(xn_stored, 16 * B)
                sp.wait_ge(fixed_out, 32)

        @block.tensor
        def _(pe):
            def turn_attention(b):
                inputs_in(pe, b)
                if b:
                    pe.wait_ge(mix_out, 4 * (b - 1))
                for t in range(NT):
                    nc.tensor.transpose(pX[:, t * P:(t + 1) * P], at[:, b * NT + t, :], R["ident"][:]).then_inc(att_p, 1)

            def project_attention(b):
                pe.wait_ge(att_ready, b + 1)
                for t in range(NT):
                    mm = nc.tensor.matmul(pX[:, t * P:(t + 1) * P], att[:, t * P:(t + 1) * P],
                                          R["wo0"][:], start=True, stop=True)
                mm.then_inc(wo_done, 1)

            def turn_tokens(b):
                pe.wait_ge(xt_ready, 2 * b) if first else pe.wait_ge(v_out, b)
                for t in range(NT):
                    pe.wait_ge(xn_ready, NT * b + t + 1)
                    nc.tensor.transpose(pT[:, t * P:(t + 1) * P], xn[:, t, :], R["ident"][:]).then_inc(xt_p, 1)

            def batch(b):
                if not first and not is_last(b):
                    turn_attention(b + 1)
                pe.wait_ge(route_out if first else sum_out, b)
                pe.wait_ge(xt_ready, 2 * (b + 1))
                for half in range(2):
                    cols = slice(half * 512, (half + 1) * 512)
                    mm = nc.tensor.matmul(pQ[:, cols], R["wq" + L][:], xt[:, cols], start=True, stop=True)
                mm.then_inc(q_p, 1)
                if first:
                    pe.wait_ge(sum_out, b)
                for half in range(2):
                    cols = slice(half * 512, (half + 1) * 512)
                    mm = nc.tensor.matmul(pK[:, cols], R["wk" + L][:], xt[:, cols], start=True, stop=True)
                mm.then_inc(k_p, 1)
                if not first and not is_last(b):
                    project_attention(b + 1)
                pe.wait_ge(v_out, b)
                for t in range(NT):
                    mm = nc.tensor.matmul(pV[:, t * P:(t + 1) * P], xt[:, t * P:(t + 1) * P],
                                          R["wv" + L][:], start=True, stop=True)
                mm.then_inc(v_p, 1)
                if first:
                    if not is_last(b):
                        turn_tokens(b + 1)
                    pe.wait_ge(qk_f, 2 * b + 1)
                    for t in range(NT):
                        mm = nc.tensor.matmul(pQ[:, t * 8:t * 8 + E], xt[:, t * P:(t + 1) * P],
                                              R["rw"][:], start=True, stop=True)
                    mm.then_inc(route_p, 1)
                pe.wait_ge(qk_f, 2 * b + (2 if first else 1))
                pe.wait_ge(sq_ready, b + 1)
                for half in range(2):
                    cols = slice(half * 512, (half + 1) * 512)
                    nc.tensor.matmul(pS[0:32, cols], R["blk"][:, 0:32], qsq[:, cols], start=True, stop=True)
                    mm = nc.tensor.matmul(pS[32:64, cols], R["blk"][:, 32:64], ksq[:, cols], start=True, stop=True)
                mm.then_inc(sum_p, 1)
                if not first:
                    if not is_last(b):
                        pe.wait_ge(wo_added, b + 2)
                    for r in range(4):
                        if r >= 2:
                            pe.wait_ge(mix_out, 4 * b + r - 1)
                        for j in range(2):
                            t, at_col = 2 * r + j, (r % 2) * 512 + j * 256
                            mm = nc.tensor.matmul(pX[:, at_col:at_col + 256], xt[:, t * P:(t + 1) * P],
                                                  R["cs"][:], start=True, stop=True)
                        mm.then_inc(mix_p, 1)
                    if not is_last(b):
                        turn_tokens(b + 1)
            if first:
                each_batch(pe, batch, turn_tokens)
            else:
                turn_attention(0)
                project_attention(0)
                turn_tokens(0)
                for b in range(B):
                    batch(b)
            pe.wait_ge(top_ready, 1)
            nc.tensor.transpose(pK[0:1, 0:64], top[:], R["ident"][0:64, 0:64]).then_inc(turned, 1)

        @block.scalar
        def _(act):
            def keep_attention(b):
                for half in range(2):
                    cols = slice(half * 512, (half + 1) * 512)
                    act.wait_ge(att_p, NT * b + 4 * (half + 1))
                    cp = nc.scalar.activation(att[:, cols], pX[:, cols], ACT.Copy)
                cp.then_inc(att_ready, 1)

            def keep_sums(b):
                act.wait_ge(sum_p, b + 1)
                if not is_first(b):
                    act.wait_ge(sum_stored, 32 * b)
                nc.scalar.activation(sums[:], pS[0:64, :], ACT.Copy)
                nc.scalar.activation(sump[:, 0, :], pS[0:64, :], ACT.Copy).then_inc(sum_out, 1)

            def magnitudes(b):
                act.wait_ge(pow_ready, b + 1)
                nc.scalar.activation(mag[:, :, :], mag[:, :, :], ACT.Sqrt).then_inc(mag_ready, 1)

            def begin(b):
                if not first and is_first(b):
                    keep_attention(b)
                act.wait_ge(var_ready, b + 1)
                nc.scalar.activation(rstd[:], mv[:, :, 1], ACT.Sqrt).then_inc(std_ready, 1)

            def batch(b):
                if first:
                    act.wait_ge(route_p, b)
                else:
                    act.wait_ge(mix_p, 4 * b)
                for half in range(2):
                    cols = slice(half * 512, (half + 1) * 512)
                    act.wait_ge(xt_p, NT * b + 4 * (half + 1))
                    nc.scalar.activation(xt[:, cols], pT[:, cols], ACT.Copy).then_inc(xt_ready, 1)
                if not first and not is_last(b):
                    keep_attention(b + 1)
                if not is_first(b):
                    keep_sums(b - 1) if first else magnitudes(b - 1)
                q_bias, q_scale = (R["bq0s"], -2.0) if first else (R["bq1"], 1.0)
                act.wait_ge(q_p, b + 1)
                act.wait_ge(qp_ready, b)
                nc.scalar.activation(qf[:], pQ[:], ACT.Identity, bias=q_bias[:], scale=q_scale)
                if first and not is_last(b):
                    begin(b + 1)
                act.wait_ge(stored, 16 * n_stores * b)
                nc.scalar.activation(qp[:, 0, :], pQ[:], ACT.Identity, bias=q_bias[:], scale=q_scale).then_inc(qk_f, 1)
                act.wait_ge(k_p, b + 1)
                act.wait_ge(kp_ready, b)
                nc.scalar.activation(kf[:], pK[:], ACT.Identity, bias=R["bk" + L][:])
                nc.scalar.activation(kp[:, 0, :], pK[:], ACT.Identity, bias=R["bk" + L][:]).then_inc(qk_f, 1)
                act.wait_ge(sum_p, b)
                act.wait_ge(qk_f, 2 * b + 2)
                nc.scalar.activation(qsq[:], qf[:], ACT.Square)
                nc.scalar.activation(ksq[:], kf[:], ACT.Square).then_inc(sq_ready, 1)
                act.wait_ge(kr_ready, b + 1)
                nc.scalar.activation(kp[:, 1, :], kr[:], ACT.Copy).then_inc(kp1_ready, 1)
                if not first:
                    for r in range(4):
                        act.wait_ge(mix_p, 4 * b + r + 1)
                        if r == 0:
                            act.wait_ge(pow_ready, b)
                        nc.scalar.activation(ri[:, 2 * r:2 * r + 2, :, :].rearrange("p t a c -> p (t a c)"),
                                             pX[:, (r % 2) * 512:(r % 2 + 1) * 512], ACT.Square
                                             ).then_inc(mix_out, 1)
                    if not is_last(b):
                        begin(b + 1)
            each_batch(act, batch, begin)
            keep_sums(B - 1) if first else magnitudes(B - 1)

        @block.gpsimd
        def _(pool):
            def begin(b):
                for t in range(b * NT, (b + 1) * NT):
                    pool.indirect_dma_start(
                        out=yro[:, t, :], out_offset=None, in_=d["yg"][:, :],
                        in_offset=bass.IndirectOffsetOnAxis(ap=R["pos"][:, t:t + 1], axis=0)
                    ).then_inc(yr_in, 16)
                pool.wait_ge(yr_in, 16 * NT * (b + 1))
                pool.sem_inc(yr_ready, 1)

            def batch(b):
                if not first and not is_last(b):
                    begin(b + 1)
                pool.wait_ge(kp_ready, b)
                pool.wait_ge(qk_f, 2 * b + 2)
                nc.gpsimd.tensor_tensor(kr[:], kf[:], kp[:, 0, :], ALU.subtract).then_inc(kr_ready, 1)
                pool.wait_ge(kp1_ready, b + 1)
                nc.gpsimd.tensor_tensor(kp[:, 2, :], kr[:], kp[:, 1, :], ALU.subtract).then_inc(kp_ready, 1)
                if first:
                    pool.wait_ge(v_out, b + 1)
                    pool.dma_start(d["v0"][bass.ds(b * H, H)].rearrange("h p w -> p h w"),
                                   vt[:].rearrange("p h t w -> p h (t w)")).then_inc(v_stored, 16)
            if first:
                nc.gpsimd.memset(ones[:], 1.0).then_inc(made, 1)
                each_batch(pool, batch)
            else:
                begin(0)
                for b in range(B):
                    batch(b)

        @block.vector
        def _(dve):
            begins, chain, sum_chain = Chain(dve, s_begin), Chain(dve, s_dve), Chain(dve, s_sums)
            if first:
                chain.step(nc.vector.memset(vt[:].rearrange("p h t w -> p (h t) w")[:, :, HD], 1.0))
                chain.wait()
            before = chain.count
            BEGIN_STEPS, STEPS, SUM_STEPS = 3, 2, 3
            x_of = lambda b, t: X[:, bass.ds(b * NT + t, 1), :].rearrange("p o c -> p (o c)")
            col = lambda tile, b, t: tile[:, bass.ds(b * NT + t, 1), :].rearrange("p o c -> p (o c)")

            def add_experts(b):
                inputs_in(dve, b)
                for y, k, added in ((ysh, 0, sh_added), (yro, 1, ro_added)):
                    if k == 1:
                        dve.wait_ge(yr_ready, b + 1)
                    for t in range(NT):
                        weight = WT[:, bass.ds(b * NT + t, 1), k:k + 1].rearrange("p o c -> p (o c)")
                        add = nc.vector.scalar_tensor_tensor(out=x_of(b, t), in0=col(y, b, t), scalar=weight,
                                                             in1=x_of(b, t), op0=ALU.mult, op1=ALU.add)
                    add.then_inc(added, 1)
                    dve.wait_ge(added, b + 1)

            def begin(b):
                begins.per_iteration(b, BEGIN_STEPS)
                xb = X[:, bass.ds(b * NT, NT), :]
                if first:
                    inputs_in(dve, b)
                if not first:
                    if isinstance(b, int) and b == 0:
                        add_experts(b)
                    dve.wait_ge(wo_done, b + 1)
                    nc.vector.tensor_tensor(xb, xb, pX[:].rearrange("p (t c) -> p t c", c=D), ALU.add
                                            ).then_inc(wo_added, 1)
                    dve.wait_ge(wo_added, b + 1)
                    nc.vector.tensor_tensor(xb, xb, bcast(R["bo0"][:], 1, NT), ALU.add).then_inc(x_ready, 1)
                    wait_alone(dve, x_ready, b + 1, passed)
                for t in range(NT):
                    st = nc.vector.bn_stats(stats[:, t, :], x_of(b, t))
                begins.step(st)
                begins.wait(passed)
                for t in range(NT):
                    st = nc.vector.bn_aggr(mv[:, t, :], stats[:, t, :])
                begins.step(st)
                begins.wait()
                nc.vector.tensor_scalar(mv[:, :, 1], mv[:, :, 1], EPS, None, ALU.add).then_inc(var_ready, 1)

            def normalise(b):
                dve.wait_ge(std_ready, b + 1)
                begins.step(nc.vector.reciprocal(rstd[:], rstd[:]))
                begins.wait()
                assert begins.count == BEGIN_STEPS
                dve.wait_ge(xt_p, NT * b)
                if first:
                    dve.wait_ge(xn_stored, 16 * b)
                for t in range(NT):
                    nc.vector.tensor_scalar(xn[:, t, :], x_of(b, t), mv[:, t, 0:1], rstd[:, t:t + 1],
                                            ALU.subtract, ALU.mult).then_inc(xn_ready, 1)

            def split_sums(b):
                sum_chain.per_iteration(b, SUM_STEPS)
                gm = R["gmax"][:, bass.ds(b + layer * B, 1)]
                dve.wait_ge(sum_out, b + 1)
                sum_chain.step(nc.vector.tensor_tensor(sumr[:], sums[:], sump[:, 0, :], ALU.subtract))
                sum_chain.step(nc.vector.tensor_reduce(gm, sums[:], axis=AX, op=ALU.max))
                sum_chain.wait()
                sum_chain.step(nc.vector.tensor_copy(sump[:, 1, :], sumr[:]))
                sum_chain.wait()
                assert sum_chain.count == SUM_STEPS
                nc.vector.tensor_tensor(sump[:, 2, :], sumr[:], sump[:, 1, :], ALU.subtract).then_inc(sump_ready, 1)

            def add_magnitudes(b):
                dve.wait_ge(mag_ready, b + 1)
                xb = X[:, bass.ds(b * NT, NT), :]
                nc.vector.tensor_tensor(xb, xb, mag[:, :, :], ALU.add).then_inc(mag_used, 1)

            def batch(b):
                chain.base, chain.count = b * STEPS + before, 0
                if not is_last(b):
                    begin(b + 1) if first else add_experts(b + 1)
                if not is_first(b):
                    split_sums(b - 1) if first else add_magnitudes(b - 1)
                if first and not is_last(b):
                    normalise(b + 1)
                dve.wait_ge(qk_f, 2 * b + 1)
                chain.step(nc.vector.tensor_tensor(qr[:], qf[:], qp[:, 0, :], ALU.subtract))
                chain.wait()
                chain.step(nc.vector.tensor_copy(qp[:, 1, :], qr[:]))
                chain.wait()
                nc.vector.tensor_tensor(qp[:, 2, :], qr[:], qp[:, 1, :], ALU.subtract).then_inc(qp_ready, 1)
                if not first and not is_last(b):
                    begin(b + 1)
                if first:
                    dve.wait_ge(route_p, b + 1)
                    nc.vector.tensor_tensor(R["LG"][:, bass.ds(b * NT, NT), :],
                                            pQ[:, 0:64].rearrange("p (t e) -> p t e", e=8)[:, :, 0:E],
                                            bcast(R["rb"][:], 1, NT), ALU.add).then_inc(route_out, 1)
                dve.wait_ge(v_p, b + 1)
                if first:
                    dve.wait_ge(v_stored, 16 * b)
                    for t in range(NT):
                        va = nc.vector.tensor_tensor(vt[:, :, t, 0:HD],
                                                     pV[:, t * P:(t + 1) * P].rearrange("p (h e) -> p h e", e=HD),
                                                     R["bv0"][:].rearrange("p (h e) -> p h e", e=HD), ALU.add)
                    va.then_inc(v_out, 1)
                else:
                    nc.vector.tensor_tensor(R["V1"][:, bass.ds(b * NT, NT), :],
                                            pV[:].rearrange("p (t c) -> p t c", c=D),
                                            bcast(R["bv1"][:], 1, NT), ALU.add).then_inc(v_out, 1)
                if not first:
                    gm = R["gmax"][:, bass.ds(b + layer * B, 1)]
                    wait_alone(dve, sum_p, b + 1, passed)
                    nc.vector.tensor_reduce(gm, pQ[0:64, :], axis=AX, op=ALU.max).then_inc(sum_out, 1)
                    if not is_last(b):
                        normalise(b + 1)
                    dve.wait_ge(mix_out, 4 * b + 4)
                    dve.wait_ge(mag_used, b)
                    nc.vector.tensor_tensor(mag[:, :, :], ri[:, :, 0, :], ri[:, :, 1, :], ALU.add).then_inc(pow_ready, 1)
                assert chain.count == STEPS, chain.count
            def start(b):
                begin(b)
                normalise(b)
            each_batch(dve, batch, start)
            split_sums(B - 1) if first else add_magnitudes(B - 1)
            dve.wait_ge(sum_out, B)
            chain.base, chain.count = B * STEPS + before, 0
            chain.wait()
            nc.vector.tensor_reduce(top[:], R["gmax"][:, layer * B:(layer + 1) * B], axis=AX,
                                    op=ALU.max).then_inc(top_ready, 1)
            dve.wait_ge(turned, 1)
            chain.step(nc.vector.tensor_reduce(over[:], pK[0:1, 0:64], axis=AX, op=ALU.max))
            chain.wait()
            chain.step(nc.vector.tensor_scalar(over[:], over[:], BOUND[layer], None, ALU.is_gt))
            chain.wait()
            chain.step(nc.vector.tensor_copy(R["flag"][:, layer:layer + 1], over[:]))
            chain.wait()


def routing(nc, d, R, room, rank_p, count_p, take):
    TOK = B * NT
    used = 0

    def part(rows, *shape):
        nonlocal used
        flat = room[0:rows, used:used + int(np.prod(shape))]
        used += int(np.prod(shape))
        assert used <= room.shape[1]
        if len(shape) == 1:
            return flat
        return flat.rearrange("p (a b) -> p a b", b=shape[1])

    tri, ones, marks, slots = part(P, P), part(P, P), part(P, TOK), part(1, PLACES)
    cnt, run = part(P, TOK, E), [part(P, TOK, E) for _ in range(2)]
    over, tiles, end, base = part(P, E, TOK), part(P, E), part(P, E), part(P, E)
    past, ex, posf = part(1, PLACES, E), part(1, PLACES), part(P, TOK)
    pr, top, inv = part(P, TOK, E), part(P, TOK), part(P, TOK)
    loaded, clipped, e_ready, chosen, counted, chain_sem, ranks_read, routed = (
        take("r_" + n) for n in ("loaded", "clipped", "e_ready", "chosen", "counted", "chain", "ranks_read",
                             "routed"))
    OH, WT = R["LG"], R["WT"]

    def load(sp):
        for tile, name in ((tri, "tri"), (ones, "all_ones"), (marks, "marks"), (slots, "slots")):
            sp.dma_start(tile, d[name]).then_inc(loaded, 16)

    def rank(pe):
        pe.wait_ge(loaded, 64)
        pe.wait_ge(chosen, 1)
        flat = OH[:, :, :].rearrange("p t e -> p (t e)")
        nc.tensor.matmul(rank_p, tri, flat, start=True, stop=True)
        nc.tensor.matmul(count_p, ones, flat, start=True, stop=True).then_inc(counted, 1)

    def powers(act):
        act.wait_ge(clipped, 1)
        nc.scalar.activation(pr, OH[:, :, :], ACT.Exp, scale=-1.0).then_inc(e_ready, 1)

    def choose(dve):
        chain = Chain(dve, chain_sem)
        shape = lambda ap: ap.rearrange("p (t e) -> p t e", e=E)
        dve.wait_ge(loaded, 64)
        nc.vector.tensor_scalar(OH[:, :, :], OH[:, :, :], -50.0, 50.0, ALU.max, ALU.min).then_inc(clipped, 1)
        yield
        dve.wait_ge(e_ready, 1)
        chain.step(nc.vector.tensor_scalar(pr[:, :, :], pr[:, :, :], 1.0, None, ALU.add))
        yield
        chain.wait()
        chain.step(nc.vector.reciprocal(pr[:, :, :], pr[:, :, :]))
        yield
        chain.wait()
        chain.step(nc.vector.tensor_reduce(top[:], pr[:, :, :], axis=AX, op=ALU.max))
        yield
        chain.wait()
        chain.step(nc.vector.tensor_tensor(pr[:, :, :], pr[:, :, :], bcast(top[:], 2, E), ALU.is_equal))
        yield
        chain.wait()
        chain.step(nc.vector.tensor_tensor(pr[:, :, :], pr[:, :, :], bcast(R["desc"][:], 1, TOK), ALU.mult))
        yield
        chain.wait()
        chain.step(nc.vector.tensor_reduce(inv[:], pr[:, :, :], axis=AX, op=ALU.max))
        yield
        chain.wait()
        nc.vector.tensor_tensor(OH[:, :, :], pr[:, :, :], bcast(inv[:], 2, E), ALU.is_equal).then_inc(chosen, 1)
        chain.step(nc.vector.tensor_scalar(top[:], top[:], 1e-8, 1.0 - 1e-8, ALU.max, ALU.min))
        yield
        chain.wait()
        dve.wait_ge(chosen, 1)
        chain.step(nc.vector.tensor_scalar(inv[:], top[:], 0.5, 1e-8, ALU.add, ALU.add))
        yield
        chain.wait()
        chain.step(nc.vector.tensor_scalar(inv[:], inv[:], 0.5, 2.0, ALU.max, ALU.min))
        yield
        chain.wait()
        chain.step(nc.vector.reciprocal(inv[:], inv[:]))
        yield
        chain.wait()
        chain.step(nc.vector.tensor_scalar(WT[:, :, 0], inv[:], 0.25, None, ALU.mult))
        chain.step(nc.vector.scalar_tensor_tensor(out=WT[:, :, 1], in0=top[:], scalar=0.5, in1=inv[:],
                                                  op0=ALU.mult, op1=ALU.mult))
        yield
        chain.wait()
        yield
        dve.wait_ge(counted, 1)
        chain.step(nc.vector.tensor_copy(cnt[:, :, :], shape(count_p)))
        chain.step(nc.vector.tensor_copy(run[0][:, :, :], shape(count_p)))
        yield
        chain.wait()
        step, now = 1, 0
        while step < TOK:
            src, dst = run[now], run[1 - now]
            chain.step(nc.vector.tensor_copy(dst[:, 0:step, :], src[:, 0:step, :]))
            chain.step(nc.vector.tensor_tensor(dst[:, step:, :], src[:, step:, :], src[:, 0:TOK - step, :], ALU.add))
            yield
            chain.wait()
            step, now = 2 * step, 1 - now
        total = run[now][:, TOK - 1, :]
        chain.step(nc.vector.tensor_tensor(over[:, :, :], bcast(total, 2, TOK), bcast(marks[:], 1, E), ALU.is_gt))
        yield
        chain.wait()
        chain.step(nc.vector.tensor_reduce(tiles[:], over[:, :, :], axis=AX, op=ALU.add))
        yield
        chain.wait()
        chain.step(nc.vector.tensor_copy(end[:, 0:1], tiles[:, 0:1]))
        yield
        chain.wait()
        for e in range(1, E):
            chain.step(nc.vector.tensor_tensor(end[:, e:e + 1], end[:, e - 1:e], tiles[:, e:e + 1], ALU.add))
            yield
            chain.wait()
        chain.step(nc.vector.tensor_tensor(base[:], end[:], tiles[:], ALU.subtract))
        yield
        chain.wait()
        chain.step(nc.vector.tensor_scalar(base[:], base[:], float(P), float(SHARED * P), ALU.mult, ALU.add))
        chain.step(nc.vector.tensor_tensor(cnt[:, :, :], run[now][:, :, :], cnt[:, :, :], ALU.subtract))
        yield
        chain.wait()
        nc.vector.tensor_tensor(cnt[:, :, :], cnt[:, :, :], shape(rank_p), ALU.add).then_inc(ranks_read, 1)
        yield
        dve.wait_ge(ranks_read, 1)
        chain.step(nc.vector.tensor_tensor(cnt[:, :, :], cnt[:, :, :], bcast(base[:], 1, TOK), ALU.add))
        yield
        chain.wait()
        chain.step(nc.vector.tensor_tensor(cnt[:, :, :], cnt[:, :, :], OH[:, :, :], ALU.mult))
        yield
        chain.wait()
        chain.step(nc.vector.tensor_reduce(posf[:], cnt[:, :, :], axis=AX, op=ALU.add))
        yield
        chain.wait()
        chain.step(nc.vector.tensor_copy(R["pos"][:], posf[:]))
        chain.step(nc.vector.tensor_tensor(past[:, :, :], bcast(end[0:1, :], 1, PLACES),
                                           bcast(slots[:], 2, E), ALU.is_le))
        yield
        chain.wait()
        chain.step(nc.vector.tensor_reduce(ex[:], past[:, :, :], axis=AX, op=ALU.add))
        yield
        chain.wait()
        chain.step(nc.vector.tensor_scalar(ex[:], ex[:], 1.0, float(E), ALU.add, ALU.min))
        yield
        chain.wait()
        nc.vector.tensor_copy(R["expert"][:, SHARED:TILES], ex[:]).then_inc(routed, 1)

    return load, rank, powers, choose, ranks_read, routed


CH = 8
RING = 3


def ring_uses(ahead, now):
    uses = []
    for place in range(GROUP):
        for j in range(CH):
            if ahead:
                uses.append(("qk", place, j))
                if (place, j) == (0, 3):
                    uses.append(("tokens", 0))
            if now and (place, j) in HIDDEN_AT:
                uses.append(("hidden", HIDDEN_AT.index((place, j))))
    return (uses + [("up", j) for j in range(JOBS) if ahead] + [("down", 0)] * now)


READ_AT = [(1, 1), (1, 4), (1, 7), (2, 1), (2, 4)]
HIDDEN_AT = [(2, 2), (2, 6), (3, 2)]
FULL_SHARED = SHARED // JOBS
ROUND = ring_uses(True, True)
CYCLE = len(ROUND)
assert CYCLE % RING == 0 and len(HIDDEN_AT) == (JOBS + 1) // 2
FIRST, LAST = ring_uses(True, False), ring_uses(False, True)
ALONE = [u for u in ROUND if u[0] != "qk"]
ALONE = [u for u in ALONE if u[0] in ("tokens", "up")] + [u for u in ALONE if u[0] in ("hidden", "down")]


def attention0(nc, d, R):
    layer, L = 0, "0"
    SLOTS = 2
    with phase_semaphores(nc) as take, ExitStack() as ctx:
        sb = lambda n, s, t=F32: ctx.enter_context(nc.sbuf_tensor(n + L, s, t))
        ps = lambda n, s: ctx.enter_context(nc.psum_tensor(n + L, s, F32))
        sem = lambda n: take("a0_" + n)
        S = [sb(f"scores{i}", [P, CH * N]) for i in range(GROUP)]
        stk = [sb(f"stk{i}", [KROWS, 2, N], BF16) for i in range(SLOTS)]
        w13, w2 = sb("w13", [P, NE, 2, I]), sb("w2", [P, NE, 3, D])
        xj, xjt = sb("xj", [P, JOBS, D]), sb("xjt", [P, JOBS * P])
        h1, gate = sb("h1", [P, JOBS, I]), sb("gate", [P, JOBS, IP])
        ht = sb("ht", [P, JOBS, IP])
        yj = ht[:, :, 0:D]
        val = [sb(f"val{i}", [P, CH, VW]) for i in range(GROUP)]
        ot = sb("ot", [P, 256])
        rden = sb("rden", [P, GROUP, NT])
        attg = sb("attg", [P, NT, 32])
        mcol = sb("mcol", [P, 1])
        zeros = attg[:, :, :].rearrange("p t w -> p (t w)")
        ring = [ps(f"ring{i}", [P, N]) for i in range(RING)]
        pvb = [ps(f"pvb{i}", [P, 512]) for i in range(2)]
        stk_in = [sem(f"stk_in{i}") for i in range(SLOTS)]
        val_in = [sem(f"val_in{i}") for i in range(GROUP)]
        ring_full, ring_free, root_done, exp_done, pv_done = (
            sem(n) for n in ("ring_full", "ring_free", "root_done", "exp_done", "pv_done"))
        zeroed = sem("zeroed")
        places_clear, placed, tok_in, w_rest, w2_in, w_in, xj_in, h1_done, tanh_done, part_done, hid_done, y_stored, y_free = (
            sem("j_" + n) for n in ("places_clear", "placed", "tok_in", "w_rest", "w2_in", "w_in", "xj_in", "h1_done", "tanh_done", "part_done", "hid_done",
                                    "y_stored", "y_free"))
        attg_free, g_slot = sem("attg_free"), sem("g_slot")
        cleared, ot_ready, turned, rden_ready, att_ready, att_out = (
            sem(n) for n in ("cleared", "ot_ready", "turned", "rden_ready", "att_ready", "att_out"))
        g_in, g_s, g_copied, g_root, g_max, g_exp, g_turn, g_pt, g_pv, g_rd, g_att, g_out = (
            sem("g_" + n) for n in ("in", "s", "copied", "root", "max", "exp", "turn", "pt",
                                    "pv", "rd", "att", "out"))
        load_router, rank, powers, choose, ranks_read, routed = routing(
            nc, d, R, w2[:, :, :, :].rearrange("p e k c -> p (e k c)"), pvb[0][:, 0:SHARED * E],
            pvb[1][:, 0:SHARED * E], take)
        tokens = w13[:, :, :, :].rearrange("p e a i -> p (e a i)")[:, 2 * I:2 * I + SHARED * D]
        block = ctx.enter_context(nc.Block())
        Q, K = 0, 1
        CHG = GROUP * CH

        def count(uses, base, use):
            return base + uses.index(use) + 1

        def take(pe, uses, base, use, ago=RING):
            if not isinstance(base, int) or base + uses.index(use) >= ago:
                pe.wait_ge(ring_free, count(uses, base, use) - ago)
            return ring[uses.index(use) % RING]

        def filled(dve, uses, base, use):
            dve.wait_ge(ring_full, count(uses, base, use))
            return ring[uses.index(use) % RING]

        def qk(pe, uses, base, group, place, j):
            slot = place % SLOTS
            if j == 0:
                pe.wait_ge(stk_in[slot], 32 * (GROUP // SLOTS * group + place // SLOTS + 1))
            tile = take(pe, uses, base, ("qk", place, j))
            for half in range(2):
                cols = slice(half * 512, (half + 1) * 512)
                mm = nc.tensor.matmul(tile[:, cols], stk[slot][:, K, j * P:(j + 1) * P],
                                      stk[slot][:, Q, cols], start=True, stop=True)
            mm.then_inc(ring_full, 1)

        def pv(pe, group, place, j):
            if j == 0:
                pe.wait_ge(val_in[place], 16 * (group + 1))
                if place >= 2:
                    pe.wait_ge(att_ready, GROUP * group + place - 1)
                pe.wait_ge(exp_done, GROUP * group + place + 1)
            for c in range(4):
                mm = nc.tensor.matmul(pvb[place % 2][32 * c:32 * c + VW, 0:256], val[place][:, j, :],
                                      S[place][:, j * N + c * 256:j * N + (c + 1) * 256],
                                      start=(j == 0), stop=(j == CH - 1))
            mm.then_inc(pv_done, 1)

        def turn(pe, group, place):
            pe.wait_ge(ot_ready, GROUP * group + place + 1)
            for t in range(2):
                mm = nc.tensor.transpose(pvb[place % 2][:, 256 + t * P:256 + (t + 1) * P],
                                         ot[:, t * P:(t + 1) * P], R["ident"][:])
            mm.then_inc(turned, 1)

        def clear_places(sp):
            for n in range(0, PLACES, NT):
                sp.dma_start(d["xg"][(SHARED + n) * P:(SHARED + n + NT) * P, :]
                             .rearrange("(p a t) c -> p a (t c)", p=P, t=2), bcast(zeros, 1, NT // 2)
                             ).then_inc(places_clear, 16)

        def load_down(pool):
            pool.wait_ge(routed, 1)
            pool.dma_start(w2[:, :, :, :], d["w2"].rearrange("e p k c -> p e k c")).then_inc(w2_in, 16)

        def place_tokens(pool):
            pool.wait_ge(tok_in, 16)
            pool.wait_ge(places_clear, 16 * (PLACES // NT))
            for t in range(B * NT):
                pool.indirect_dma_start(
                    out=d["xg"][:, :], out_offset=bass.IndirectOffsetOnAxis(ap=R["pos"][:, t:t + 1], axis=0),
                    in_=tokens[:, t * D:(t + 1) * D], in_offset=None).then_inc(placed, 16)
            pool.wait_ge(placed, 16 * B * NT)
            pool.dma_start(w13[:, 1:NE, :, :], d["w13"][1:NE].rearrange("e c a i -> c e a i")).then_inc(w_rest, 16)

        def load_jobs(sp, v):
            sp.dma_start(xj[:, :, :], d["xg"][bass.ds(v * (JOBS * P), JOBS * P), :]
                         .rearrange("(j p) c -> p j c", p=P)).then_inc(xj_in, 16)

        def expert_of(pe, v, j):
            return pe.value_load(R["expert"][0:1, bass.ds(v * JOBS + j, 1)], min_val=0, max_val=E)

        def experts_of(pe, v):
            return [expert_of(pe, v, j) for j in range(JOBS)]

        def turn_tokens(pe, uses, base, v, **ago):
            pe.wait_ge(xj_in, 16 * (v + 1))
            tile = take(pe, uses, base, ("tokens", 0), **ago)
            for j in range(JOBS):
                mm = nc.tensor.transpose(tile[:, j * P:(j + 1) * P], xj[:, j, :], R["ident"][:])
            mm.then_inc(ring_full, 1)

        def up(pe, uses, base, e, **ago):
            pe.wait_ge(ring_free, count(uses, base, ("tokens", 0)))
            for j in range(JOBS):
                tile = take(pe, uses, base, ("up", j), **ago)
                for side in range(2):
                    mm = nc.tensor.matmul(tile[:, side * 512:side * 512 + I], xjt[:, j * P:(j + 1) * P],
                                          w13[:, bass.ds(e[j], 1), side, :].rearrange("p o i -> p (o i)"),
                                          start=True, stop=True)
                mm.then_inc(ring_full, 1)

        def keep_tokens(dve, uses, base):
            tile = filled(dve, uses, base, ("tokens", 0))
            nc.vector.tensor_copy(xjt[:], tile[:, 0:JOBS * P]).then_inc(ring_free, 1)

        def keep_up(dve, uses, base, v):
            for j in range(JOBS):
                tile = filled(dve, uses, base, ("up", j))
                nc.vector.tensor_copy(h1[:, j, :], tile[:, 0:I]).then_inc(h1_done, 1)
                dve.wait_ge(h1_done, JOBS * v + j + 1)
                nc.vector.tensor_tensor(gate[:, j, 0:I], h1[:, j, :], tile[:, 512:512 + I],
                                        ALU.mult).then_inc(ring_free, 1)

        def tanh(act, uses, base):
            act.wait_ge(ring_free, count(uses, base, ("up", JOBS - 1)))
            nc.scalar.activation(h1[:, :, :], h1[:, :, :], ACT.Tanh, scale=0.5).then_inc(tanh_done, 1)

        def hidden(pool, v):
            pool.wait_ge(tanh_done, v + 1)
            nc.gpsimd.tensor_tensor(h1[:, :, :], h1[:, :, :], gate[:, :, 0:I], ALU.mult).then_inc(part_done, 1)
            pool.wait_ge(part_done, v + 1)
            nc.gpsimd.tensor_tensor(gate[:, :, 0:I], gate[:, :, 0:I], h1[:, :, :], ALU.add).then_inc(hid_done, 1)

        def turn_hidden(pe, uses, base, v, i, **ago):
            pe.wait_ge(hid_done, v + 1)
            tile = take(pe, uses, base, ("hidden", i), **ago)
            for j in range(2 * i, min(2 * i + 2, JOBS)):
                for c in range(3):
                    at_col = (j % 2) * 512 + c * P
                    mm = nc.tensor.transpose(tile[:, at_col:at_col + P], gate[:, j, c * P:(c + 1) * P],
                                             R["ident"][:])
            mm.then_inc(ring_full, 1)

        def keep_hidden(dve, uses, base, v, i):
            tile = filled(dve, uses, base, ("hidden", i))
            if i == 0:
                dve.wait_ge(y_free, v + 1)
            n = min(2, JOBS - 2 * i)
            nc.vector.tensor_copy(ht[:, 2 * i:2 * i + n, :],
                                  tile[:].rearrange("p (j w) -> p j w", w=512)[:, 0:n, 0:IP]
                                  ).then_inc(ring_free, 1)

        def down(pe, uses, base, e, **ago):
            pe.wait_ge(w2_in, 16)
            pe.wait_ge(ring_free, count(uses, base, ("hidden", JOBS // 2)))
            tile = take(pe, uses, base, ("down", 0), **ago)
            for j in range(JOBS):
                for c in range(3):
                    mm = nc.tensor.matmul(tile[:, j * P:(j + 1) * P], ht[:, j, c * P:(c + 1) * P],
                                          w2[:, bass.ds(e[j], 1), c, :].rearrange("p o n -> p (o n)"),
                                          start=(c == 0), stop=(c == 2))
            mm.then_inc(ring_full, 1)

        def keep_down(dve, uses, base):
            tile = filled(dve, uses, base, ("down", 0))
            nc.vector.tensor_copy(yj, tile[:, 0:JOBS * P].rearrange("p (j c) -> p j c", c=D)
                                  ).then_inc(ring_free, 1)

        def store_jobs(pool, uses, base, v):
            pool.wait_ge(ring_free, count(uses, base, ("down", 0)))
            pool.dma_start(d["yg"][bass.ds(v * (JOBS * P), JOBS * P), :].rearrange("(j p) c -> p j c", p=P),
                           yj).then_inc(y_stored, 16)
            pool.wait_ge(y_stored, 16 * (v + 1))
            pool.sem_inc(y_free, 1)

        def pe_round(pe, base, ahead, now, after_first=None):
            uses, e_up = ring_uses(ahead is not None, now is not None), []
            for place in range(GROUP):
                for j in range(CH):
                    if now is not None:
                        pv(pe, now, place, j)
                        if j == 3 and place:
                            turn(pe, now, place - 1)
                    if ahead is not None:
                        qk(pe, uses, base, ahead, place, j)
                        if (place, j) == (0, 3):
                            turn_tokens(pe, uses, base, ahead)
                    if now is not None and (place, j) in HIDDEN_AT:
                        turn_hidden(pe, uses, base, now, HIDDEN_AT.index((place, j)))
                    if ahead is not None and (place, j) in READ_AT:
                        e_up.append(expert_of(pe, ahead, len(e_up)))
                if after_first is not None and place == 0:
                    after_first(pe)
            if now is not None:
                turn(pe, now, GROUP - 1)
            if ahead is not None:
                up(pe, uses, base, e_up)
            if now is not None:
                down(pe, uses, base, experts_of(pe, now))
                if ahead is not None:
                    pe.wait_ge(att_ready, GROUP * now + GROUP)

        def take_out(dve, group, place):
            dve.wait_ge(pv_done, CHG * group + (place + 1) * CH)
            nc.vector.tensor_copy(ot[:], pvb[place % 2][:, 0:256]).then_inc(ot_ready, 1)

        def divide(dve, group, place):
            dve.wait_ge(turned, GROUP * group + place + 1)
            if place == 0:
                dve.wait_ge(attg_free, group + 1)
            t = pvb[place % 2][:, 256:512].rearrange("p (k w) -> p k w", w=32)
            nc.vector.reciprocal(rden[:, place, :], t[:, :, HD]).then_inc(rden_ready, 1)
            dve.wait_ge(rden_ready, GROUP * group + place + 1)
            nc.vector.tensor_tensor(attg[:, :, place * HD:(place + 1) * HD], t[:, :, 0:HD],
                                    bcast(rden[:, place, :], 2, HD), ALU.mult).then_inc(att_ready, 1)

        def keep_distances(dve, uses, base, now, place, j):
            tile = filled(dve, uses, base, ("qk", place, j))
            if now is not None:
                dve.wait_ge(pv_done, CHG * now + place * CH + j + 1)
            nc.vector.tensor_scalar(S[place][:, j * N:(j + 1) * N], tile[:], 1e-12, None,
                                    ALU.max).then_inc(ring_free, 1)

        def dve_round(dve, base, ahead, now, between=None):
            uses = ring_uses(ahead is not None, now is not None)
            for place in range(GROUP):
                for j in range(CH):
                    if ahead is not None:
                        keep_distances(dve, uses, base, now, place, j)
                        if (place, j) == (0, 3):
                            keep_tokens(dve, uses, base)
                        if between is not None:
                            next(between, None)
                    if now is not None:
                        if (place, j) in HIDDEN_AT:
                            keep_hidden(dve, uses, base, now, HIDDEN_AT.index((place, j)))
                        if j == 5 and place:
                            divide(dve, now, place - 1)
                if now is not None:
                    take_out(dve, now, place)
            if now is not None:
                divide(dve, now, GROUP - 1)
            if ahead is not None:
                keep_up(dve, uses, base, ahead)
            if now is not None:
                keep_down(dve, uses, base)

        def store_out(pool, group):
            pool.wait_ge(att_ready, GROUP * group + GROUP)
            for t in range(2):
                dst = d["att" + L][bass.ds(group, 1), :, :].rearrange(
                    "o (c t p) w -> t p (o c) w", c=4, t=2)[t]
                pool.dma_start(dst, attg[:, 4 * t:4 * t + 4, :]).then_inc(att_out, 16)
            pool.wait_ge(att_out, 32 * (group + 1))
            pool.sem_inc(attg_free, 1)

        def load_stack(sp, n, slot, done):
            sp.dma_start(stk[slot][0:SUM_ROW], d["stack0"][bass.ds(n * HD, HD)]
                         .rearrange("e r s t -> (e r) s t")).then_inc(done, 16)
            sp.dma_start(stk[slot][SUM_ROW:ROWS], d["sums0"][bass.ds(n, 1)]
                         .rearrange("o r s t -> (o r) s t")).then_inc(done, 16)

        def general(eng, which):
            if which == "dve":
                eng.sem_inc(g_att, 1)
            if which == "pool":
                eng.sem_inc(g_slot, 1)
            with eng.Fori(0, GROUPS) as u:
                with eng.Fori(0, GROUP) as h:
                    n = u * GROUP + h
                    if which == "sp":
                        eng.wait_ge(g_att, NT * n + 1)
                        eng.wait_ge(zeroed, 1)
                        load_stack(eng, n, 0, g_in)
                        eng.dma_start(val[0][:], d["v" + L][bass.ds(n, 1)]
                                      .rearrange("o p (j w) -> (o p) j w", w=VW)).then_inc(g_in, 16)
                    if which == "pool":
                        eng.wait_ge(g_att, NT * (n + 1) + 1)
                        eng.dma_start(d["att" + L][bass.ds(u, 1), :, bass.ds(h * HD, HD)]
                                      .rearrange("o (t p) w -> p (o t) w", p=P),
                                      attg[:, :, 0:HD]).then_inc(g_out, 16)
                        eng.wait_ge(g_out, 16 * (n + 1))
                        eng.sem_inc(g_slot, 1)
                    for i in range(NT) if which in ("pe", "act", "dve") else ():
                        k = n * NT + i
                        if which == "pe":
                            if i == 0:
                                eng.wait_ge(g_in, 48 * (n + 1))
                            eng.wait_ge(g_att, k + 1)
                            for half in range(2):
                                cols = slice(half * 512, (half + 1) * 512)
                                mm = nc.tensor.matmul(ring[0][:, cols], stk[0][:, Q, i * P:(i + 1) * P],
                                                      stk[0][:, K, cols], start=True, stop=True)
                            mm.then_inc(g_s, 1)
                            eng.wait_ge(g_exp, k + 1)
                            for j in range(CH):
                                mm = nc.tensor.transpose(ring[1][:, j * P:(j + 1) * P],
                                                         S[0][:, j * P:(j + 1) * P], R["ident"][:])
                            mm.then_inc(g_turn, 1)
                            eng.wait_ge(g_pt, k + 1)
                            for j in range(CH):
                                mm = nc.tensor.matmul(pvb[0][:, 0:VW], S[1][:, j * P:(j + 1) * P],
                                                      val[0][:, j, :], start=(j == 0), stop=(j == CH - 1))
                            mm.then_inc(g_pv, 1)
                        if which == "dve":
                            eng.wait_ge(g_s, k + 1)
                            nc.vector.tensor_scalar(S[0][:, 0:N], ring[0][:], 1e-12, None,
                                                    ALU.max).then_inc(g_copied, 1)
                            eng.wait_ge(g_root, k + 1)
                            nc.vector.tensor_reduce(mcol[:], S[0][:, 0:N], axis=AX, op=ALU.min).then_inc(g_max, 1)
                            eng.wait_ge(g_turn, k + 1)
                            nc.vector.tensor_copy(S[1][:, 0:N], ring[1][:]).then_inc(g_pt, 1)
                            eng.wait_ge(g_pv, k + 1)
                            nc.vector.reciprocal(rden[:, 0, 0:1], pvb[0][:, HD:VW]).then_inc(g_rd, 1)
                            eng.wait_ge(g_rd, k + 1)
                            if i == 0:
                                eng.wait_ge(g_slot, n + 1)
                            nc.vector.tensor_scalar(attg[:, i, 0:HD], pvb[0][:, 0:HD], rden[:, 0, 0:1], None,
                                                    ALU.mult).then_inc(g_att, 1)
                        if which == "act":
                            eng.wait_ge(g_copied, k + 1)
                            nc.scalar.activation(S[0][:, 0:N], S[0][:, 0:N], ACT.Sqrt).then_inc(g_root, 1)
                            eng.wait_ge(g_max, k + 1)
                            nc.scalar.activation(S[0][:, 0:N], S[0][:, 0:N], ACT.Exp, bias=mcol[:],
                                                 scale=-1.0).then_inc(g_exp, 1)

        def jobs_alone(eng, which):
            uses, n = ALONE, len(ALONE)
            if which == "sp":
                load_jobs(eng, 0)
                eng.wait_ge(placed, 16 * B * NT)
                with eng.Fori(1, GROUPS) as v:
                    eng.wait_ge(ring_free, count(uses, n * (v - 1), ("tokens", 0)))
                    load_jobs(eng, v)
            if which == "pool":
                load_down(eng)
                place_tokens(eng)
                eng.sem_inc(y_free, 1)
                with eng.Fori(0, GROUPS) as v:
                    hidden(eng, v)
                    store_jobs(eng, uses, n * v, v)
            if which == "pe":
                eng.wait_ge(w_in, 16)
                eng.wait_ge(g_att, NT * HEADS + 1)
                def tiles(v):
                    turn_tokens(eng, uses, n * v, v, ago=1)
                    e = experts_of(eng, v)
                    up(eng, uses, n * v, e, ago=1)
                    for i in range(len(HIDDEN_AT)):
                        turn_hidden(eng, uses, n * v, v, i, ago=1)
                    down(eng, uses, n * v, e, ago=1)
                tiles(0)
                eng.wait_ge(w_rest, 16)
                with eng.Fori(1, GROUPS) as v:
                    tiles(v)
            if which == "act":
                with eng.Fori(0, GROUPS) as v:
                    tanh(eng, uses, n * v)
            if which == "dve":
                with eng.Fori(0, GROUPS) as v:
                    keep_tokens(eng, uses, n * v)
                    keep_up(eng, uses, n * v, v)
                    for i in range(len(HIDDEN_AT)):
                        keep_hidden(eng, uses, n * v, v, i)
                    keep_down(eng, uses, n * v)

        def by_guard(eng, which, fast, route=None):
            flag = eng.value_load(R["flag"][0:1, layer:layer + 1], min_val=0, max_val=1)
            with eng.If(flag != 0):
                if route is not None:
                    route(eng)
                general(eng, which)
                jobs_alone(eng, which)
            with eng.Else():
                fast(eng)

        @block.sync
        def _(sp):

            def load(group, place):
                sp.wait_ge(zeroed, place % SLOTS + 1)
                load_stack(sp, group * GROUP + place, place % SLOTS, stk_in[place % SLOTS])

            def load_shared(sp):
                sp.wait_ge(zeroed, SLOTS + 3)
                sp.dma_start(w13[:, 0:1, :, :], d["w13"][0:1].rearrange("e c a i -> c e a i")).then_inc(w_in, 16)
                load_router(sp)
                sp.dma_start(tokens.rearrange("p (t c) -> p t c", c=D),
                             d["xg"][0:SHARED * P, :].rearrange("(t p) c -> p t c", p=P)).then_inc(tok_in, 16)
                clear_places(sp)

            def fast(sp):
                load(0, 0)
                load(0, 1)
                load_jobs(sp, 0)
                load_shared(sp)
                for place in range(SLOTS, GROUP):
                    sp.wait_ge(ring_full, count(ROUND, 0, ("qk", place - SLOTS, CH - 1)))
                    load(0, place)
                for lo, hi in ((1, FULL_SHARED), (FULL_SHARED, GROUPS)):
                    if lo == FULL_SHARED:
                        sp.wait_ge(placed, 16 * B * NT)
                    with sp.Fori(lo, hi) as u:
                        for place in range(GROUP):
                            before = u - 1 if place < SLOTS else u
                            sp.wait_ge(ring_full, count(ROUND, CYCLE * before,
                                                        ("qk", (place - SLOTS) % GROUP, CH - 1)))
                            load(u, place)
                            if place == 1:
                                sp.wait_ge(ring_free, count(ROUND, CYCLE * (u - 1), ("tokens", 0)))
                                load_jobs(sp, u)
            by_guard(sp, "sp", fast, load_shared)

        @block.gpsimd
        def _(pool):
            def load(group, place):
                pool.dma_start(val[place][:], d["v" + L][bass.ds(group * GROUP + place, 1)]
                               .rearrange("o p (j w) -> (o p) j w", w=VW)).then_inc(val_in[place], 16)

            def fast(pool):
                pool.sem_inc(attg_free, 1)
                pool.sem_inc(y_free, 1)
                for place in range(GROUP):
                    load(0, place)
                load_down(pool)

                def group(u, start=False):
                    for place in range(GROUP):
                        pool.wait_ge(pv_done, CHG * u + (place + 1) * CH)
                        load(u + 1, place)
                        if place == 0:
                            hidden(pool, u)
                            if start:
                                place_tokens(pool)
                    store_out(pool, u)
                    store_jobs(pool, ROUND, CYCLE * (u + 1), u)
                group(0, start=True)
                with pool.Fori(1, GROUPS - 1) as u:
                    group(u)
                hidden(pool, GROUPS - 1)
                store_out(pool, GROUPS - 1)
                store_jobs(pool, LAST, CYCLE * GROUPS, GROUPS - 1)
            by_guard(pool, "pool", fast)

        @block.tensor
        def _(pe):
            def fast(pe):
                pe.wait_ge(cleared, 2)
                pe.wait_ge(zeroed, SLOTS + 2)
                pe.wait_ge(w_in, 16)
                pe_round(pe, 0, 0, None, after_first=rank)
                pe.wait_ge(ring_free, CYCLE)
                pe.sem_inc(ring_full, CYCLE - len(FIRST))
                pe.wait_ge(ranks_read, 1)
                for lo, hi in ((0, FULL_SHARED - 1), (FULL_SHARED - 1, GROUPS - 1)):
                    if lo:
                        pe.wait_ge(w_rest, 16)
                    with pe.Fori(lo, hi) as u:
                        pe_round(pe, CYCLE * (u + 1), u + 1, u)
                pe_round(pe, CYCLE * GROUPS, None, GROUPS - 1)
            by_guard(pe, "pe", fast, rank)

        @block.vector
        def _(dve):
            for i in range(SLOTS):
                nc.vector.memset(stk[i][:].rearrange("r s t -> r (s t)").bitcast(F32), 0.0).then_inc(zeroed, 1)
            nc.vector.memset(gate[:, :, I:IP], 0.0).then_inc(zeroed, 1)
            nc.vector.memset(R["expert"][:], 0).then_inc(zeroed, 1)
            nc.vector.memset(zeros, 0.0).then_inc(zeroed, 1)
            def route_dve(dve):
                for _ in choose(dve):
                    pass
                dve.wait_ge(places_clear, 16 * (PLACES // NT))

            def fast(dve):
                for i in range(2):
                    nc.vector.memset(pvb[i][:], 0.0).then_inc(cleared, 1)
                steps = choose(dve)
                next(steps)
                dve_round(dve, 0, 0, None, between=steps)
                for _ in steps:
                    pass
                dve.wait_ge(places_clear, 16 * (PLACES // NT))
                dve.wait_ge(ring_free, len(FIRST))
                dve.sem_inc(ring_free, CYCLE - len(FIRST))
                with dve.Fori(0, GROUPS - 1) as u:
                    dve_round(dve, CYCLE * (u + 1), u + 1, u)
                dve_round(dve, CYCLE * GROUPS, None, GROUPS - 1)
            by_guard(dve, "dve", fast, route_dve)

        @block.scalar
        def _(act):
            def fast(act):
                def roots(u):
                    for place in range(GROUP):
                        act.wait_ge(ring_free, count(ROUND, CYCLE * u, ("qk", place, CH - 1)))
                        nc.scalar.activation(S[place][:], S[place][:], ACT.Sqrt).then_inc(root_done, 1)

                def exps(u):
                    for place in range(GROUP):
                        if place == 2:
                            tanh(act, ROUND, CYCLE * u)
                        act.wait_ge(root_done, GROUP * u + place + 1)
                        nc.scalar.activation(S[place][:], S[place][:], ACT.Exp, scale=-1.0).then_inc(exp_done, 1)

                powers(act)
                for place in range(GROUP):
                    for j in range(1, CH, 2):
                        act.wait_ge(ring_free, count(FIRST, 0, ("qk", place, j)))
                        part = S[place][:, (j - 1) * N:(j + 1) * N]
                        root = nc.scalar.activation(part, part, ACT.Sqrt)
                    root.then_inc(root_done, 1)
                exps(0)
                with act.Fori(1, GROUPS) as u:
                    roots(u)
                    exps(u)
            by_guard(act, "act", fast, powers)


def attention1(nc, d, R):
    RING1, HALF = 4, 2 * GROUP
    SUMMED = 3
    with phase_semaphores(nc) as take, ExitStack() as ctx:
        sb = lambda n, s, t=F32: ctx.enter_context(nc.sbuf_tensor("a1_" + n, s, t))
        sem = lambda n: take("a1_" + n)
        stk = [sb(f"stk{i}", [KROWS, 2, N], BF16) for i in range(GROUP)]
        den = [sb(f"den{i}", [P, GROUP, NT]) for i in range(2)]
        wsum = [sb(f"wsum{i}", [P, GROUP, NT]) for i in range(2)]
        top, neg = sb("top", [P, 1]), sb("neg", [P, 1])
        E = [sb(f"exp{i}", [P, 2, N]) for i in range(SUMMED)]
        ring = [ctx.enter_context(nc.psum_tensor(f"a1_ring{i}", [P, N], F32)) for i in range(RING1)]
        stk_in = [sem(f"stk_in{i}") for i in range(GROUP)]
        qk_done, exp_done, summed, inv_done, w_done, v_done = (
            sem(n) for n in ("qk_done", "exp_done", "summed", "inv_done", "w_done", "v_done"))
        zeroed, biased = sem("zeroed"), sem("biased")
        g_in, g_s, g_max, g_neg, g_exp, g_inv, g_w, g_v = (
            sem("g_" + n) for n in ("in", "s", "max", "neg", "exp", "inv", "w", "v"))
        block = ctx.enter_context(nc.Block())
        Q, K = 0, 1

        def load(sp, n, place, done):
            sp.dma_start(stk[place][0:SUM_ROW], d["stack1"][bass.ds(n * HD, HD)]
                         .rearrange("e r s t -> (e r) s t")).then_inc(done, 16)

        def scores(out, place, i):
            for half in range(2):
                cols = slice(half * 512, (half + 1) * 512)
                mm = nc.tensor.matmul(out[:, cols], stk[place][:, Q, i * P:(i + 1) * P],
                                      stk[place][:, K, cols], start=True, stop=True)
            return mm

        def weigh(dve, b, column, side, count, inv_sem, w_sem, v_sem):
            nc.vector.reciprocal(wsum[side][:], den[side][:]).then_inc(inv_sem, 1)
            dve.wait_ge(inv_sem, count)
            nc.vector.tensor_tensor(wsum[side][:], wsum[side][:], den[side][:], ALU.mult).then_inc(w_sem, 1)
            dve.wait_ge(w_sem, count)
            vals = R["V1"][:, bass.ds(b * NT, NT), bass.ds(column, GROUP * HD)].rearrange(
                "p t (h e) -> p t h e", e=HD)
            for h in range(GROUP):
                mul = nc.vector.tensor_tensor(vals[:, :, h, :], vals[:, :, h, :],
                                              bcast(wsum[side][:, h, :], 2, HD), ALU.mult)
            mul.then_inc(v_sem, 1)

        def general(eng, which):
            if which == "dve":
                eng.sem_inc(g_v, 1)
            with eng.Fori(0, B) as b:
                with eng.Fori(0, GROUP) as g:
                    u = b * GROUP + g
                    for h in range(GROUP):
                        n = u * GROUP + h
                        if which == "sp":
                            eng.wait_ge(zeroed, GROUP)
                            eng.wait_ge(g_v, u + 1)
                            load(eng, n, h, g_in)
                        for i in range(NT):
                            k = n * NT + i
                            if which == "pe":
                                if i == 0:
                                    eng.wait_ge(g_in, 16 * GROUP * (u + 1))
                                if h == 0 and i == 0:
                                    eng.wait_ge(g_v, u + 1)
                                elif i or h:
                                    eng.wait_ge(g_exp, k)
                                scores(ring[0][:], h, i).then_inc(g_s, 1)
                            if which == "dve":
                                eng.wait_ge(g_s, k + 1)
                                nc.vector.tensor_reduce(top[:], ring[0][:], axis=AX, op=ALU.max).then_inc(g_max, 1)
                                eng.wait_ge(g_max, k + 1)
                                nc.vector.tensor_scalar(neg[:], top[:], -SCALE1, None, ALU.mult).then_inc(g_neg, 1)
                                eng.wait_ge(g_exp, k + 1)
                            if which == "act":
                                eng.wait_ge(g_neg, k + 1)
                                nc.scalar.activation(ring[0][:], ring[0][:], ACT.Exp, scale=SCALE1, bias=neg[:],
                                                     accum_out=den[0][:, h, i:i + 1]).then_inc(g_exp, 1)
                    if which == "dve":
                        weigh(eng, b, g * GROUP * HD, 0, u + 1, g_inv, g_w, g_v)

        def by_guard(eng, which, fast):
            flag = eng.value_load(R["flag"][0:1, 1:2], min_val=0, max_val=1)
            with eng.If(flag != 0):
                general(eng, which)
            with eng.Else():
                fast(eng)

        @block.sync
        def _(sp):
            def fast(sp):
                for place in range(GROUP):
                    sp.wait_ge(zeroed, place + 1)
                    load(sp, place, place, stk_in[place])
                with sp.Fori(1, GROUPS) as u:
                    for place in range(GROUP):
                        sp.wait_ge(qk_done, GROUP * NT * (u - 1) + (place + 1) * NT)
                        load(sp, u * GROUP + place, place, stk_in[place])
            by_guard(sp, "sp", fast)

        @block.gpsimd
        def _(pool):
            for b in range(B):
                xb = R["X"][:, b * NT:(b + 1) * NT, :]
                nc.gpsimd.tensor_tensor(xb, xb, bcast(R["bo1"][:], 1, NT), ALU.add).then_inc(biased, 1)

        @block.tensor
        def _(pe):
            def heads(body, start):
                for h in range(HALF):
                    pe.wait_ge(stk_in[h % GROUP], 16 * (2 * body + h // GROUP + 1))
                    for i in range(NT):
                        k = (body * HALF + h) * NT + i
                        if not start or h * NT + i >= RING1:
                            pe.wait_ge(exp_done, k - RING1 + 1)
                        scores(ring[i % RING1], h % GROUP, i).then_inc(qk_done, 1)

            def fast(pe):
                heads(0, True)
                with pe.Fori(1, HEADS // HALF) as body:
                    heads(body, False)
            by_guard(pe, "pe", fast)

        @block.scalar
        def _(act):
            def heads(body, start):
                for h in range(HALF):
                    side = h // GROUP
                    if h % GROUP == 0 and not start:
                        act.wait_ge(v_done, 2 * (body - 1) + side + 1)
                    for i in range(NT):
                        tile, pair = ring[i % RING1], i // 2
                        act.wait_ge(qk_done, (body * HALF + h) * NT + i + 1)
                        if pair < SUMMED:
                            if i % 2 == 0 and (not start or h):
                                act.wait_ge(summed, SUMMED * (body * HALF + h - 1) + pair + 1)
                            exp = nc.scalar.activation(E[pair][:, i % 2, :], tile[:], ACT.Exp, scale=SCALE1)
                        else:
                            exp = nc.scalar.activation(tile[:], tile[:], ACT.Exp, scale=SCALE1,
                                                       accum_out=den[side][:, h % GROUP, i:i + 1])
                        exp.then_inc(exp_done, 1)

            def fast(act):
                heads(0, True)
                with act.Fori(1, HEADS // HALF) as body:
                    heads(body, False)
            by_guard(act, "act", fast)

        @block.vector
        def _(dve):
            for i in range(GROUP):
                nc.vector.memset(stk[i][:].rearrange("r s t -> r (s t)").bitcast(F32), 0.0).then_inc(zeroed, 1)
            def fast(dve):
                with dve.Fori(0, B) as b:
                    with dve.Fori(0, 2) as half:
                        for side in range(2):
                            u = b * 4 + half * 2 + side
                            for h in range(GROUP):
                                n = u * GROUP + h
                                for pair in range(SUMMED):
                                    dve.wait_ge(exp_done, n * NT + 2 * pair + 2)
                                    nc.vector.tensor_reduce(den[side][:, h, 2 * pair:2 * pair + 2], E[pair][:],
                                                            axis=AX, op=ALU.add).then_inc(summed, 1)
                            dve.wait_ge(exp_done, GROUP * NT * (u + 1))
                            dve.wait_ge(summed, GROUP * SUMMED * (u + 1))
                            weigh(dve, b, half * 2 * GROUP * HD + side * GROUP * HD, side, u + 1,
                                  inv_done, w_done, v_done)
            by_guard(dve, "dve", fast)


def finish(nc, d, R):
    with phase_semaphores(nc) as take, ExitStack() as ctx:
        sb = lambda n, s, t=F32: ctx.enter_context(nc.sbuf_tensor(n, s, t))
        ps = lambda n, s: ctx.enter_context(nc.psum_tensor(n, s, F32))
        sem = lambda n: take(n)
        V1 = R["V1"]
        att = [sb(f"fatt{i}", [P, N]) for i in range(2)]
        pT = [ps(f"fpT{i}", [P, N]) for i in range(2)]
        pO = [ps(f"fpO{i}", [P, N]) for i in range(2)]
        turned, att_ready, wo_done, added, out_done = (
            sem(n) for n in ("f_turned", "f_att_ready", "f_wo_done", "f_added", "f_out_done"))
        block = ctx.enter_context(nc.Block())

        @block.sync
        def _(sp):
            for b in range(B):
                sp.wait_ge(added, b + 1)
                sp.dma_start(d["out"][b * N:(b + 1) * N, :].rearrange("(t p) c -> p t c", p=P),
                             R["X"][:, b * NT:(b + 1) * NT, :]).then_inc(out_done, 16)
            sp.wait_ge(out_done, 16 * B)

        @block.tensor
        def _(pe):
            def turn(b):
                if b >= 2:
                    pe.wait_ge(att_ready, 2 * (b - 1))
                for t in range(NT):
                    nc.tensor.transpose(pT[b % 2][:, t * P:(t + 1) * P], V1[:, b * NT + t, :],
                                        R["ident"][:]).then_inc(turned, 1)

            turn(0)
            for b in range(B):
                if b + 1 < B:
                    turn(b + 1)
                if b >= 2:
                    pe.wait_ge(added, b - 1)
                pe.wait_ge(att_ready, 2 * (b + 1))
                for t in range(NT):
                    mm = nc.tensor.matmul(pO[b % 2][:, t * P:(t + 1) * P], att[b % 2][:, t * P:(t + 1) * P],
                                          R["wo1"][:], start=True, stop=True)
                mm.then_inc(wo_done, 1)

        @block.scalar
        def _(act):
            for b in range(B):
                if b >= 2:
                    act.wait_ge(wo_done, b - 1)
                for half in range(2):
                    cols = slice(half * 512, (half + 1) * 512)
                    act.wait_ge(turned, NT * b + 4 * (half + 1))
                    nc.scalar.activation(att[b % 2][:, cols], pT[b % 2][:, cols], ACT.Copy).then_inc(att_ready, 1)

        @block.vector
        def _(dve):
            for b in range(B):
                xb = R["X"][:, b * NT:(b + 1) * NT, :]
                dve.wait_ge(wo_done, b + 1)
                nc.vector.tensor_tensor(xb, xb, pO[b % 2][:].rearrange("p (t c) -> p t c", c=D),
                                        ALU.add).then_inc(added, 1)


def build(nc, d):
    with ExitStack() as ctx:
        R = {}
        with ExitStack() as own:
            load_constants(nc, ctx, own, d, R)
            R["X"] = own.enter_context(nc.sbuf_tensor("X_0", [P, B * NT, D], F32))
            prepare(nc, d, R, 0)
        attention0(nc, d, R)
        for name in ("X", "V1"):
            R[name] = ctx.enter_context(nc.sbuf_tensor(name + "_1", [P, B * NT, D], F32))
        prepare(nc, d, R, 1)
        attention1(nc, d, R)
        finish(nc, d, R)


def kernel(L0_attn_x, L0_attn_wq, L0_attn_bq, L0_attn_wk, L0_attn_bk, L0_attn_wv, L0_attn_bv,
           L0_attn_wo, L0_attn_bo, L0_ffn_router_w, L0_ffn_routing_bias, L0_ffn_sw1, L0_ffn_sw2,
           L0_ffn_sw3, L0_ffn_ew1, L0_ffn_ew2, L0_ffn_ew3, L1_attn_w_in, L1_attn_b_in,
           L1_attn_w_out, L1_attn_b_out, L1_ffn_theta, L1_ffn_phi, L1_ffn_theta_noise,
           L1_ffn_phi_noise):
    import concourse.bacc as bacc
    from concourse.bass_utils import run_bass_kernel_spmd

    w_in = np.asarray(L1_attn_w_in).reshape(H, 3, HD, D)
    b_in = np.asarray(L1_attn_b_in).reshape(H, 3, HD)
    w1 = np.concatenate([np.asarray(L0_ffn_sw1)[None], np.asarray(L0_ffn_ew1)])
    w3 = np.concatenate([np.asarray(L0_ffn_sw3)[None], np.asarray(L0_ffn_ew3)])
    w2 = np.concatenate([np.asarray(L0_ffn_sw2)[None], np.asarray(L0_ffn_ew2)])
    w13 = np.stack([w1, w3], axis=1).transpose(0, 3, 1, 2)
    w2c = np.zeros((NE, 3 * P, D), np.float32)
    w2c[:, :I] = w2.transpose(0, 2, 1)
    w2c = w2c.reshape(NE, 3, P, D).transpose(0, 2, 1, 3)
    blk = np.zeros((P, 64), np.float32)
    for r in range(P):
        blk[r, r // HD] = 0.25
        blk[r, 32 + r // HD] = 1.0
    arrays = {
        "x": np.asarray(L0_attn_x).reshape(B * N, D),
        "wq0": np.asarray(L0_attn_wq).T, "wk0": np.asarray(L0_attn_wk).T,
        "wv0": np.asarray(L0_attn_wv).T, "wo0": np.asarray(L0_attn_wo).T,
        "bq0": np.asarray(L0_attn_bq)[:, None], "bk0": np.asarray(L0_attn_bk)[:, None],
        "bv0": np.asarray(L0_attn_bv)[None], "bo0": np.asarray(L0_attn_bo)[None],
        "rw": np.asarray(L0_ffn_router_w).T, "rb": np.asarray(L0_ffn_routing_bias)[None],
        "w13": w13, "w2": w2c,
        "wq1": w_in[:, 0].reshape(D, D).T, "wk1": w_in[:, 1].reshape(D, D).T,
        "wv1": w_in[:, 2].reshape(D, D).T, "wo1": np.asarray(L1_attn_w_out).T,
        "bq1": b_in[:, 0].reshape(D, 1), "bk1": b_in[:, 1].reshape(D, 1),
        "bv1": b_in[:, 2].reshape(1, D), "bo1": np.asarray(L1_attn_b_out)[None],
        "theta": np.asarray(L1_ffn_theta), "phi": np.asarray(L1_ffn_phi),
        "theta_noise": np.asarray(L1_ffn_theta_noise), "phi_noise": np.asarray(L1_ffn_phi_noise),
        "ident": np.eye(P, dtype=np.float32), "blk": blk,
        "tri": np.triu(np.ones((P, P), np.float32), 1), "all_ones": np.ones((P, P), np.float32),
        "marks": np.repeat(P * np.arange(B * NT, dtype=np.float32)[None], P, axis=0),
        "slots": np.arange(PLACES, dtype=np.float32)[None],
        "desc": np.repeat(np.arange(E, 0, -1, dtype=np.float32)[None], P, axis=0),
    }
    for pack, kinds in PACKS.items():
        for kind, widths in kinds.items():
            arrays[f"{pack}_{kind}"] = np.concatenate([arrays.pop(n) for n in widths], axis=1)
    arrays = {n: np.ascontiguousarray(a) for n, a in arrays.items()}
    nc = bacc.Bacc("TRN2", target_bir_lowering=False, num_devices=1)
    d = {n: nc.dram_tensor(f"in_{n}", a.shape, F32, kind="ExternalInput").ap() for n, a in arrays.items()}
    for layer in "01":
        d["stack" + layer] = nc.dram_tensor("stack" + layer, (HEADS * HD, len(PAIRS), 2, N), BF16,
                                            kind="Internal").ap()
    d["sums0"] = nc.dram_tensor("sum_rows0", (HEADS, 6, 2, N), BF16, kind="Internal").ap()
    for n in ("xg", "yg"):
        d[n] = nc.dram_tensor(n, (TILES * P, D), F32, kind="Internal").ap()
    d["v0"] = nc.dram_tensor("v0", (HEADS, P, NT * VW), F32, kind="Internal").ap()
    d["att0"] = nc.dram_tensor("att0", (GROUPS, N, GROUP * HD), F32, kind="Internal").ap()
    d["out"] = nc.dram_tensor("out", (B * N, D), F32, kind="ExternalOutput").ap()
    build(nc, d)
    r = run_bass_kernel_spmd(nc, [{f"in_{n}": a for n, a in arrays.items()}], core_ids=[0])
    return r.results[0]["out"].reshape(B, N, D)
```
